# Optimizing a Trainium2 kernel written in Bass

```python
import numpy as np
import jax
import jax.numpy as jnp

def _softmax(x, axis=-1):
    return jax.nn.softmax(x, axis=axis)

def _gelu(x):
    return jax.nn.gelu(x, approximate=True)

def _silu(x):
    return jax.nn.silu(x)

def _sigmoid(x):
    return jax.nn.sigmoid(x)

def _layernorm(x, axis=-1, eps=1e-05):
    m = jnp.mean(x, axis=axis, keepdims=True)
    v = jnp.var(x, axis=axis, keepdims=True)
    return (x - m) / jnp.sqrt(v + eps)

def _scatter_add(tgt, idx, src, axis=0):
    return tgt.at[idx].add(src)

def _segment_sum(src, seg, n):
    return jax.ops.segment_sum(src, seg, n)
kernel_name = 'mk_decoder_preln_d2_seqx_r8_962f89'

def setup_inputs(seed: int=0):
    np.random.seed(seed)
    _w = jnp.asarray

    def _rec_inputs():
        import jax
        import jax.numpy as jnp
        _rk = jax.random.key(seed)
        x = 0.0002417 + 0.9998 * jax.random.normal(jax.random.fold_in(_rk, 1), (16, 64, 128), jnp.float32)
        _lenS = 64 - jax.random.randint(jax.random.fold_in(_rk, 7), (16,), 0, max(1, 64 // 4) + 1, jnp.int32)
        _lenS2 = 64 - jax.random.randint(jax.random.fold_in(_rk, 8), (16,), 0, max(1, 64 // 4) + 1, jnp.int32)
        _ctx_1024P = jax.random.normal(jax.random.fold_in(_rk, 11), (16, 16, 128), jnp.float32)
        _ctx_1024c = jax.random.dirichlet(jax.random.fold_in(_rk, 511), 0.3 * jnp.ones((16,), jnp.float32), (16, 64))
        _ctx_1024t = jnp.einsum('bsk,bkd->bsd', _ctx_1024c, _ctx_1024P)
        _ctx_1024t = _ctx_1024t * jax.lax.rsqrt(jnp.mean(jnp.square(_ctx_1024t)) + 1e-12) * 0.953939
        ctx_1024 = 7.22013e-05 + 1.00017 * (_ctx_1024t + 0.3 * jax.random.normal(jax.random.fold_in(_rk, 611), (16, 64, 128), jnp.float32))
        _validS = jnp.arange(64)[None, :] < _lenS[:, None]
        _validS2 = jnp.arange(64)[None, :] < _lenS2[:, None]
        _causal = jnp.tril(jnp.ones((64, 64), dtype=bool))
        mask_Bx1x1xS2_fk0 = jnp.where(jnp.broadcast_to(_validS2[:, None, None, :], (16, 1, 1, 64)), 0.0, 1.0).astype(jnp.float32)
        return (x, ctx_1024, mask_Bx1x1xS2_fk0)
    x, ctx_1024, mask_Bx1x1xS2_fk0 = _rec_inputs()

    def _L0_attn_setup():
        import jax, jax.numpy as jnp
        import numpy as np
        DIM = 128
        NUM_HEADS = 16
        NUM_KV_HEADS = 4
        HEAD_DIM = DIM // NUM_HEADS
        ROPE_BASE = 10000.0
        EPS = 1e-08
        BSZ, SEQ = (8, 128)

        def bitlinear(x, w, eps=EPS):
            alpha = jax.lax.stop_gradient(jnp.maximum(jnp.mean(jnp.abs(w)), eps))
            w_t = jnp.round(jnp.clip(w / alpha, -1.0, 1.0))
            w_q = w + jax.lax.stop_gradient(w_t * alpha - w)
            gamma = jax.lax.stop_gradient(jnp.maximum(jnp.max(jnp.abs(x), axis=-1, keepdims=True), eps) / 127.0)
            x_int = jnp.round(jnp.clip(x / gamma, -128.0, 127.0))
            x_q = x + jax.lax.stop_gradient(x_int * gamma - x)
            return x_q @ (w_q / alpha).T * alpha

        def rms_norm(x):
            eps = jnp.finfo(x.dtype).eps
            return x * jax.lax.rsqrt(jnp.mean(x * x, axis=-1, keepdims=True) + eps)

        def rope_cache(seq_len, head_dim, base):
            inv_freq = 1.0 / base ** (jnp.arange(0, head_dim, 2, dtype=jnp.float32) / head_dim)
            t = jnp.arange(seq_len, dtype=jnp.float32)
            freqs = jnp.outer(t, inv_freq)
            return (jnp.cos(freqs), jnp.sin(freqs))

        def apply_rotary(x, cos, sin):
            half = x.shape[-1] // 2
            x1, x2 = (x[..., :half], x[..., half:])
            return jnp.concatenate((x1 * cos + x2 * sin, -x1 * sin + x2 * cos), axis=-1)
        key = jax.random.key(seed)
        ks = jax.random.split(key, 6)
        x = jax.random.normal(ks[0], (BSZ, SEQ, DIM), dtype=jnp.float32)
        Wq = jax.random.normal(ks[1], (DIM, DIM), dtype=jnp.float32) * 0.02
        Wk = jax.random.normal(ks[2], (NUM_KV_HEADS * HEAD_DIM, DIM), dtype=jnp.float32) * 0.02
        Wv = jax.random.normal(ks[3], (NUM_KV_HEADS * HEAD_DIM, DIM), dtype=jnp.float32) * 0.02
        Wp = jax.random.normal(ks[4], (DIM, DIM), dtype=jnp.float32) * 0.02
        q_gain = jnp.ones((NUM_HEADS,), dtype=jnp.float32)
        return {'x': x, 'Wq': Wq, 'Wk': Wk, 'Wv': Wv, 'Wp': Wp, 'q_gain': q_gain}
    _L0_attn_all = _L0_attn_setup()
    _L0_attn_in = {k: v for k, v in _L0_attn_all.items() if k in ('Wq', 'Wk', 'Wv', 'Wp', 'q_gain')}
    del _L0_attn_all

    def _L0_xattn_setup():
        import jax, jax.numpy as jnp
        import numpy as np
        B, S, D, H = (4, 256, 128, 16)
        DEPTH = D // H

        def _split_heads(x):
            b, s, _ = x.shape
            return x.reshape(b, s, H, DEPTH).transpose(0, 2, 1, 3)
        key = jax.random.key(seed)
        ks = jax.random.split(key, 12)
        inp = {'v': jax.random.normal(ks[0], (B, S, D), dtype=jnp.float32), 'k': jax.random.normal(ks[1], (B, S, D), dtype=jnp.float32), 'q': jax.random.normal(ks[2], (B, S, D), dtype=jnp.float32), 'mask': jax.random.randint(ks[3], (B, 1, 1, S), 0, 2).astype(jnp.float32), 'Wq': jax.random.normal(ks[4], (D, D), dtype=jnp.float32) / np.sqrt(D), 'bq': jnp.zeros((D,), dtype=jnp.float32), 'Wk': jax.random.normal(ks[5], (D, D), dtype=jnp.float32) / np.sqrt(D), 'bk': jnp.zeros((D,), dtype=jnp.float32), 'Wv': jax.random.normal(ks[6], (D, D), dtype=jnp.float32) / np.sqrt(D), 'bv': jnp.zeros((D,), dtype=jnp.float32), 'Wo': jax.random.normal(ks[7], (D, D), dtype=jnp.float32) / np.sqrt(D), 'bo': jnp.zeros((D,), dtype=jnp.float32)}
        return inp
    _L0_xattn_all = _L0_xattn_setup()
    _L0_xattn_in = {k: v for k, v in _L0_xattn_all.items() if k in ('Wq', 'bq', 'Wk', 'bk', 'Wv', 'bv', 'Wo', 'bo')}
    del _L0_xattn_all

    def _L0_ffn_setup():
        import jax, jax.numpy as jnp
        import numpy as np
        E = 8
        JITTER = 0.01

        def _sparse_mixer_routing(logits):
            top_vals, top_idx = jax.lax.top_k(logits, 2)
            eidx = jnp.arange(logits.shape[-1])

            def _multiplier(thr, base_logits, idx):
                factor = jnp.maximum(jnp.abs(logits), thr)
                mask = (thr - logits) / factor > 2.0 * JITTER
                probs = jax.nn.softmax(jnp.where(mask, -jnp.inf, base_logits), axis=-1)
                return jnp.take_along_axis(probs, idx, axis=-1)
            mult1 = _multiplier(top_vals[:, :1], logits, top_idx[:, :1])
            scat = jnp.where(eidx[None, :] == top_idx[:, :1], -jnp.inf, logits)
            mult2 = _multiplier(top_vals[:, 1:2], scat, top_idx[:, 1:2])
            return (jnp.concatenate([mult1, mult2], axis=-1), top_idx)
        key = jax.random.key(seed)
        ks = jax.random.split(key, 5)
        H, F = (128, 512)
        scale = 0.02
        return {'hidden_states': jax.random.normal(ks[0], (1, 256, H), jnp.float32), 'gate_w': jax.random.normal(ks[1], (H, E), jnp.float32) * scale, 'w1': jax.random.normal(ks[2], (E, H, F), jnp.float32) * scale, 'w2': jax.random.normal(ks[3], (E, F, H), jnp.float32) * scale, 'w3': jax.random.normal(ks[4], (E, H, F), jnp.float32) * scale}
    _L0_ffn_all = _L0_ffn_setup()
    _L0_ffn_in = {k: v for k, v in _L0_ffn_all.items() if k in ('gate_w', 'w1', 'w2', 'w3')}
    del _L0_ffn_all

    def _L1_attn_setup():
        import jax, jax.numpy as jnp
        import numpy as np
        D_MODEL = 128
        D_QK = 128
        H = 16
        HEAD_DIM = D_QK // H
        V_DIM = D_MODEL // H
        B, S = (2, 256)
        key = jax.random.key(seed)
        ks = jax.random.split(key, 9)
        sd = 1.0 / np.sqrt(D_MODEL)
        return {'x': jax.random.normal(ks[0], (B, S, D_MODEL), dtype=jnp.float32), 'Wqk_w': jax.random.normal(ks[1], (2 * D_QK, D_MODEL), dtype=jnp.float32) * sd, 'Wqk_b': jax.random.normal(ks[2], (2 * D_QK,), dtype=jnp.float32) * 0.01, 'Wv_w': jax.random.normal(ks[3], (D_MODEL, D_MODEL), dtype=jnp.float32) * sd, 'Wv_b': jax.random.normal(ks[4], (D_MODEL,), dtype=jnp.float32) * 0.01, 'Wn_w': jax.random.normal(ks[5], (H, D_MODEL), dtype=jnp.float32) * sd, 'Wn_b': jax.random.normal(ks[6], (H,), dtype=jnp.float32) * 0.01, 'Wo_w': jax.random.normal(ks[7], (D_MODEL, D_MODEL), dtype=jnp.float32) * sd, 'Wo_b': jax.random.normal(ks[8], (D_MODEL,), dtype=jnp.float32) * 0.01}
    _L1_attn_all = _L1_attn_setup()
    _L1_attn_in = {k: v for k, v in _L1_attn_all.items() if k in ('Wqk_w', 'Wqk_b', 'Wv_w', 'Wv_b', 'Wn_w', 'Wn_b', 'Wo_w', 'Wo_b')}
    del _L1_attn_all

    def _L1_xattn_setup():
        import jax, jax.numpy as jnp
        import numpy as np
        EPS = 1e-12

        def _l2norm(x):
            n = jnp.linalg.norm(x, axis=-1, keepdims=True)
            return x / jnp.maximum(n, EPS)
        key = jax.random.key(seed)
        k1, k2 = jax.random.split(key)
        img_feat = jax.random.normal(k1, (8, 512, 128), dtype=jnp.float32)
        text_feat = jax.random.normal(k2, (8, 64, 128), dtype=jnp.float32)
        return {'img_feat': img_feat, 'text_feat': text_feat}
    _L1_xattn_all = _L1_xattn_setup()
    _L1_xattn_in = {k: v for k, v in _L1_xattn_all.items() if k in ()}
    del _L1_xattn_all

    def _L1_ffn_setup():
        import jax, jax.numpy as jnp
        import numpy as np
        MANT_BITS = 8
        _PWL_X = jnp.linspace(-4.0, 4.0, 33, dtype=jnp.float32)
        _PWL_Y = 0.5 * _PWL_X * (1.0 + jax.lax.erf(_PWL_X / jnp.sqrt(jnp.float32(2.0))))

        def float2fix(x, mantissa_bits):
            s = jnp.float32(2.0 ** mantissa_bits)
            q = jnp.round(x * s) / s
            return x + jax.lax.stop_gradient(q - x)

        def pwlin_gelu_basic(x, mantissa_bits_in, mantissa_bits_out):
            xq = float2fix(x, mantissa_bits_in)
            y = jnp.interp(xq, _PWL_X, _PWL_Y)
            y = jnp.where(xq > 4.0, xq, jnp.where(xq < -4.0, jnp.float32(0.0), y))
            return float2fix(y, mantissa_bits_out)
        key = jax.random.key(seed)
        k_x, k_w1, k_b1, k_w2, k_b2 = jax.random.split(key, 5)
        dim, ff_dim = (128, 512)
        B, S = (32, 64)
        sc1 = 1.0 / np.sqrt(dim)
        sc2 = 1.0 / np.sqrt(ff_dim)
        return {'x': jax.random.normal(k_x, (B, S, dim), dtype=jnp.float32), 'w1': jax.random.uniform(k_w1, (dim, ff_dim), jnp.float32, -sc1, sc1), 'b1': jax.random.uniform(k_b1, (ff_dim,), jnp.float32, -sc1, sc1), 'w2': jax.random.uniform(k_w2, (ff_dim, dim), jnp.float32, -sc2, sc2), 'b2': jax.random.uniform(k_b2, (dim,), jnp.float32, -sc2, sc2)}
    _L1_ffn_all = _L1_ffn_setup()
    _L1_ffn_in = {k: v for k, v in _L1_ffn_all.items() if k in ('w1', 'b1', 'w2', 'b2')}
    del _L1_ffn_all
    return {'x': x, 'ctx_1024': ctx_1024, 'mask_Bx1x1xS2_fk0': mask_Bx1x1xS2_fk0, 'L0_attn_Wq': _L0_attn_in['Wq'], 'L0_attn_Wk': _L0_attn_in['Wk'], 'L0_attn_Wv': _L0_attn_in['Wv'], 'L0_attn_Wp': _L0_attn_in['Wp'], 'L0_attn_q_gain': _L0_attn_in['q_gain'], 'L0_xattn_Wq': _L0_xattn_in['Wq'], 'L0_xattn_bq': _L0_xattn_in['bq'], 'L0_xattn_Wk': _L0_xattn_in['Wk'], 'L0_xattn_bk': _L0_xattn_in['bk'], 'L0_xattn_Wv': _L0_xattn_in['Wv'], 'L0_xattn_bv': _L0_xattn_in['bv'], 'L0_xattn_Wo': _L0_xattn_in['Wo'], 'L0_xattn_bo': _L0_xattn_in['bo'], 'L0_ffn_gate_w': _L0_ffn_in['gate_w'], 'L0_ffn_w1': _L0_ffn_in['w1'], 'L0_ffn_w2': _L0_ffn_in['w2'], 'L0_ffn_w3': _L0_ffn_in['w3'], 'L1_attn_Wqk_w': _L1_attn_in['Wqk_w'], 'L1_attn_Wqk_b': _L1_attn_in['Wqk_b'], 'L1_attn_Wv_w': _L1_attn_in['Wv_w'], 'L1_attn_Wv_b': _L1_attn_in['Wv_b'], 'L1_attn_Wn_w': _L1_attn_in['Wn_w'], 'L1_attn_Wn_b': _L1_attn_in['Wn_b'], 'L1_attn_Wo_w': _L1_attn_in['Wo_w'], 'L1_attn_Wo_b': _L1_attn_in['Wo_b'], 'L1_ffn_w1': _L1_ffn_in['w1'], 'L1_ffn_b1': _L1_ffn_in['b1'], 'L1_ffn_w2': _L1_ffn_in['w2'], 'L1_ffn_b2': _L1_ffn_in['b2']}

def reference(x, ctx_1024, mask_Bx1x1xS2_fk0, L0_attn_Wq, L0_attn_Wk, L0_attn_Wv, L0_attn_Wp, L0_attn_q_gain, L0_xattn_Wq, L0_xattn_bq, L0_xattn_Wk, L0_xattn_bk, L0_xattn_Wv, L0_xattn_bv, L0_xattn_Wo, L0_xattn_bo, L0_ffn_gate_w, L0_ffn_w1, L0_ffn_w2, L0_ffn_w3, L1_attn_Wqk_w, L1_attn_Wqk_b, L1_attn_Wv_w, L1_attn_Wv_b, L1_attn_Wn_w, L1_attn_Wn_b, L1_attn_Wo_w, L1_attn_Wo_b, L1_ffn_w1, L1_ffn_b1, L1_ffn_w2, L1_ffn_b2):
    import jax
    import jax.numpy as jnp

    def _L0_attn_ref(x, Wq, Wk, Wv, Wp, q_gain):
        import jax, jax.numpy as jnp
        import numpy as np
        DIM = 128
        NUM_HEADS = 16
        NUM_KV_HEADS = 4
        HEAD_DIM = DIM // NUM_HEADS
        ROPE_BASE = 10000.0
        EPS = 1e-08
        BSZ, SEQ = (8, 128)

        def bitlinear(x, w, eps=EPS):
            alpha = jax.lax.stop_gradient(jnp.maximum(jnp.mean(jnp.abs(w)), eps))
            w_t = jnp.round(jnp.clip(w / alpha, -1.0, 1.0))
            w_q = w + jax.lax.stop_gradient(w_t * alpha - w)
            gamma = jax.lax.stop_gradient(jnp.maximum(jnp.max(jnp.abs(x), axis=-1, keepdims=True), eps) / 127.0)
            x_int = jnp.round(jnp.clip(x / gamma, -128.0, 127.0))
            x_q = x + jax.lax.stop_gradient(x_int * gamma - x)
            return x_q @ (w_q / alpha).T * alpha

        def rms_norm(x):
            eps = jnp.finfo(x.dtype).eps
            return x * jax.lax.rsqrt(jnp.mean(x * x, axis=-1, keepdims=True) + eps)

        def rope_cache(seq_len, head_dim, base):
            inv_freq = 1.0 / base ** (jnp.arange(0, head_dim, 2, dtype=jnp.float32) / head_dim)
            t = jnp.arange(seq_len, dtype=jnp.float32)
            freqs = jnp.outer(t, inv_freq)
            return (jnp.cos(freqs), jnp.sin(freqs))

        def apply_rotary(x, cos, sin):
            half = x.shape[-1] // 2
            x1, x2 = (x[..., :half], x[..., half:])
            return jnp.concatenate((x1 * cos + x2 * sin, -x1 * sin + x2 * cos), axis=-1)
        bsz, seqlen, dim = x.shape
        q = bitlinear(x, Wq).reshape(bsz, seqlen, NUM_HEADS, HEAD_DIM).transpose(0, 2, 1, 3)
        k = bitlinear(x, Wk).reshape(bsz, seqlen, NUM_KV_HEADS, HEAD_DIM).transpose(0, 2, 1, 3)
        v = bitlinear(x, Wv).reshape(bsz, seqlen, NUM_KV_HEADS, HEAD_DIM).transpose(0, 2, 1, 3)
        q = rms_norm(q)
        k = rms_norm(k)
        cos, sin = rope_cache(seqlen, HEAD_DIM, ROPE_BASE)
        q = apply_rotary(q, cos, sin)
        k = apply_rotary(k, cos, sin)
        q = q * q_gain[None, :, None, None]
        rep = NUM_HEADS // NUM_KV_HEADS
        k = jnp.repeat(k, rep, axis=1)
        v = jnp.repeat(v, rep, axis=1)
        scale = 1.0 / jnp.sqrt(jnp.float32(HEAD_DIM))
        scores = jnp.einsum('bhqd,bhkd->bhqk', q, k) * scale
        causal = jnp.tril(jnp.ones((seqlen, seqlen), dtype=bool))
        scores = jnp.where(causal, scores, jnp.finfo(scores.dtype).min)
        attn = jax.nn.softmax(scores, axis=-1)
        y = jnp.einsum('bhqk,bhkd->bhqd', attn, v)
        y = y.transpose(0, 2, 1, 3).reshape(bsz, seqlen, dim)
        return bitlinear(y, Wp)

    def _L0_xattn_ref(v, k, q, mask, Wq, bq, Wk, bk, Wv, bv, Wo, bo):
        import jax, jax.numpy as jnp
        import numpy as np
        B, S, D, H = (4, 256, 128, 16)
        DEPTH = D // H

        def _split_heads(x):
            b, s, _ = x.shape
            return x.reshape(b, s, H, DEPTH).transpose(0, 2, 1, 3)
        qh = _split_heads(q @ Wq + bq)
        kh = _split_heads(k @ Wk + bk)
        vh = _split_heads(v @ Wv + bv)
        logits = jnp.einsum('bhqd,bhkd->bhqk', qh, kh) / jnp.sqrt(jnp.asarray(DEPTH, dtype=qh.dtype))
        logits = logits + mask * -1000000000.0
        attn = jax.nn.softmax(logits, axis=-1)
        out = jnp.einsum('bhqk,bhkd->bhqd', attn, vh)
        out = out.transpose(0, 2, 1, 3).reshape(q.shape[0], -1, D)
        return out @ Wo + bo

    def _L0_ffn_ref(hidden_states, gate_w, w1, w2, w3):
        import jax, jax.numpy as jnp
        import numpy as np
        E = 8
        JITTER = 0.01

        def _sparse_mixer_routing(logits):
            top_vals, top_idx = jax.lax.top_k(logits, 2)
            eidx = jnp.arange(logits.shape[-1])

            def _multiplier(thr, base_logits, idx):
                factor = jnp.maximum(jnp.abs(logits), thr)
                mask = (thr - logits) / factor > 2.0 * JITTER
                probs = jax.nn.softmax(jnp.where(mask, -jnp.inf, base_logits), axis=-1)
                return jnp.take_along_axis(probs, idx, axis=-1)
            mult1 = _multiplier(top_vals[:, :1], logits, top_idx[:, :1])
            scat = jnp.where(eidx[None, :] == top_idx[:, :1], -jnp.inf, logits)
            mult2 = _multiplier(top_vals[:, 1:2], scat, top_idx[:, 1:2])
            return (jnp.concatenate([mult1, mult2], axis=-1), top_idx)
        B, S, H = hidden_states.shape
        x = hidden_states.reshape(-1, H)
        logits = x @ gate_w
        mult, sel = _sparse_mixer_routing(logits)
        w = jnp.sum(mult[:, :, None] * (sel[:, :, None] == jnp.arange(E)[None, None, :]), axis=1)
        h = jax.nn.silu(jnp.einsum('th,ehf->etf', x, w1)) * jnp.einsum('th,ehf->etf', x, w3)
        out = jnp.einsum('etf,efh,te->th', h, w2, w)
        return out.reshape(B, S, H)

    def _L1_attn_ref(x, Wqk_w, Wqk_b, Wv_w, Wv_b, Wn_w, Wn_b, Wo_w, Wo_b):
        import jax, jax.numpy as jnp
        import numpy as np
        D_MODEL = 128
        D_QK = 128
        H = 16
        HEAD_DIM = D_QK // H
        V_DIM = D_MODEL // H
        B, S = (2, 256)
        b, s, _ = x.shape
        qk = x @ Wqk_w.T + Wqk_b
        qk = qk.reshape(b, s, 2, H, HEAD_DIM)
        q, k = (qk[:, :, 0], qk[:, :, 1])
        v = (x @ Wv_w.T + Wv_b).reshape(b, s, H, V_DIM)
        n = jnp.exp(-(x @ Wn_w.T + Wn_b))
        kv = jnp.einsum('bshd,bsht->bshdt', k, v)
        kv = jnp.cumsum(kv, axis=1)
        out = jnp.einsum('bshd,bshdt->bsht', q, kv)
        out = n[..., None] * out
        out = out.reshape(b, s, D_MODEL)
        return out @ Wo_w.T + Wo_b

    def _L1_xattn_ref(img_feat, text_feat):
        import jax, jax.numpy as jnp
        import numpy as np
        EPS = 1e-12

        def _l2norm(x):
            n = jnp.linalg.norm(x, axis=-1, keepdims=True)
            return x / jnp.maximum(n, EPS)
        img_norm = _l2norm(img_feat)
        text_norm = _l2norm(text_feat)
        sim = jnp.einsum('bic,btc->bit', img_norm, text_norm)
        min_idx = jnp.argmax(sim, axis=-1)
        text_aligned = jnp.take_along_axis(text_feat, min_idx[..., None], axis=1)
        return text_aligned

    def _L1_ffn_ref(x, w1, b1, w2, b2):
        import jax, jax.numpy as jnp
        import numpy as np
        MANT_BITS = 8
        _PWL_X = jnp.linspace(-4.0, 4.0, 33, dtype=jnp.float32)
        _PWL_Y = 0.5 * _PWL_X * (1.0 + jax.lax.erf(_PWL_X / jnp.sqrt(jnp.float32(2.0))))

        def float2fix(x, mantissa_bits):
            s = jnp.float32(2.0 ** mantissa_bits)
            q = jnp.round(x * s) / s
            return x + jax.lax.stop_gradient(q - x)

        def pwlin_gelu_basic(x, mantissa_bits_in, mantissa_bits_out):
            xq = float2fix(x, mantissa_bits_in)
            y = jnp.interp(xq, _PWL_X, _PWL_Y)
            y = jnp.where(xq > 4.0, xq, jnp.where(xq < -4.0, jnp.float32(0.0), y))
            return float2fix(y, mantissa_bits_out)
        h = jnp.einsum('bsd,df->bsf', x, w1) + b1
        h = float2fix(h, MANT_BITS)
        h = pwlin_gelu_basic(h, MANT_BITS, MANT_BITS)
        h = float2fix(h, MANT_BITS)
        out = jnp.einsum('bsf,fd->bsd', h, w2) + b2
        return float2fix(out, MANT_BITS)
    x = x + _L0_attn_ref(_layernorm(x, axis=-1), L0_attn_Wq, L0_attn_Wk, L0_attn_Wv, L0_attn_Wp, L0_attn_q_gain)
    x = x + _L0_xattn_ref(ctx_1024, ctx_1024, _layernorm(x, axis=-1), mask_Bx1x1xS2_fk0, L0_xattn_Wq, L0_xattn_bq, L0_xattn_Wk, L0_xattn_bk, L0_xattn_Wv, L0_xattn_bv, L0_xattn_Wo, L0_xattn_bo)
    x = x + _L0_ffn_ref(_layernorm(x, axis=-1), L0_ffn_gate_w, L0_ffn_w1, L0_ffn_w2, L0_ffn_w3)
    x = x + _L1_attn_ref(_layernorm(x, axis=-1), L1_attn_Wqk_w, L1_attn_Wqk_b, L1_attn_Wv_w, L1_attn_Wv_b, L1_attn_Wn_w, L1_attn_Wn_b, L1_attn_Wo_w, L1_attn_Wo_b)
    x = x + _L1_xattn_ref(_layernorm(x, axis=-1), ctx_1024)
    x = x + _L1_ffn_ref(_layernorm(x, axis=-1), L1_ffn_w1, L1_ffn_b1, L1_ffn_w2, L1_ffn_b2)
    return x

_drawn_inputs = setup_inputs


def setup_inputs(seed=0):
    import zlib

    import numpy as np

    out = dict(_drawn_inputs(seed))
    spreads = {'L0_attn_q_gain': (1.0, 0.6),
     'L0_xattn_bq': (0.0, 0.1),
     'L0_xattn_bk': (0.0, 2.0),
     'L0_xattn_bv': (0.0, 0.1),
     'L0_xattn_bo': (0.0, 0.1)}
    factors = {'L0_attn_Wq': 8.0,
     'L0_attn_Wk': 7.639,
     'L0_attn_Wv': 4.258,
     'L0_attn_Wp': 4.252,
     'L1_attn_Wqk_b': 2.827,
     'L1_attn_Wv_b': 3.092,
     'L1_attn_Wn_b': 6.505,
     'L1_attn_Wo_b': 200.0,
     'L1_ffn_w1': 8.0,
     'L1_ffn_b1': 31.829,
     'L1_ffn_w2': 8.0,
     'L1_ffn_b2': 200.0}
    for name, (base, spread) in spreads.items():
        noise = np.random.default_rng([zlib.crc32(name.encode()), seed]).standard_normal(out[name].shape)
        drawn = base * np.exp(spread * noise) if base else spread * noise
        out[name] = jnp.asarray(drawn.astype(out[name].dtype))
    for name, factor in factors.items():
        out[name] = (out[name] * factor).astype(out[name].dtype)
    return out
```

```python
from contextlib import ExitStack

import numpy as np

import concourse.bass as bass
from concourse import mybir

F32 = mybir.dt.float32
BF16 = mybir.dt.bfloat16
ALU = mybir.AluOpType
ACT = mybir.ActivationFunctionType
X = mybir.AxisListType.X

P = 128
D = 128
BATCH, SEQ = 16, 64
NT = BATCH * SEQ // P
H, HD, NG, NR = 16, 8, 4, 4
E, F, FC = 8, 512, 4
SCALE = float(1.0 / np.sqrt(np.float32(HD)))
MASKED = -1.0e30
MAGIC = 1.5 * 2.0 ** 23
LN_EPS = 1e-5
RMS_EPS = float(np.finfo(np.float32).eps)
AUG = HD + 1
OW = H * AUG
FIX = 256.0
JITTER = 0.01


def build(nc, d, out):
    ctx = ExitStack()
    with ctx:
        def sb(name, shape, dt=F32):
            return ctx.enter_context(nc.sbuf_tensor(name, shape, dt))

        def sem(name):
            return ctx.enter_context(nc.semaphore(name))

        x = sb("x", [P, NT, D])
        text = sb("text", [P, NT, D])
        textT = sb("textT", [P, NT, 4 * 64])
        tnormT = sb("tnormT", [P, NT, P])
        consts = sb("consts", [P, d["consts"].shape[1]])
        at = [0]

        def const(*shape):
            n = int(np.prod(shape))
            ap = consts[:, at[0]:at[0] + n]
            at[0] += n
            if len(shape) == 2:
                ap = ap.rearrange("p (a b) -> p a b", b=shape[1])
            return ap

        ident, pairI, dup = const(P), const(64), const(2, P)
        gmask, hmask = const(NG), const(2)
        causal01, causal_add = const(64), const(64)
        rope_c, rope_s = const(20, HD), const(20, HD)
        iota8, iota64 = const(E), const(64)
        params = sb("params", [P, d["params"].shape[1]])
        at[0] = 0

        def param(*shape):
            n = int(np.prod(shape))
            ap = params[:, at[0]:at[0] + n]
            at[0] += n
            if len(shape) == 2:
                ap = ap.rearrange("p (a b) -> p a b", b=shape[1])
            return ap

        w_qkv, w_p = param(192), param(D)
        gain = param(20)
        w = {}
        for L in "BD":
            w[L, "q"], w[L, "k"] = param(8, P), param(8, P)
            w[L, "v"], w[L, "o"] = param(D), param(D)
            w[L, "bq"], w[L, "bv"], w[L, "bo"] = param(8), param(D), param(D)
        w_n, gate_w = param(H), param(E)
        f_w1, f_b1, f_w2, f_b2 = param(F), param(FC), param(FC, D), param(D)
        rows = sb("rows", [3, d["rows"].shape[1]])
        k_aug = {"B": rows[:, 0:512].rearrange("p (r m) -> p r m", r=NR),
                 "D": rows[0:1, 512:1024].rearrange("p (r m) -> p r m", r=NR)}
        mask_rows = rows[:, 1024:1536].rearrange("p (t k) -> p t k", t=NT)
        n_bias, one_row = rows[0:1, 1536:1552], rows[0:1, 1552:1680]

        w1s, w3s = sb("w1s", [P, E, F]), sb("w3s", [P, E, F])
        w2s = sb("w2s", [P, E, FC, D])

        identb = sb("identb", [P, P], BF16)
        causal_b = sb("causal_b", [P, 64], BF16)
        ones = sb("ones", [P, P])
        tern = sb("tern", [P, 320], BF16)
        tq = sb("tq", [P, 320])
        wabs = sb("wabs", [P, 4])
        alphas = sb("alphas", [P, 4])
        inv_alphas = sb("inv_alphas", [P, 4])
        alpha20 = sb("alpha20", [P, 20])
        cgain, sgain = sb("cgain", [P, 20, HD]), sb("sgain", [P, 20, HD])

        stats = sb("stats", [P, NT, 6])
        mv = sb("mv", [P, NT, 2])
        powed = sb("powed", [P, 2, NT])
        rstd = sb("rstd", [P, NT])
        norms = sb("norms", [P, NT])
        minus_half, half_ = sb("minus_half", [P, 20]), sb("half", [P, 20])
        small = sb("small", [P, 4])
        xn = sb("xn", [P, 2, D])
        xint = sb("xint", [P, 2, D], BF16)
        gam = sb("gam", [P, 2, 1])
        xnT = sb("xnT", [P, 2, 4 * 64])
        xintT = sb("xintT", [P, 2, P], BF16)
        sq = sb("sq", [P, 2, 20, HD])
        rr = sb("rr", [P, 3, 20])
        qn, m1, m2 = (sb(n, [P, 20, HD]) for n in ("qn", "m1", "m2"))
        gav = sb("gav", [P, 1])
        qpad = sb("qpad", [P, 2, NR, NG, 32])
        kpad = sb("kpad", [P, 2, NG, 32])
        vtok = sb("vtok", [P, 2, NG * HD])
        qT = sb("qT", [P, 2, NR, P])
        kbd = sb("kbd", [P, 2, NR, NG, 64])
        vbd = sb("vbd", [P, 2, 8, 2, 2 * AUG])
        probs = sb("probs", [P, 2, H, 64])
        mx = sb("mx", [P, H])
        pT = sb("pT", [P, 2, 8, P])
        rden = sb("rden", [P, H])
        nexp = sb("nexp", [P, 2, H])
        y = sb("y", [P, 2, H, HD])
        yint = sb("yint", [P, 2, D], BF16)
        ygam = sb("ygam", [P, 2, 1])
        yT = sb("yT", [P, 2, P])
        yintT = sb("yintT", [P, 2, P], BF16)
        qt = sb("qt", [P, D])

        xall = sb("xall", [P, NT, D])
        xallT = sb("xallT", [P, NT, P])
        xw = sb("xw", [P, 2, NT, D])
        xwT = sb("xwT", [P, 2, NT, P])
        sg = sb("sg", [P, 2, 512])
        hh = sb("hh", [P, 2, 512])
        oT = xwT[:, 0, :, :]
        lg = sb("lg", [P, NT, E])
        r8 = [sb(f"r8_{i}", [P, NT, E]) for i in range(7)]
        r1 = [sb(f"r1_{i}", [P, NT]) for i in range(6)]
        wt = sb("wt", [P, NT, E])
        sim, sim2 = sb("sim", [P, NT, 64]), sb("sim2", [P, NT, 64])
        pick = sb("pick", [P, NT, P])
        pickT = xwT[:, 1, :, :]
        ha, hi_, hn = ([w1s[:, 2 * k + i, :] for i in range(2)] for k in range(3))
        g0, g1 = ([w3s[:, 2 * k + i, :] for i in range(2)] for k in range(2))
        hd, fo = w3s[:, 4, :], w3s[:, 5, :]
        hq = w2s[:, :, :, :].rearrange("p e c n -> p (e c n)").rearrange("p (c n) -> p c n", c=FC)
        b1x = sb("b1x", [P, FC])
        quarter = sb("quarter", [P, 1])

        Sp = ctx.enter_context(nc.psum_tensor("Sp", [P, 2, 1024], F32))
        Tp = ctx.enter_context(nc.psum_tensor("Tp", [P, 1024], F32))
        Op = ctx.enter_context(nc.psum_tensor("Op", [P, 512], F32))
        Mp = ctx.enter_context(nc.psum_tensor("Mp", [P, 512], F32))

        dma_x, dma_text, dma_const, dma_param, dma_rows = (sem(n) for n in (
            "x_loaded", "text_loaded", "consts_loaded", "params_loaded", "rows_loaded"))
        dma_w = [sem(f"expert{e}_loaded") for e in range(E)]
        stored = sem("stored")
        presets = sem("presets_done")
        step = sem("dve_step")
        astep = sem("act_step")
        wabs_ready, alpha_mm, tern_ready = sem("wabs_ready"), sem("alpha_mm"), sem("tern_ready")
        tsum_ready, tnorm_ready = sem("tsum_ready"), sem("tnorm_ready")
        tn_ready, textT_mm, textT_in = sem("tn_ready"), sem("textT_mm"), sem("textT_in")
        names = ("var_ready rstd_ready rms_ready rms_in xn_ready xnT_mm xnT_in qkv_mm sq_ready pad_ready qk_mm q_in k_in v_in n_in scores_mm "
                 "shifted probs_ready pT_mm pT_in pv_mm y_ready yT_mm yT_in out_mm x_updated")
        A = {L: {n: sem(f"{L}_{n}") for n in names.split()} for L in "ABD"}
        C = {n: sem("C_" + n) for n in ("var_ready rstd_ready xn_ready xnT_mm xnT_in logits_mm z_ready zexp_ready xw_ready xwT_mm xwT_in gu_mm silu_ready "
                                        "h_ready down_mm oT_in y_mm x_updated").split()}
        G = {n: sem("G_" + n) for n in "var_ready rstd_ready norm_ready xn_ready xnT_mm xnT_in sim_mm pick_ready pickT_mm pickT_in got_mm x_updated".split()}
        Z = {n: sem("Z_" + n) for n in "var_ready rstd_ready xn_ready xnT_mm xnT_in h_mm h_in node_ready gelu_ready b1_ready hq_ready out_mm fin".split()}

        block = ctx.enter_context(nc.Block())

        @block.sync
        def _(sp):
            sp.dma_start(params[:, :], d["params"]).then_inc(dma_param, 16)
            sp.dma_start(text[:, :, :], d["ctx"].rearrange("(t p) n -> p t n", p=P)).then_inc(dma_text, 16)
            for e in range(E):
                sp.dma_start(w1s[:, e, :], d["w1"][e]).then_inc(dma_w[e], 16)
                sp.dma_start(w3s[:, e, :], d["w3"][e]).then_inc(dma_w[e], 16)
                sp.dma_start(w2s[:, e, :, :], d["w2"][e].rearrange("(c p) n -> p c n", p=P)).then_inc(dma_w[e], 16)
            for half in range(2):
                sp.wait_ge(Z["fin"], half + 1)
                sp.dma_start(out.rearrange("(t p) n -> p t n", p=P)[:, 4 * half:4 * half + 4, :],
                             x[:, 4 * half:4 * half + 4, :]).then_inc(stored, 16)
            sp.wait_ge(stored, 32)

        @block.gpsimd
        def _(pool):
            for z in (qpad, kpad, kbd, vbd, pick):
                nc.gpsimd.memset(z[:], 0.0).then_inc(presets, 1)
            nc.gpsimd.memset(ones[:], 1.0).then_inc(presets, 1)
            nc.gpsimd.memset(quarter[:], 0.25).then_inc(presets, 1)
            nc.gpsimd.memset(minus_half[:], -0.5).then_inc(presets, 1)
            nc.gpsimd.memset(half_[:], 0.5).then_inc(presets, 1)
            pool.wait_ge(presets, 9)
            nc.gpsimd.memset(vbd[0:64, :, :, :, HD:HD + 1], 1.0).then_inc(presets, 1)
            nc.gpsimd.memset(vbd[64:128, :, :, :, 2 * HD + 1:2 * HD + 2], 1.0).then_inc(presets, 1)

            def power(o, base, exponent):
                return nc.gpsimd.tensor_tensor(o, base, exponent[:, 0:o.shape[1]], ALU.pow)

            def rstds(s):
                pool.wait_ge(s["var_ready"], 1)
                power(rstd[:, :], powed[:, 0, :], minus_half).then_inc(s["rstd_ready"], 1)

            pool.wait_ge(tsum_ready, 1)
            power(norms[:, :], powed[:, 1, :], half_).then_inc(tnorm_ready, 1)
            rstds(A["A"])
            for t in range(NT):
                pool.wait_ge(A["A"]["rms_ready"], t + 1)
                power(rr[:, 1, :], rr[:, 2, :], minus_half).then_inc(A["A"]["rms_in"], 1)
            rstds(A["B"])
            rstds(C)
            rstds(A["D"])
            rstds(G)
            power(norms[:, :], powed[:, 1, :], half_).then_inc(G["norm_ready"], 1)
            rstds(Z)

        PRESETS = 11

        @block.tensor
        def _(pe):
            mm, tr = nc.tensor.matmul, nc.tensor.transpose
            pe.wait_ge(dma_const, 16)
            pe.wait_ge(presets, PRESETS)
            pe.wait_ge(wabs_ready, 4)
            mm(Mp[:, 0:4], ones[:, :], wabs[:, :], start=True, stop=True).then_inc(alpha_mm, 1)
            pe.wait_ge(dma_text, 16)
            for t in range(NT):
                if t:
                    pe.wait_ge(textT_in, 2 * t)
                for k in range(2):
                    src = text[:, t, :] if k == 0 else xall[:, t, :]
                    if k == 1:
                        pe.wait_ge(tn_ready, t + 1)
                    tr(Sp[:, k, 0:P], src, ident).then_inc(textT_mm, 1)
            pe.wait_ge(dma_param, 16)
            pe.wait_ge(dma_rows, 16)

            def attention(L, prev, prev_n):
                s = A[L]

                def front(t):
                    b = t % 2
                    if t and L != "A":
                        pe.wait_ge(s["v_in"], t)
                    if t >= 3:
                        pe.wait_ge(s["x_updated"], t - 2)
                    pe.wait_ge(s["xn_ready"], t + 1)
                    if L == "A":
                        tr(Mp[:, 0:64].bitcast(BF16), xint[:, b, :], identb[:, :]).then_inc(s["xnT_mm"], 1)
                        pe.wait_ge(s["xnT_in"], t + 1)
                        mm(Mp[:, 128:320], xintT[:, b, :], tern[:, 0:192], start=True, stop=True).then_inc(s["qkv_mm"], 1)
                        return
                    tr(Mp[:, 0:P], xn[:, b, :], ident).then_inc(s["xnT_mm"], 1)
                    if t >= 2:
                        pe.wait_ge(s["shifted"], t - 1)
                    pe.wait_ge(s["xnT_in"], t + 1)
                    src = textT[:, t, :] if L == "B" else xnT[:, b, :]
                    for r in range(NR):
                        for half in range(2):
                            mm(Sp[:, b, r * P + half * 64:r * P + half * 64 + 64], w[L, "q"][:, 2 * r + half, :],
                               xnT[:, b, P * half:P * half + 64], start=True, stop=True)
                    aug = mask_rows[:, t, :] if L == "B" else one_row[:, 0:64]
                    for r in range(NR):
                        o = Sp[:, b, 512 + 64 * r:512 + 64 * r + 64]
                        mm(o, w[L, "k"][:, 2 * r, :], src[:, 0:64], start=True, stop=False)
                        mm(o, w[L, "k"][:, 2 * r + 1, :], src[:, P:P + 64], start=False, stop=False)
                        mm(o, k_aug[L][:, r, :], aug, start=False, stop=True)
                    if L == "D":
                        o = Sp[:, b, 768:768 + H]
                        mm(o, xnT[:, b, 64:64 + P], w_n, start=True, stop=False)
                        mm(o, one_row, n_bias, start=False, stop=True)
                    for half in range(2):
                        ins = mm(Mp[:, 128 + 128 * half:256 + 128 * half], src[:, P * half:P * half + P], w[L, "v"], start=True, stop=True)
                    ins.then_inc(s["qk_mm"], 1)

                def turn(t):
                    b = t % 2
                    if t >= 2:
                        pe.wait_ge(s["shifted"], t - 1)
                    pe.wait_ge(s["pad_ready"], t + 1)
                    for r in range(NR):
                        tr(Sp[:, b, r * P:r * P + P], qpad[:, b, r, :, :].rearrange("p g c -> p (g c)"), ident)
                    mm(Sp[:, b, 512:576], kpad[:, b, :, :].rearrange("p g c -> p (g c)"), pairI, start=True, stop=True)
                    for half in range(2):
                        ins = mm(Sp[:, b, 640 + 32 * half:672 + 32 * half], dup[:, half, :], vtok[:, b, :],
                                 start=True, stop=True)
                    ins.then_inc(s["qk_mm"], 1)

                def scores(t):
                    b = t % 2
                    pe.wait_ge(s["q_in"], t + 1)
                    pe.wait_ge(s["k_in"], t + 1)
                    if L == "A":
                        pe.wait_ge(s["v_in"], t + 1)
                    if L == "D":
                        pe.wait_ge(s["n_in"], t + 1)
                    for r in range(NR):
                        if L == "A" and r % 2 == 0:
                            mm(Sp[:, b, 256 * r:256 * r + 512], identb[:, :],
                               causal_b[:, :].unsqueeze(1).to_broadcast([P, 8, 64]), start=True, stop=False,
                               skip_group_check=True)
                        k = kbd[:, b, 0 if L == "A" else r, :, :].rearrange("p g c -> p (g c)")
                        ins = mm(Sp[:, b, 256 * r:256 * r + 256], qT[:, b, r, :], k, start=L != "A", stop=True,
                                 skip_group_check=L == "A")
                    ins.then_inc(s["scores_mm"], 1)

                def turn_probs(t):
                    b = t % 2
                    pe.wait_ge(s["probs_ready"] if L != "D" else s["shifted"], t + 1)
                    if t:
                        pe.wait_ge(s["pT_in"], 2 * t)
                    flat = probs[:, b, :, :].rearrange("p h k -> p (h k)")
                    for j in range(8):
                        ins = tr(Tp[:, j * P:j * P + P], flat[:, j * P:j * P + P], ident)
                        if j % 4 == 3:
                            ins.then_inc(s["pT_mm"], 1)

                def values(t):
                    b = t % 2
                    pe.wait_ge(s["v_in"], t + 1)
                    if t:
                        pe.wait_ge(s["y_ready"], t)
                    o = Op[:, 0:2 * OW].rearrange("p (a c) -> p a c", a=2)
                    for j in range(8):
                        if j % 4 == 0:
                            pe.wait_ge(s["pT_in"], 2 * t + 1 + j // 4)
                        v = vbd[:, b, j % 2 if L == "A" else j, :, :]
                        ins = mm(o[:, :, 2 * AUG * j:2 * AUG * j + 2 * AUG], pT[:, b, j, :], v, start=True, stop=True)
                    ins.then_inc(s["pv_mm"], 1)

                def tail(t):
                    b = t % 2
                    pe.wait_ge(s["y_ready"], t + 1)
                    if t:
                        pe.wait_ge(s["x_updated"], t)
                    pe.wait_ge(s["pad_ready"] if L == "A" else s["v_in"], min(t + 3, NT))
                    if L == "A":
                        tr(Mp[:, 0:64].bitcast(BF16), yint[:, b, :], identb[:, :]).then_inc(s["yT_mm"], 1)
                        pe.wait_ge(s["yT_in"], t + 1)
                        mm(Mp[:, 384:512], yintT[:, b, :], tern[:, 192:320], start=True, stop=True).then_inc(s["out_mm"], 1)
                        return
                    tr(Mp[:, 0:P], y[:, b, :, :].rearrange("p h c -> p (h c)"), ident).then_inc(s["yT_mm"], 1)
                    pe.wait_ge(s["yT_in"], t + 1)
                    mm(Mp[:, 384:512], yT[:, b, :], w[L, "o"], start=True, stop=True).then_inc(s["out_mm"], 1)

                pe.wait_ge(prev, prev_n)
                if L == "A":
                    pe.wait_ge(tern_ready, 2)
                front(0)
                if L == "A":
                    turn(0)
                for t in range(NT):
                    scores(t)
                    if t + 1 < NT:
                        front(t + 1)
                    turn_probs(t)
                    if t + 1 < NT and L == "A":
                        turn(t + 1)
                    values(t)
                    if t:
                        tail(t - 1)
                tail(NT - 1)

            def turn_all(s, prev, prev_n):
                pe.wait_ge(prev, prev_n)
                for t in range(NT):
                    pe.wait_ge(s["xn_ready"], t + 1)
                    if t >= 2:
                        pe.wait_ge(s["xnT_in"], t - 1)
                    tr(Tp[:, 512 * (t % 2):512 * (t % 2) + P], xall[:, t, :], ident).then_inc(s["xnT_mm"], 1)

            attention("A", textT_in, 2 * NT)
            attention("B", A["A"]["x_updated"], NT)

            turn_all(C, A["B"]["x_updated"], NT)
            for t in range(NT):
                pe.wait_ge(C["xnT_in"], t + 1)
                ins = mm(Mp[:, E * t:E * t + E], xallT[:, t, :], gate_w, start=True, stop=True)
            ins.then_inc(C["logits_mm"], 1)
            units = [(e, half, c) for e in range(E) for half in range(2) for c in range(FC)]

            def turn_xw(e):
                pe.wait_ge(C["xw_ready"], e + 1)
                if e:
                    pe.wait_ge(C["xwT_in"], 2 * e)
                for t in range(NT):
                    ins = tr(Tp[:, t * P:t * P + P], xw[:, e % 2, t, :], ident)
                    if t % 4 == 3:
                        ins.then_inc(C["xwT_mm"], 1)

            def down(u):
                e, half, c = units[u]
                pe.wait_ge(C["h_ready"], u + 1)
                acc = Op if half == 0 else Mp
                mm(acc[:, :], w2s[:, e, c, :], hh[:, u % 2, :], start=(e == 0 and c == 0),
                   stop=(e == E - 1 and c == FC - 1)).then_inc(C["down_mm"], 1)

            turn_xw(0)
            for u, (e, half, c) in enumerate(units):
                if half == 0 and c == 0:
                    pe.wait_ge(dma_w[e], 48)
                if c == 0:
                    pe.wait_ge(C["xwT_in"], 2 * e + half + 1)
                if u >= 2:
                    pe.wait_ge(C["h_ready"], u - 1)
                xs = xallT[:, 4 * half:4 * half + 4, :].rearrange("p t n -> p (t n)")
                xws = xwT[:, e % 2, 4 * half:4 * half + 4, :].rearrange("p t n -> p (t n)")
                mm(Sp[:, u % 2, 0:512], w1s[:, e, c * P:c * P + P], xs, start=True, stop=True)
                mm(Sp[:, u % 2, 512:1024], w3s[:, e, c * P:c * P + P], xws, start=True, stop=True)\
                    .then_inc(C["gu_mm"], 1)
                if u:
                    down(u - 1)
                if half == 1 and c == 1 and e + 1 < E:
                    turn_xw(e + 1)
            down(len(units) - 1)
            for t in range(NT):
                pe.wait_ge(C["oT_in"], t // 4 + 1)
                ins = tr(Tp[:, t * P:t * P + P], oT[:, t, :], ident)
                if t % 4 == 3:
                    ins.then_inc(C["y_mm"], 1)

            attention("D", C["x_updated"], 2)

            turn_all(G, A["D"]["x_updated"], NT)
            for t in range(NT):
                pe.wait_ge(G["xnT_in"], t + 1)
                for half in range(2):
                    c = slice(64 * half, 64 * half + 64)
                    ins = mm(Op[c, 64 * t:64 * t + 64], xallT[:, t, c], tnormT[:, t, c], start=True, stop=True)
            ins.then_inc(G["sim_mm"], 1)
            pe.wait_ge(G["pick_ready"], 2)
            for t in range(NT):
                ins = tr(Tp[:, t * P:t * P + P], pick[:, t, :], ident)
                if t % 4 == 3:
                    ins.then_inc(G["pickT_mm"], 1)
            for t in range(NT):
                pe.wait_ge(G["pickT_in"], t // 4 + 1)
                ins = mm(Sp[:, 0, t * P:t * P + P], pickT[:, t, :], text[:, t, :], start=True, stop=True)
                if t % 4 == 3:
                    ins.then_inc(G["got_mm"], 1)

            turn_all(Z, G["x_updated"], 2)
            for u in range(2 * FC):
                half, c = divmod(u, FC)
                pe.wait_ge(Z["xnT_in"], 4 * half + 4)
                if u >= 2:
                    pe.wait_ge(Z["h_in"], u - 1)
                mm(Sp[:, u % 2, 0:512], f_w1[:, c * P:c * P + P],
                   xallT[:, 4 * half:4 * half + 4, :].rearrange("p t n -> p (t n)"), start=True, stop=True)\
                    .then_inc(Z["h_mm"], 1)
            for t in range(NT):
                pe.wait_ge(Z["hq_ready"], FC * (t // 4 + 1))
                acc = Op if t < 4 else Mp
                for c in range(FC):
                    ins = mm(acc[:, (t % 4) * P:(t % 4) * P + P], hq[:, c, t * P:t * P + P], f_w2[:, c, :],
                             start=(c == 0), stop=(c == FC - 1))
                if t % 4 == 3:
                    ins.then_inc(Z["out_mm"], 1)

        @block.scalar
        def _(act):
            act.dma_start(consts[:, :], d["consts"]).then_inc(dma_const, 16)
            act.dma_start(x[:, :, :], d["x"].rearrange("(t p) n -> p t n", p=P)).then_inc(dma_x, 16)
            act.dma_start(rows[:, :], d["rows"]).then_inc(dma_rows, 16)

            def copy(o, i):
                return nc.scalar.activation(o, i, ACT.Copy)

            def copy_twice(o, i):
                return copy(o.rearrange("p (a w n) -> p a w n", a=2, w=2),
                            i.rearrange("p (a n) -> p a n", a=2).unsqueeze(2).to_broadcast([P, 2, 2, 64]))

            for t in range(NT):
                for k in range(2):
                    act.wait_ge(textT_mm, 2 * t + k + 1)
                    if k == 0:
                        copy_twice(textT[:, t, :], Sp[:, k, 0:P]).then_inc(textT_in, 1)
                    else:
                        copy(tnormT[:, t, :], Sp[:, k, 0:P]).then_inc(textT_in, 1)

            def attention(L):
                s = A[L]

                def front(t):
                    b = t % 2
                    act.wait_ge(s["xnT_mm"], t + 1)
                    if t >= 2:
                        act.wait_ge(s["qkv_mm"] if L == "A" else s["qk_mm"], t - 1)
                    if L == "A":
                        copy(xintT[:, b, :], Mp[:, 0:64].bitcast(BF16)).then_inc(s["xnT_in"], 1)
                    else:
                        copy_twice(xnT[:, b, :], Mp[:, 0:P]).then_inc(s["xnT_in"], 1)

                def square(t):
                    b = t % 2
                    act.wait_ge(s["qkv_mm"], t + 1)
                    if t >= 2:
                        act.wait_ge(s["pad_ready"], t - 1)
                    nc.scalar.activation(sq[:, b, :, :].rearrange("p s c -> p (s c)"), Mp[:, 128:288], ACT.Square)\
                        .then_inc(s["sq_ready"], 1)

                def keys(t):
                    b = t % 2
                    act.wait_ge(s["qk_mm"], t + 1)
                    if t >= 2:
                        act.wait_ge(s["scores_mm"], t - 1)
                    if L == "A":
                        copy(qT[:, b, :, :].rearrange("p r n -> p (r n)"), Sp[:, b, 0:512]).then_inc(s["q_in"], 1)
                        return
                    for g in range(NG):
                        c = slice(32 * g, 32 * g + 32)
                        ins = copy(kbd[c, b, :, g, :], Sp[c, b, 512:768].rearrange("p (r k) -> p r k", r=NR))
                    ins.then_inc(s["k_in"], 1)
                    if L == "D":
                        if t >= 2:
                            act.wait_ge(s["y_ready"], t - 1)
                        nc.scalar.activation(nexp[:, b, :], Sp[:, b, 768:768 + H], ACT.Exp, scale=-1.0)\
                            .then_inc(s["n_in"], 1)

                def exps(t):
                    b = t % 2
                    act.wait_ge(s["shifted"], t + 1)
                    e = probs[:, b, :, :].rearrange("p h k -> p (h k)")
                    nc.scalar.activation(e, e, ACT.Exp, scale=SCALE).then_inc(s["probs_ready"], 1)

                def turned(t):
                    b = t % 2
                    if t >= 2:
                        act.wait_ge(s["pv_mm"], t - 1)
                    for k in range(2):
                        act.wait_ge(s["pT_mm"], 2 * t + k + 1)
                        copy(pT[:, b, 4 * k:4 * k + 4, :].rearrange("p j n -> p (j n)"),
                             Tp[:, 512 * k:512 * k + 512]).then_inc(s["pT_in"], 1)

                def tail(t):
                    b = t % 2
                    act.wait_ge(s["yT_mm"], t + 1)
                    if t >= 2:
                        act.wait_ge(s["out_mm"], t - 1)
                    if L == "A":
                        copy(yintT[:, b, :], Mp[:, 0:64].bitcast(BF16)).then_inc(s["yT_in"], 1)
                    else:
                        copy(yT[:, b, :], Mp[:, 0:P]).then_inc(s["yT_in"], 1)

                front(0)
                if L == "A":
                    square(0)
                keys(0)
                for t in range(NT):
                    if t + 1 < NT:
                        front(t + 1)
                    if L != "D":
                        exps(t)
                    if t + 1 < NT and L == "A":
                        square(t + 1)
                    if t + 1 < NT and L != "A":
                        keys(t + 1)
                    turned(t)
                    if t + 1 < NT and L == "A":
                        keys(t + 1)
                    if t:
                        tail(t - 1)
                tail(NT - 1)

            def turned_all(s):
                for t in range(NT):
                    act.wait_ge(s["xnT_mm"], t + 1)
                    copy(xallT[:, t, :], Tp[:, 512 * (t % 2):512 * (t % 2) + P]).then_inc(s["xnT_in"], 1)

            attention("A")
            attention("B")

            turned_all(C)

            def turned_xw(e):
                for k in range(2):
                    act.wait_ge(C["xwT_mm"], 2 * e + k + 1)
                    if e >= 2:
                        act.wait_ge(C["gu_mm"], 8 * (e - 1))
                    copy(xwT[:, e % 2, 4 * k:4 * k + 4, :].rearrange("p t n -> p (t n)"),
                         Tp[:, 512 * k:512 * k + 512]).then_inc(C["xwT_in"], 1)

            for k in range(2):
                act.wait_ge(C["z_ready"], k + 1)
                nc.scalar.activation(r8[5 + k][:, :, :], r8[5 + k][:, :, :], ACT.Exp).then_inc(C["zexp_ready"], 1)
            turned_xw(0)
            for u in range(E * 2 * FC):
                act.wait_ge(C["gu_mm"], u + 1)
                if u >= 2:
                    act.wait_ge(C["h_ready"], u - 1)
                nc.scalar.activation(sg[:, u % 2, :], Sp[:, u % 2, 0:512], ACT.Silu).then_inc(C["silu_ready"], 1)
                e, k = divmod(u, 8)
                if k == 6 and e + 1 < E:
                    turned_xw(e + 1)
            act.wait_ge(C["down_mm"], E * 2 * FC)
            for half in range(2):
                copy(oT[:, 4 * half:4 * half + 4, :].rearrange("p t n -> p (t n)"), (Op if half == 0 else Mp)[:, :])\
                    .then_inc(C["oT_in"], 1)

            attention("D")

            turned_all(G)
            for k in range(2):
                act.wait_ge(G["pickT_mm"], k + 1)
                copy(pickT[:, 4 * k:4 * k + 4, :].rearrange("p t n -> p (t n)"),
                     Tp[:, 512 * k:512 * k + 512]).then_inc(G["pickT_in"], 1)

            turned_all(Z)
            act.wait_ge(Z["b1_ready"], 1)
            act.wait_ge(presets, PRESETS)

            def gelus(u):
                b = u % 2
                act.wait_ge(Z["node_ready"], u + 1)
                nc.scalar.activation(g0[b], hn[b], ACT.Gelu, scale=0.25)
                nc.scalar.activation(g1[b], hn[b], ACT.Gelu, bias=quarter[:, :], scale=0.25)\
                    .then_inc(Z["gelu_ready"], 1)

            for u in range(2 * FC):
                c = u % FC
                act.wait_ge(Z["h_mm"], u + 1)
                if u >= 2:
                    act.wait_ge(Z["hq_ready"], u - 1)
                nc.scalar.activation(ha[u % 2], Sp[:, u % 2, 0:512], ACT.Identity, bias=b1x[:, c:c + 1],
                                     scale=FIX).then_inc(Z["h_in"], 1)
                if u:
                    gelus(u - 1)
            gelus(2 * FC - 1)

        @block.vector
        def _(dve):
            v = nc.vector
            count = [0]

            def link(ins):
                count[0] += 1
                ins.then_inc(step, 1)
                dve.wait_ge(step, count[0])

            def moments(s, l2=False):
                for t in range(NT):
                    ins = v.bn_stats(stats[:, t, :], x[:, t, :])
                link(ins)
                for t in range(NT):
                    ins = v.bn_aggr(mv[:, t, :], stats[:, t, :])
                link(ins)
                if l2:
                    v.tensor_scalar(powed[:, 1, :], mv[:, :, 1], float(D), None, ALU.mult)
                v.tensor_scalar(powed[:, 0, :], mv[:, :, 1], LN_EPS, None, ALU.add).then_inc(s["var_ready"], 1)
                dve.wait_ge(s["rstd_ready"], 1)
                if l2:
                    dve.wait_ge(s["norm_ready"], 1)
                    link(v.tensor_tensor(norms[:, :], norms[:, :], rstd[:, :], ALU.mult))
                    link(v.tensor_scalar(norms[:, :], norms[:, :], 1e-12, None, ALU.max))
                    link(v.reciprocal(norms[:, :], norms[:, :]))
                    link(v.tensor_tensor(rstd[:, :], rstd[:, :], norms[:, :], ALU.mult))

            def normalise(o, t):
                return v.tensor_scalar(o, x[:, t, :], mv[:, t, 0:1], rstd[:, t:t + 1], ALU.subtract, ALU.mult)

            def quantise(src, g, o):
                link(v.tensor_reduce(small[:, 0:1], src, X, ALU.max, apply_absolute_value=True))
                link(v.tensor_scalar(g, small[:, 0:1], 1e-8, 1.0 / 127.0, ALU.max, ALU.mult))
                link(v.reciprocal(small[:, 1:2], g))
                link(v.tensor_scalar(qt[:, :], src, small[:, 1:2], 127.0, ALU.mult, ALU.min))
                link(v.tensor_scalar(qt[:, :], qt[:, :], -128.0, MAGIC, ALU.max, ALU.add))
                return v.tensor_scalar(o, qt[:, :], MAGIC, None, ALU.subtract)

            dve.wait_ge(dma_param, 16)
            parts = ((0, 128), (128, 160), (160, 192))
            for i, (a, b) in enumerate(parts):
                v.tensor_reduce(wabs[:, i:i + 1], w_qkv[:, a:b], X, ALU.add, apply_absolute_value=True)\
                    .then_inc(wabs_ready, 1)
            v.tensor_reduce(wabs[:, 3:4], w_p, X, ALU.add, apply_absolute_value=True).then_inc(wabs_ready, 1)
            dve.wait_ge(dma_const, 16)
            v.tensor_copy(identb[:, :], ident).then_inc(tern_ready, 1)
            link(v.tensor_copy(causal_b[:, :], causal_add))
            link(v.tensor_tensor(cgain[:, :, :], rope_c, gain.unsqueeze(2).to_broadcast([P, 20, HD]), ALU.mult))
            link(v.tensor_tensor(sgain[:, :, :], rope_s, gain.unsqueeze(2).to_broadcast([P, 20, HD]), ALU.mult))
            dve.wait_ge(alpha_mm, 1)
            for i, n in enumerate((128, 32, 32, 128)):
                link(v.tensor_scalar(alphas[:, i:i + 1], Mp[:, i:i + 1], 1.0 / (n * D), 1e-8, ALU.mult, ALU.max))
            link(v.memset(alpha20[:, :], 1.0))
            link(v.tensor_scalar(alpha20[:, 0:16], alpha20[:, 0:16], alphas[:, 0:1], None, ALU.mult))
            link(v.tensor_scalar(alpha20[:, 16:20], alpha20[:, 16:20], alphas[:, 1:2], None, ALU.mult))
            link(v.reciprocal(inv_alphas[:, :], alphas[:, :]))
            for i, (a, b) in enumerate(parts + ((192, 320),)):
                src = w_qkv[:, a:b] if i < 3 else w_p
                link(v.tensor_scalar(tq[:, a:b], src, inv_alphas[:, i:i + 1], 1.0, ALU.mult, ALU.min))
            link(v.tensor_scalar(tq[:, :], tq[:, :], -1.0, MAGIC, ALU.max, ALU.add))
            v.tensor_scalar(tern[:, :], tq[:, :], MAGIC, None, ALU.subtract).then_inc(tern_ready, 1)

            dve.wait_ge(dma_text, 16)
            link(v.tensor_tensor(xall[:, :, :], text[:, :, :], text[:, :, :], ALU.mult))
            v.tensor_reduce(powed[:, 1, :], xall[:, :, :], X, ALU.add).then_inc(tsum_ready, 1)
            dve.wait_ge(tnorm_ready, 1)
            link(v.tensor_scalar(norms[:, :], norms[:, :], 1e-12, None, ALU.max))
            link(v.reciprocal(norms[:, :], norms[:, :]))
            for t in range(NT):
                v.tensor_scalar(xall[:, t, :], text[:, t, :], norms[:, t:t + 1], None, ALU.mult).then_inc(tn_ready, 1)
            dve.wait_ge(dma_x, 16)
            dve.wait_ge(presets, PRESETS)

            def attention(L):
                s = A[L]

                def front(t):
                    b = t % 2
                    if t >= 2:
                        dve.wait_ge(s["xnT_mm"], t - 1)
                    if L == "A":
                        link(normalise(xn[:, b, :], t))
                        quantise(xn[:, b, :], gam[:, b, :], xint[:, b, :]).then_inc(s["xn_ready"], 1)
                    else:
                        normalise(xn[:, b, :], t).then_inc(s["xn_ready"], 1)

                def rotate(t):
                    b = t % 2
                    link(v.tensor_scalar(rr[:, 0, :], alpha20[:, :], gam[:, b, :], None, ALU.mult))
                    link(v.tensor_tensor(gav[:, :], gam[:, b, :], alphas[:, 2:3], ALU.mult))
                    dve.wait_ge(s["sq_ready"], t + 1)
                    link(v.tensor_reduce(rr[:, 1, :], sq[:, b, :, :], X, ALU.add))
                    link(v.scalar_tensor_tensor(rr[:, 2, :], rr[:, 1, :], 1.0 / HD, rr[:, 0, :], ALU.mult, ALU.mult))
                    link(v.tensor_tensor(rr[:, 1, :], rr[:, 2, :], rr[:, 0, :], ALU.mult))
                    v.tensor_scalar(rr[:, 2, :], rr[:, 1, :], RMS_EPS, None, ALU.add).then_inc(s["rms_ready"], 1)
                    dve.wait_ge(s["rms_in"], t + 1)
                    link(v.tensor_tensor(rr[:, 1, :], rr[:, 1, :], rr[:, 0, :], ALU.mult))
                    qk = Mp[:, 128:288].rearrange("p (s c) -> p s c", c=HD)
                    link(v.tensor_tensor(qn[:, :, :], qk, rr[:, 1, :].unsqueeze(2).to_broadcast([P, 20, HD]), ALU.mult))
                    if t >= 2:
                        dve.wait_ge(s["qk_mm"], t - 1)
                    v.tensor_scalar(vtok[:, b, :], Mp[:, 288:320], gav[:, :], None, ALU.mult)
                    v.tensor_tensor(m1[:, :, :], qn[:, :, :], cgain[:, :, :], ALU.mult)
                    swapped = qn[:, :, :].rearrange("p s (u c) -> p s u c", u=2)[:, :, ::-1, :]
                    link(v.tensor_tensor(m2[:, :, :].rearrange("p s (u c) -> p s u c", u=2), swapped,
                                         sgain[:, :, :].rearrange("p s (u c) -> p s u c", u=2), ALU.mult))
                    for half in range(2):
                        c = slice(64 * half, 64 * half + 64)
                        o = slice(HD * half, HD * half + HD)
                        v.tensor_tensor(qpad[c, b, :, :, o], m1[c, 0:16, :].rearrange("p (r g) c -> p r g c", g=NG),
                                        m2[c, 0:16, :].rearrange("p (r g) c -> p r g c", g=NG), ALU.add)
                        ins = v.tensor_tensor(kpad[c, b, :, o], m1[c, 16:20, :], m2[c, 16:20, :], ALU.add)
                    ins.then_inc(s["pad_ready"], 1)

                def take(t):
                    b = t % 2
                    dve.wait_ge(s["qk_mm"], t + 1)
                    if L == "A":
                        k = Sp[:, b, 512:576].unsqueeze(1).to_broadcast([P, NG, 64])
                        v.tensor_tensor(kbd[:, b, 0, :, :], k, gmask.unsqueeze(2).to_broadcast([P, NG, 64]), ALU.mult)\
                            .then_inc(s["k_in"], 1)
                        vv = Sp[:, b, 640:704].rearrange("p (a j w c) -> p a j w c", a=2, j=2, w=2)
                        for w_ in range(2):
                            c = slice(64 * w_, 64 * w_ + 64)
                            ins = v.tensor_copy(vbd[c, b, 0:2, :, AUG * w_:AUG * w_ + HD].rearrange("p j a c -> p a j c"),
                                                vv[c, :, :, w_, :])
                        ins.then_inc(s["v_in"], 1)
                        return
                    v.tensor_tensor(qT[:, b, :, :].rearrange("p r (a n) -> p (r a) n", a=2),
                                    Sp[:, b, 0:512].rearrange("p (q n) -> p q n", n=64),
                                    w[L, "bq"].unsqueeze(2).to_broadcast([P, 8, 64]), ALU.add).then_inc(s["q_in"], 1)
                    vv = Mp[:, 128:384].rearrange("p (a j w c) -> p a j w c", a=2, j=8, w=2)
                    bv = w[L, "bv"].rearrange("p (j w c) -> p j w c", j=8, w=2)
                    for w_ in range(2):
                        c = slice(64 * w_, 64 * w_ + 64)
                        for half in range(2):
                            ins = v.tensor_tensor(vbd[c, b, :, half, AUG * w_:AUG * w_ + HD], vv[c, half, :, w_, :],
                                                  bv[c, :, w_, :], ALU.add)
                    ins.then_inc(s["v_in"], 1)

                def shift(t):
                    b = t % 2
                    dve.wait_ge(s["scores_mm"], t + 1)
                    sc = Sp[:, b, :].rearrange("p (h k) -> p h k", h=H)
                    if L == "D":
                        v.tensor_tensor(probs[:, b, :, :], sc, causal01.unsqueeze(1).to_broadcast([P, H, 64]), ALU.mult)\
                            .then_inc(s["shifted"], 1)
                        return
                    link(v.tensor_reduce(mx[:, :], sc, X, ALU.max))
                    v.tensor_tensor(probs[:, b, :, :], sc, mx[:, :].unsqueeze(2).to_broadcast([P, H, 64]), ALU.subtract)\
                        .then_inc(s["shifted"], 1)

                def norm(t):
                    b = t % 2
                    dve.wait_ge(s["pv_mm"], t + 1)
                    o = Op[:, 0:2 * OW].rearrange("p (a s c) -> p a s c", a=2, c=AUG)
                    if L == "D":
                        dve.wait_ge(s["n_in"], t + 1)
                    else:
                        v.reciprocal(rden[0:64, :], o[0:64, 0, :, HD])
                        link(v.reciprocal(rden[64:128, :], o[64:128, 1, :, HD]))
                    for half in range(2):
                        c = slice(64 * half, 64 * half + 64)
                        f = nexp[c, b, :] if L == "D" else rden[c, :]
                        ins = v.tensor_tensor(y[c, b, :, :], o[c, half, :, 0:HD],
                                              f.unsqueeze(2).to_broadcast([64, H, HD]), ALU.mult)
                        if L == "A" and half == 1:
                            link(ins)
                    if L == "A":
                        ins = quantise(y[:, b, :, :].rearrange("p h c -> p (h c)"), ygam[:, b, :], yint[:, b, :])
                    ins.then_inc(s["y_ready"], 1)

                def update(t):
                    b = t % 2
                    dve.wait_ge(s["out_mm"], t + 1)
                    if L == "A":
                        link(v.tensor_tensor(small[:, 3:4], ygam[:, b, :], alphas[:, 3:4], ALU.mult))
                        v.scalar_tensor_tensor(x[:, t, :], Mp[:, 384:512], small[:, 3:4], x[:, t, :], ALU.mult, ALU.add)\
                            .then_inc(s["x_updated"], 1)
                    else:
                        link(v.tensor_tensor(qt[:, :], Mp[:, 384:512], w[L, "bo"], ALU.add))
                        v.tensor_tensor(x[:, t, :], x[:, t, :], qt[:, :], ALU.add).then_inc(s["x_updated"], 1)

                moments(s)
                front(0)
                front(1)
                if L == "A":
                    rotate(0)
                take(0)
                for t in range(NT):
                    shift(t)
                    if t + 1 < NT:
                        if L == "A":
                            rotate(t + 1)
                        take(t + 1)
                    norm(t)
                    if t:
                        update(t - 1)
                    if t + 2 < NT:
                        front(t + 2)
                update(NT - 1)
                dve.wait_ge(s["x_updated"], NT)

            def normalise_all(s, l2=False):
                moments(s, l2)
                for t in range(NT):
                    normalise(xall[:, t, :], t).then_inc(s["xn_ready"], 1)

            attention("A")
            attention("B")

            normalise_all(C)
            dve.wait_ge(C["logits_mm"], 1)
            link(v.tensor_copy(lg[:, :, :].rearrange("p t e -> p (t e)"), Mp[:, 0:NT * E]))
            it = iota8.unsqueeze(1).to_broadcast([P, NT, E])

            def over(a):
                return a[:, :].unsqueeze(2).to_broadcast([P, NT, E])

            def top(src, m, oh, tmp, i1):
                link(v.tensor_reduce(m[:, :], src[:, :, :], X, ALU.max))
                link(v.tensor_tensor(tmp[:, :, :], src[:, :, :], over(m), ALU.is_equal))
                link(v.tensor_scalar(tmp[:, :, :], tmp[:, :, :], -64.0, None, ALU.mult))
                link(v.tensor_tensor(tmp[:, :, :], tmp[:, :, :], it, ALU.add))
                link(v.tensor_reduce(i1[:, :], tmp[:, :, :], X, ALU.min))
                link(v.tensor_tensor(oh[:, :, :], tmp[:, :, :], over(i1), ALU.is_equal))

            def masked(thr, base, kept, z):
                link(v.scalar_tensor_tensor(kept[:, :, :], lg[:, :, :], -1.0, lg[:, :, :], ALU.mult, ALU.max))
                link(v.tensor_tensor(kept[:, :, :], kept[:, :, :], over(thr), ALU.max))
                link(v.tensor_scalar(kept[:, :, :], kept[:, :, :], 1e-30, None, ALU.max))
                link(v.reciprocal(kept[:, :, :], kept[:, :, :]))
                link(v.tensor_tensor(z[:, :, :], lg[:, :, :], over(thr), ALU.subtract))
                link(v.tensor_tensor(kept[:, :, :], kept[:, :, :], z[:, :, :], ALU.mult))
                link(v.tensor_scalar(kept[:, :, :], kept[:, :, :], -2.0 * JITTER, None, ALU.is_ge))
                return v.tensor_tensor(z[:, :, :], base[:, :, :], over(thr), ALU.subtract)

            top(lg, r1[0], r8[0], r8[3], r1[2])
            link(v.scalar_tensor_tensor(r8[2][:, :, :], r8[0][:, :, :], -3.0e38, lg[:, :, :], ALU.mult, ALU.add))
            top(r8[2], r1[1], r8[1], r8[3], r1[2])
            for k, base in ((0, lg), (1, r8[2])):
                masked(r1[k], base, r8[3 + k], r8[5 + k]).then_inc(C["z_ready"], 1)
                dve.wait_ge(C["z_ready"], k + 1)
            dve.wait_ge(C["zexp_ready"], 2)
            for k in range(2):
                link(v.tensor_tensor(r8[5 + k][:, :, :], r8[5 + k][:, :, :], r8[3 + k][:, :, :], ALU.mult))
                link(v.tensor_reduce(r1[3][:, :], r8[5 + k][:, :, :], X, ALU.add))
                link(v.reciprocal(r1[4][:, :], r1[3][:, :]))
                link(v.tensor_tensor(r8[k][:, :, :], r8[k][:, :, :], over(r1[4]), ALU.mult))
            link(v.tensor_tensor(wt[:, :, :], r8[0][:, :, :], r8[1][:, :, :], ALU.add))

            def weigh(e):
                if e >= 2:
                    dve.wait_ge(C["xwT_mm"], 2 * (e - 1))
                v.tensor_tensor(xw[:, e % 2, :, :], xall[:, :, :], wt[:, :, e:e + 1].to_broadcast([P, NT, D]), ALU.mult)\
                    .then_inc(C["xw_ready"], 1)

            weigh(0)
            for u in range(E * 2 * FC):
                if u % 8 == 0 and u // 8 + 1 < E:
                    weigh(u // 8 + 1)
                dve.wait_ge(C["silu_ready"], u + 1)
                if u >= 2:
                    dve.wait_ge(C["down_mm"], u - 1)
                v.tensor_tensor(hh[:, u % 2, :], sg[:, u % 2, :], Sp[:, u % 2, 512:1024], ALU.mult)\
                    .then_inc(C["h_ready"], 1)
            for half in range(2):
                dve.wait_ge(C["y_mm"], half + 1)
                xs = x[:, 4 * half:4 * half + 4, :].rearrange("p t n -> p (t n)")
                v.tensor_tensor(xs, xs, Tp[:, 512 * half:512 * half + 512], ALU.add).then_inc(C["x_updated"], 1)
            dve.wait_ge(C["x_updated"], 2)

            attention("D")

            normalise_all(G, l2=True)
            dve.wait_ge(G["sim_mm"], 1)
            sc = Op[:, :].rearrange("p (t k) -> p t k", t=NT)
            link(v.tensor_reduce(r1[0][:, :], sc, X, ALU.max))
            b1 = r1[0][:, :].unsqueeze(2).to_broadcast([P, NT, 64])
            link(v.tensor_tensor(sim[:, :, :], sc, b1, ALU.is_equal))
            link(v.tensor_scalar(sim[:, :, :], sim[:, :, :], -1024.0, None, ALU.mult))
            link(v.tensor_tensor(sim2[:, :, :], sim[:, :, :], iota64.unsqueeze(1).to_broadcast([P, NT, 64]), ALU.add))
            link(v.tensor_reduce(r1[1][:, :], sim2[:, :, :], X, ALU.min))
            for half in range(2):
                c = slice(64 * half, 64 * half + 64)
                v.tensor_tensor(pick[c, :, c], sim2[c, :, :], r1[1][c, :].unsqueeze(2).to_broadcast([64, NT, 64]),
                                ALU.is_equal).then_inc(G["pick_ready"], 1)
            for half in range(2):
                dve.wait_ge(G["got_mm"], half + 1)
                xs = x[:, 4 * half:4 * half + 4, :].rearrange("p t n -> p (t n)")
                v.tensor_tensor(xs, xs, Sp[:, 0, 512 * half:512 * half + 512], ALU.add).then_inc(G["x_updated"], 1)
            dve.wait_ge(G["x_updated"], 2)

            v.tensor_scalar(b1x[:, :], f_b1, FIX, None, ALU.mult).then_inc(Z["b1_ready"], 1)
            normalise_all(Z)

            def nodes(u):
                b = u % 2
                dve.wait_ge(Z["h_in"], u + 1)
                link(v.tensor_scalar(hi_[b], ha[b], MAGIC, MAGIC, ALU.add, ALU.subtract))
                link(v.tensor_scalar(hn[b], hi_[b], 1.0 / 64, -63.0 / 128, ALU.mult, ALU.add))
                v.tensor_scalar(hn[b], hn[b], MAGIC, MAGIC, ALU.add, ALU.subtract)\
                    .then_inc(Z["node_ready"], 1)
                dve.wait_ge(Z["node_ready"], u + 1)
                v.scalar_tensor_tensor(hi_[b], hi_[b], 1.0 / 64, hn[b], ALU.mult, ALU.subtract)

            def blend(u):
                b = u % 2
                half, c = divmod(u, FC)
                dve.wait_ge(Z["gelu_ready"], u + 1)
                link(v.tensor_tensor(g1[b], g1[b], g0[b], ALU.subtract))
                link(v.tensor_tensor(g1[b], g1[b], hi_[b], ALU.mult))
                link(v.tensor_tensor(hd, g1[b], g0[b], ALU.add))
                link(v.tensor_scalar(hd, hd, FIX, MAGIC, ALU.mult, ALU.add))
                v.tensor_scalar(hq[:, c, 512 * half:512 * half + 512], hd, MAGIC, 1.0 / FIX, ALU.subtract, ALU.mult)\
                    .then_inc(Z["hq_ready"], 1)

            nodes(0)
            for u in range(2 * FC):
                if u + 1 < 2 * FC:
                    nodes(u + 1)
                blend(u)
            for half in range(2):
                dve.wait_ge(Z["out_mm"], half + 1)
                if half:
                    dve.wait_ge(Z["fin"], half)
                acc = (Op if half == 0 else Mp)[:, :].rearrange("p (t n) -> p t n", t=4)
                o = fo.rearrange("p (t n) -> p t n", t=4)
                link(v.tensor_tensor(o, acc, f_b2.unsqueeze(1).to_broadcast([P, 4, D]), ALU.add))
                link(v.tensor_scalar(fo, fo, FIX, MAGIC, ALU.mult, ALU.add))
                link(v.tensor_scalar(fo, fo, MAGIC, 1.0 / FIX, ALU.subtract, ALU.mult))
                xs = x[:, 4 * half:4 * half + 4, :].rearrange("p t n -> p (t n)")
                v.tensor_tensor(xs, xs, fo, ALU.add).then_inc(Z["fin"], 1)


def layout(a):
    f = np.float32
    order = np.array([4 * g + r for r in range(NR) for g in range(NG)])

    def heads(m, axis):
        shape = m.shape[:axis] + (H, HD) + m.shape[axis + 1:]
        return np.take(m.reshape(shape), order, axis).reshape(m.shape)

    def spread(m):
        m = m.reshape(-1, NR, NG, HD)
        o = np.zeros((m.shape[0], NR, 2, NG, 32), f)
        for half in range(2):
            o[:, :, half, :, AUG * half:AUG * half + HD] = m
        return o

    def wide(v, n=P):
        return np.broadcast_to(np.asarray(v, f).reshape(1, -1), (n, np.asarray(v).size))

    eye = np.eye(P, dtype=f)
    half_of, at = np.divmod(np.arange(P), 64)
    pair_i = (at[:, None] == np.arange(64)).astype(f)
    dup = np.stack([(np.arange(P)[:, None] == 64 * h + at[None, :]).astype(f) for h in range(2)], 1)
    gmask = (np.arange(P)[:, None] // 32 == np.arange(NG)).astype(f)
    hmask = (half_of[:, None] == np.arange(2)).astype(f)
    keep = np.arange(64)[None, :] <= at[:, None]
    inv = f(1.0) / np.power(f(10000.0), np.arange(0, HD, 2, dtype=f) / f(HD)).astype(f)
    ang = (at.astype(f)[:, None] * inv[None, :]).astype(f)
    c, s = np.cos(ang).astype(f), np.sin(ang).astype(f)
    rope_c = np.broadcast_to(np.concatenate([c, c], 1)[:, None], (P, 20, HD))
    rope_s = np.broadcast_to(np.concatenate([s, -s], 1)[:, None], (P, 20, HD))
    consts = [eye, pair_i, dup, gmask, hmask, keep.astype(f), np.where(keep, f(0), f(MASKED)), rope_c, rope_s,
              wide(np.arange(E)), wide(np.arange(64))]

    p = {"B": {}, "D": {}}
    for L, n in (("B", "L0_xattn_"), ("D", "")):
        if L == "B":
            q, k, v, o = (np.asarray(a[n + "W" + i]) for i in "qkvo")
            bq, bk, bv, bo = (np.asarray(a[n + "b" + i]) for i in "qkvo")
        else:
            qk, bqk = np.asarray(a["L1_attn_Wqk_w"]), np.asarray(a["L1_attn_Wqk_b"])
            q, k, bq, bk = qk[:D].T, qk[D:].T, bqk[:D], bqk[D:]
            v, bv = np.asarray(a["L1_attn_Wv_w"]).T, np.asarray(a["L1_attn_Wv_b"])
            o, bo = np.asarray(a["L1_attn_Wo_w"]).T, np.asarray(a["L1_attn_Wo_b"])
        b = spread(heads(bq[None], 1))
        for half in range(2):
            b[:, :, half, :, AUG * half + HD] = 1.0
        p[L] = dict(q=spread(heads(q, 1)), k=spread(heads(k, 1)), v=heads(v, 1), o=heads(o, 0),
                    bq=b.reshape(8, P).T, bv=wide(heads(bv[None], 1)), bo=wide(bo))
        r = np.zeros((3, NR, NG, 32), f)
        for half in range(2):
            r[half, :, :, AUG * half + HD] = f(-1e9 / np.float64(SCALE)) if L == "B" else 0.0
            r[2, :, :, AUG * half:AUG * half + HD] = heads(bk[None], 1).reshape(NR, NG, HD)
        p[L]["rows"] = r.reshape(3, NR * P)
    w_qkv = np.concatenate([heads(np.asarray(a["L0_attn_Wq"]).T, 1), np.asarray(a["L0_attn_Wk"]).T,
                            np.asarray(a["L0_attn_Wv"]).T], 1)
    gain = np.concatenate([np.asarray(a["L0_attn_q_gain"])[order], np.ones(4, f)])
    params = [w_qkv, heads(np.asarray(a["L0_attn_Wp"]).T, 0), wide(gain)]
    for L in "BD":
        params += [p[L][i] for i in ("q", "k", "v", "o", "bq", "bv", "bo")]
    params += [np.asarray(a["L1_attn_Wn_w"])[order].T, a["L0_ffn_gate_w"], a["L1_ffn_w1"],
               np.asarray(a["L1_ffn_b1"]).reshape(FC, P).T,
               np.asarray(a["L1_ffn_w2"]).reshape(FC, P, D).transpose(1, 0, 2), wide(a["L1_ffn_b2"])]
    rows = np.zeros((3, 1680), f)
    rows[:, 0:512] = p["B"]["rows"]
    rows[0, 512:1024] = p["D"]["rows"][2]
    rows[0:2, 1024:1536] = np.asarray(a["mask_Bx1x1xS2_fk0"]).reshape(NT, 2, 64).transpose(1, 0, 2).reshape(2, 512)
    rows[2, 1024:1536] = 1.0
    rows[0, 1536:1552] = np.asarray(a["L1_attn_Wn_b"])[order]
    rows[0, 1552:1680] = 1.0

    def side_by_side(parts):
        return np.ascontiguousarray(np.concatenate([np.asarray(i).reshape(P, -1) for i in parts], 1).astype(f, copy=False))

    return {
        "consts": side_by_side(consts), "params": side_by_side(params), "rows": rows,
        "x": np.ascontiguousarray(a["x"]).reshape(NT * P, D), "ctx": np.ascontiguousarray(a["ctx_1024"]).reshape(NT * P, D),
        "w1": np.ascontiguousarray(a["L0_ffn_w1"]), "w2": np.ascontiguousarray(a["L0_ffn_w2"]),
        "w3": np.ascontiguousarray(a["L0_ffn_w3"]),
    }


def kernel(**inputs):
    from concourse import bacc
    from concourse.bass_utils import run_bass_kernel_spmd

    nc = bacc.Bacc("TRN2", target_bir_lowering=False, num_devices=1)
    arrays, d = {}, {}
    for name, a in layout(inputs).items():
        arrays[f"in_{name}"] = a
        d[name] = nc.dram_tensor(f"in_{name}", a.shape, mybir.dt.from_np(a.dtype), kind="ExternalInput").ap()
    out = nc.dram_tensor("out", (NT * P, D), F32, kind="ExternalOutput").ap()
    build(nc, d, out)
    r = run_bass_kernel_spmd(nc, [arrays], core_ids=[0])
    return np.asarray(r.results[0]["out"]).reshape(BATCH, SEQ, D)
```

```python
from contextlib import ExitStack

import numpy as np

import concourse.bass as bass
from concourse import mybir

F32 = mybir.dt.float32
BF16 = mybir.dt.bfloat16
ALU = mybir.AluOpType
ACT = mybir.ActivationFunctionType
X = mybir.AxisListType.X

P = 128
D = 128
BATCH, SEQ = 16, 64
NT = BATCH * SEQ // P
NQ = NT // 2
H, HD, NG, NR = 16, 8, 4, 4
E, F, FC = 8, 512, 4
SCALE = float(1.0 / np.sqrt(np.float32(HD)))
MASKED = -1.0e30
MAGIC = 1.5 * 2.0 ** 23
LN_EPS = 1e-5
RMS_EPS = float(np.finfo(np.float32).eps)
AUG = HD + 1
OW = H * AUG
FIX = 256.0
JITTER = 0.01
NB = 4

JOBS = [(j[0], int(j[1])) for j in (
    "A0 A1 A2 B0 B1 A3 B2 B3 A4 A5 B4 B5 D0 D1 A6 A7 B6 D2 B7 D3 D4 D5 D6 D7").split()]
URGENCY = {}


def stages():
    st = {}

    def add(name, i, engine, cost, after, bank=None, emptied_by=()):
        st[name, i] = (engine, cost, [a for a in after if a and a[1] >= 0], bank, emptied_by)

    where = {j: n for n, j in enumerate(JOBS)}
    a_jobs = [n for n, (L, _) in enumerate(JOBS) if L == "A"]
    for n, (L, t) in enumerate(JOBS):
        def before(name):
            return name, n - 2
        A, masked = L == "A", L != "D"
        x_from = {"A": None, "B": ("update", where["A", t]), "D": ("addback", t // 2)}[L]
        add("stats", n, "vector", 0.6, [x_from])
        add("rstd", n, "pool", 0.5, [("stats", n)])
        add("front", n, "vector", 2.0 if A else 0.3, [("rstd", n), before("xT")])
        add("xT", n, "tensor", 0.1, [("front", n), before("proj")], "Mp", [("xTin", n)])
        add("xTin", n, "scalar", 0.2, [("xT", n), before("proj")])
        add("proj", n, "tensor", 0.1 if A else 0.7, [("xTin", n), L == "B" and ("textin", t // 2)], "Mp",
            [("qkvout" if A else "add", n)])
        if A:
            add("qkvout", n, "scalar", 0.4, [("proj", n), n >= 2 and ("rotB", a_jobs[max(a_jobs.index(n) - 2, 0)])])
            if a_jobs.index(n) < 2:
                add("qkvout", n, "scalar", 0.4, [("proj", n)])
            add("rotA", n, "vector", 1.1, [("qkvout", n)])
            add("rms", n, "pool", 3.6, [("rotA", n)])
            add("rotB", n, "vector", 2.4, [("rms", n), before("turn")])
        else:
            add("add", n, "vector", 0.5, [("proj", n), before("turn"), n >= 2 and JOBS[n - 2][0] != "A" and before("pad")])
            add("pad", n, "scalar", 1.0, [("add", n), before("turn"), ("params", 0)])
        add("turn", n, "tensor", 0.9 if A else 1.9, [("rotB" if A else "pad", n), before("scores")], "Sp", [("takeq", n), ("take", n)])
        add("takeq", n, "scalar", 0.5, [("turn", n), before("scores")])
        add("take", n, "vector", 0.8 if A else 1.0, [("turn", n), before("scores"), before("values")])
        add("scores", n, "tensor", 2.1 if A else 1.8, [("takeq", n), ("take", n)], "Sp", [("shift", n)])
        add("shift", n, "vector", 2.4 if masked else 1.1, [("scores", n), before("tp1")])
        if masked:
            add("exps", n, "scalar", 0.9, [("shift", n)])
        add("tp0", n, "tensor", 0.4, [("exps" if masked else "shift", n), ("tp1", n - 1)], "Tp", [("tpin0", n)])
        add("tp1", n, "tensor", 0.4, [("tp0", n)], "Tp", [("tpin1", n)])
        add("tpin0", n, "scalar", 0.5, [("tp0", n), before("values"), ("tpin1", n - 1)])
        add("tpin1", n, "scalar", 0.5, [("tp1", n), ("tpin0", n)])
        add("values", n, "tensor", 1.7, [("tpin1", n), ("take", n), before("yT")], "Op", [("norm", n)])
        add("norm", n, "vector", {"A": 2.7, "B": 0.9, "D": 0.5}[L], [("values", n), before("yT")])
        add("yT", n, "tensor", 0.1, [("norm", n), before("out")], "Op", [("yTin", n)])
        add("yTin", n, "scalar", 0.2, [("yT", n), before("out")])
        add("out", n, "tensor", 0.2, [("yTin", n)], "Op", [("update", n)])
        add("update", n, "vector", 0.5, [("out", n)])
    add("params", 0, "vector", 0.3, [("stats", where["A", 1])])
    add("tsum", 0, "vector", 2.5, [])
    add("tnorm", 0, "pool", 1.6, [("tsum", 0)])
    add("tnorm2", 0, "vector", 0.6, [("tnorm", 0)])
    for i in range(NQ):
        add("text", i, "tensor", 0.2, [], "Mp", [("textin", i)])
        add("textin", i, "scalar", 0.3, [("text", i)])
        add("tn", i, "vector", 0.4, [("tnorm2", 0), ("tnT", i - 1)])
        add("tnT", i, "tensor", 0.2, [("tn", i)], "Mp", [("tnin", i)])
        add("tnin", i, "scalar", 0.3, [("tnT", i)])
    for q in range(NQ):
        reused = ("weigh", E * (q - 1) - 1)
        add("pstats", q, "vector", 0.9, [("update", where["B", 2 * q + i]) for i in range(2)])
        add("prstd", q, "pool", 0.6, [("pstats", q)])
        add("pnorm", q, "vector", 0.5, [("prstd", q), reused, ("pT", q - 2)])
        add("pT", q, "tensor", 0.2, [("pnorm", q)], "Tp", [("pTin", q)])
        add("pTin", q, "scalar", 0.3, [("pT", q), q >= 2 and ("gu", E * FC * (q - 1) - 1)])
        add("logits", q, "tensor", 0.1, [("pTin", q)], "Mp", [("lgcopy", q)])
        add("lgcopy", q, "vector", 0.1, [("logits", q), ("routeB", q - 1)])
        add("routeA", q, "vector", 5.0, [("lgcopy", q)])
        add("zexp", q, "scalar", 0.2, [("routeA", q)])
        add("routeB", q, "vector", 2.0, [("zexp", q), reused])
        add("oT", q, "scalar", 0.3, [("down", E * FC * (q + 1) - 1), ("back", q - 1)])
        add("back", q, "tensor", 0.2, [("oT", q)], "Tp", [("addback", q)])
        add("addback", q, "vector", 0.3, [("back", q)])
    for k in range(NQ * E):
        add("weigh", k, "vector", 0.3, [("routeB", k // E), ("xwT", k - 2)])
        add("xwT", k, "tensor", 0.2, [("weigh", k)], "Tp", [("xwTin", k)])
        add("xwTin", k, "scalar", 0.3, [("xwT", k), k >= 2 and ("gu", FC * (k - 1) - 1)])
    for u in range(NQ * E * FC):
        q = u // (E * FC)
        add("gu", u, "tensor", 0.87, [("xwTin", u // FC), ("pTin", q)], f"FU{u % 2}", [("gate", u)])
        add("uo", u, "scalar", 0.5, [("gu", u), ("h", u - NB)])
        add("gate", u, "vector", 0.3, [("uo", u), ("down", u - NB)])
        add("h", u, "pool", 0.7, [("gate", u)])
        add("down", u, "tensor", 0.4, [("h", u), u % (E * FC) == 0 and ("oT", q - 1)])
    for p in range(NQ):
        add("gstats", p, "vector", 1.0, [("update", where["D", 2 * p + i]) for i in range(2)])
        add("gpow", p, "pool", 1.2, [("gstats", p)])
        add("gnorm", p, "vector", 1.3, [("gpow", p), ("zT", p - 1), ("tnT", NQ - 1)])
        add("gT", p, "tensor", 0.2, [("gnorm", p), ("zh1", p - 1)], "Tp", [("gTin", p)])
        add("gTin", p, "scalar", 0.3, [("gT", p), ("zh1", p - 1)])
        add("sim", p, "tensor", 0.4, [("gTin", p), ("tnin", NQ - 1)], "Mp", [("best", p)])
        add("best", p, "vector", 1.3, [("sim", p), ("pickT", p - 1)])
        add("pickT", p, "tensor", 0.2, [("best", p)], "Tp", [("pickin", p)])
        add("pickin", p, "scalar", 0.3, [("pickT", p), ("got", p - 1)])
        add("got", p, "tensor", 0.4, [("pickin", p)], "Op", [("gadd", p)])
        add("gadd", p, "vector", 1.3, [("got", p)])
        add("zpow", p, "pool", 0.6, [("gadd", p)])
        add("znorm", p, "vector", 0.5, [("zpow", p), ("gT", p)])
        add("zT", p, "tensor", 0.2, [("znorm", p)], "Tp", [("zTin", p)])
        add("zTin", p, "scalar", 0.3, [("zT", p), ("sim", p)])
        for k in range(2):
            add(f"zh{k}", p, "tensor", 0.9, [("zTin", p), k == 1 and ("zh0", p)], ("Tp", "Mp")[k], [(f"ha{k}", p)])
            add(f"ha{k}", p, "scalar", 0.5, [(f"zh{k}", p), (f"nodes{k}", p - 1), k == 1 and ("ha0", p)])
            add(f"nodes{k}", p, "vector", 2.0, [(f"ha{k}", p), (f"blend{k}", p - 1), k == 1 and ("nodes0", p)])
            add(f"blend{k}", p, "vector", 2.3, [("gelu", p), ("zout", p - 1), k == 1 and ("blend0", p)])
        add("gelu", p, "scalar", 4.6, [("nodes0", p), ("nodes1", p), ("blend1", p - 1)])
        add("zout", p, "tensor", 1.7, [("blend0", p), ("blend1", p)], "Mp", [("finish", p)])
        add("finish", p, "vector", 1.4, [("zout", p)])
    last = {}
    for name, i in sorted(st):
        if name in last:
            st[name, i][2].append((name, last[name]))
        last[name] = i
    return st


def plan():
    st = stages()
    followers, path = {}, {}
    for s, (_, _, after, _, _) in st.items():
        for a in after:
            followers.setdefault(a, []).append(s)
    missing = {s: len(followers.get(s, ())) for s in st}
    stack = [s for s in st if not missing[s]]
    while stack:
        s = stack.pop()
        path[s] = st[s][1] + 0.07 + max((path[f] for f in followers.get(s, ())), default=0.0)
        for a in st[s][2]:
            missing[a] -= 1
            if not missing[a]:
                stack.append(a)
    urgency = {s: path[s] + URGENCY.get(s[0], 0) for s in st}
    engines = ("vector", "scalar", "tensor", "pool")
    order = {e: [] for e in engines}
    ready = {e: [] for e in engines}
    missing = {s: len(st[s][2]) for s in st}
    for s in st:
        if not missing[s]:
            ready[st[s][0]].append(s)
    free_at = {"vector": 13.0, "scalar": 6.0, "tensor": 9.0, "pool": 9.0}
    full, empties = {}, {}
    for s, (_, _, _, bank, emptied_by) in st.items():
        for r in emptied_by:
            empties.setdefault(r, []).append(s)
    events = [(t, 1, ()) for t in free_at.values()]
    while events:
        now = min(e[0] for e in events)
        for event in sorted(e for e in events if e[0] == now):
            events.remove(event)
            s = event[2]
            if not s:
                continue
            for filler in empties.get(s, ()):
                full[st[filler][3]] -= 1
            for f in followers.get(s, ()):
                missing[f] -= 1
                if not missing[f]:
                    ready[st[f][0]].append(f)
        for e in engines:
            can = [s for s in ready[e] if not full.get(st[s][3])] if free_at[e] <= now else []
            if can:
                s = max(can, key=lambda c: (urgency[c], c))
                ready[e].remove(s)
                order[e].append(s)
                if st[s][3]:
                    full[st[s][3]] = len(st[s][4])
                free_at[e] = now + st[s][1]
                events += [(free_at[e], 1, ()), (free_at[e] + 0.07, 0, s)]
    assert sum(len(o) for o in order.values()) == len(st)
    return order


def build(nc, d, out):
    ctx = ExitStack()
    with ctx:
        def sb(name, shape, dt=F32):
            return ctx.enter_context(nc.sbuf_tensor(name, shape, dt))

        def sem(name):
            return ctx.enter_context(nc.semaphore(name))

        def carve(tensor):
            at = [0]

            def take(*shape):
                n = int(np.prod(shape))
                ap = tensor[:, at[0]:at[0] + n]
                at[0] += n
                return ap.rearrange("p (a b) -> p a b", b=shape[1]) if len(shape) == 2 else ap
            return take

        x = sb("x", [P, NT, D])
        text = sb("text", [P, NT, D])
        textT = sb("textT", [P, NT, P])
        tnormT = sb("tnormT", [P, NT, P])
        consts = sb("consts", [P, d["consts"].shape[1]])
        const = carve(consts)
        ident, pairI, dup = const(P), const(64), const(2, P)
        gmask, causal01, causal_add = const(2), const(64), const(64)
        rope_c, rope_s = const(20, HD), const(20, HD)
        iota8, iota64 = const(E), const(64)
        params_a = sb("params_a", [P, d["params_a"].shape[1]])
        param = carve(params_a)
        w_qkv, w_p, gain = param(192), param(D), param(20)
        params = sb("params", [P, d["params"].shape[1]])
        param = carve(params)
        w_in, w_out, b_in, b_out = {}, {}, {}, {}
        for L, n in (("B", 384), ("D", 400)):
            w_in[L], w_out[L], b_in[L], b_out[L] = param(n), param(D), param(n), param(D)
        mask = param(NT)
        gate_w = param(E)
        f_w1, f_b1, f_w2, f_b2 = param(F), param(FC), param(FC, D), param(D)

        w1s, w3s = sb("w1s", [P, E, F]), sb("w3s", [P, E, F])
        w2s = sb("w2s", [P, E, FC, D])

        identb = sb("identb", [P, P], BF16)
        causal_b = sb("causal_b", [P, 64], BF16)
        ones = sb("ones", [P, P])
        tern = sb("tern", [P, 320], BF16)
        tq = sb("tq", [P, 320])
        wabs = sb("wabs", [P, 4])
        alphas = sb("alphas", [P, 4])
        inv_alphas = sb("inv_alphas", [P, 4])
        alpha20 = sb("alpha20", [P, 20])
        cgain, sgain = sb("cgain", [P, 20, HD]), sb("sgain", [P, 20, HD])
        mask_neg = sb("mask_neg", [P, NT])

        stats = sb("stats", [P, NT, 6])
        mv = sb("mv", [P, NT, 2])
        powed = sb("powed", [P, 2, NT])
        rstd = sb("rstd", [P, NT])
        norms, xnorm = sb("norms", [P, NT]), sb("xnorm", [P, NT])
        text_sum = sb("text_sum", [P, NT])
        minus_half, half_ = sb("minus_half", [P, 20]), sb("half", [P, 20])
        small = sb("small", [P, 4])
        xn = sb("xn", [P, 2, D])
        xint = sb("xint", [P, 2, D], BF16)
        gam = sb("gam", [P, 4, 1])
        xnT = sb("xnT", [P, 2, P])
        xintT = sb("xintT", [P, 2, P], BF16)
        qkv = sb("qkv", [P, 2, 192])
        proj = sb("proj", [P, 2, 400])
        sq = sb("sq", [P, 2, 20, HD])
        rr, rk = sb("rr", [P, 2, 20]), sb("rk", [P, 20])
        rms = sb("rms", [P, 2, 2, 20])
        fac = sb("fac", [P, 2, 20])
        qn, m1, m2 = (sb(n, [P, 20, HD]) for n in ("qn", "m1", "m2"))
        gav = sb("gav", [P, 1])
        qpad = sb("qpad", [P, 2, NR, NG, 32])
        kpad = sb("kpad", [P, 2, NR, NG, 32])
        kpad_m = sb("kpad_m", [P, 2, NR, NG, 32])
        vtok = sb("vtok", [P, 2, NG * HD])
        qT = sb("qT", [P, 2, NR, P])
        kbd = sb("kbd", [P, 2, NR, 2, 64])
        vbd = sb("vbd", [P, 2, 8, 2, 2 * AUG])
        probs = sb("probs", [P, 2, H, 64])
        mx = sb("mx", [P, H])
        pT = sb("pT", [P, 2, 8, P])
        rden = sb("rden", [P, H])
        nexp = sb("nexp", [P, 2, H])
        y = sb("y", [P, 2, H, HD])
        yint = sb("yint", [P, 2, D], BF16)
        ygam = sb("ygam", [P, 2, 1])
        yT = sb("yT", [P, 2, P])
        yintT = sb("yintT", [P, 2, P], BF16)
        qt = sb("qt", [P, D])
        out_b = sb("out_b", [P, D])

        xall = sb("xall", [P, 2, 2, D])
        xallT = sb("xallT", [P, 2, 2, P])
        xw = sb("xw", [P, 2, 2, D])
        xwT = sb("xwT", [P, 2, 2, P])
        th = sb("th", [P, NB, 256])
        hh = sb("hh", [P, NB, 256])
        uu = sb("uu", [P, NB, 256])
        oT = sb("oT", [P, 2, P])
        lg = sb("lg", [P, 2, E])
        r8 = [sb(f"r8_{i}", [P, 2, E]) for i in range(7)]
        r1 = [sb(f"r1_{i}", [P, 2]) for i in range(5)]
        wt = sb("wt", [P, 2, 2, E])

        xz = sb("xz", [P, 2, D])
        xzT = sb("xzT", [P, 2, P])
        sim, sim2 = sb("sim", [P, 2, 64]), sb("sim2", [P, 2, 64])
        best = [sb(f"best{i}", [P, 2]) for i in range(2)]
        pick = sb("pick", [P, 2, P])
        pickT = sb("pickT", [P, 2, P])
        ha, hi_, hn, g0, g1 = (sb(n, [P, 2, 512]) for n in ("ha", "hi", "hn", "g0", "g1"))
        hd, fo = sb("hd", [P, 512]), sb("fo", [P, 2 * D])
        hq = sb("hq", [P, FC, 256])
        b1x = sb("b1x", [P, FC])
        quarter = sb("quarter", [P, 1])

        Sp = ctx.enter_context(nc.psum_tensor("Sp", [P, 1024], F32))
        FU = ctx.enter_context(nc.psum_tensor("FU", [P, 2, 512], F32))
        Tp = ctx.enter_context(nc.psum_tensor("Tp", [P, 512], F32))
        Op = ctx.enter_context(nc.psum_tensor("Op", [P, 512], F32))
        Mp = ctx.enter_context(nc.psum_tensor("Mp", [P, 512], F32))
        AC = ctx.enter_context(nc.psum_tensor("AC", [P, 512], F32))

        dma_x, dma_text, dma_const, dma_param_a, dma_param = (sem(n) for n in (
            "x_loaded", "text_loaded", "consts_loaded", "params_a_loaded", "params_loaded"))
        dma_w = [sem(f"expert{e}_loaded") for e in range(E)]
        stored = sem("stored")
        presets, step = sem("presets_done"), sem("dve_step")
        wabs_ready, alpha_mm, tern_ready = sem("wabs_ready"), sem("alpha_mm"), sem("tern_ready")
        tsum_ready, tnorm_ready, tn_ready = sem("tsum_ready"), sem("tnorm_ready"), sem("tn_ready")
        mask_ready = sem("mask_ready")
        text_mm, text_in, tn_mm, tn_in = sem("text_mm"), sem("text_in"), sem("tn_mm"), sem("tn_in")
        S = {n: sem("S_" + n) for n in (
            "var_ready rstd_ready xn_ready xT_mm xT_in proj_mm turn_mm act_took dve_took scores_mm shifted "
            "pT_mm pT_in pv_mm y_ready yT_mm yT_in out_mm x_updated "
            "qkv_in rms_ready rms_in rotated added padded probs_ready n_in").split()}
        C = {n: sem("C_" + n) for n in "var_ready rstd_ready xn_ready xT_mm xT_in logits_mm z_ready zexp_ready xw_ready xwT_mm xwT_in "
             "lg_in gu_mm u_in gated h_ready down_mm oT_in back_mm x_updated".split()}
        G = {n: sem("G_" + n) for n in "var_ready powers_ready xn_ready xT_mm xT_in sim_mm pick_ready pickT_mm pickT_in got_mm x_updated".split()}
        Z = {n: sem("Z_" + n) for n in "b1_ready var_ready rstd_ready xn_ready xT_mm xT_in h_mm h_in node_ready node_rest gelu_ready hq_ready out_mm fin".split()}

        kind = [L for L, _ in JOBS]
        tile = [t for _, t in JOBS]
        order = plan()

        def nth(n, kinds):
            return sum(k in kinds for k in kind[:n])

        def job(L, t):
            return JOBS.index((L, t))

        block = ctx.enter_context(nc.Block())

        @block.sync
        def _(sp):
            sp.dma_start(params_a[:, :], d["params_a"]).then_inc(dma_param_a, 16)
            sp.dma_start(text[:, :, :], d["ctx"].rearrange("(t p) n -> p t n", p=P)).then_inc(dma_text, 16)
            sp.dma_start(params[:, :], d["params"]).then_inc(dma_param, 16)
            for e in range(E):
                sp.dma_start(w1s[:, e, :], d["w1"][e]).then_inc(dma_w[e], 16)
                sp.dma_start(w3s[:, e, :], d["w3"][e]).then_inc(dma_w[e], 16)
                sp.dma_start(w2s[:, e, :, :], d["w2"][e].rearrange("(c p) n -> p c n", p=P)).then_inc(dma_w[e], 16)
            for p in range(NQ):
                sp.wait_ge(Z["fin"], p + 1)
                sp.dma_start(out.rearrange("(t p) n -> p t n", p=P)[:, 2 * p:2 * p + 2, :],
                             x[:, 2 * p:2 * p + 2, :]).then_inc(stored, 16)
            sp.wait_ge(stored, 16 * NQ)

        PRESETS = 13

        @block.gpsimd
        def _(pool):
            for m in (qpad, kpad, kpad_m, vbd, pick):
                nc.gpsimd.memset(m[:], 0.0).then_inc(presets, 1)
            nc.gpsimd.memset(ones[:], 1.0).then_inc(presets, 1)
            nc.gpsimd.memset(quarter[:], 0.25).then_inc(presets, 1)
            nc.gpsimd.memset(minus_half[:], -0.5).then_inc(presets, 1)
            nc.gpsimd.memset(half_[:], 0.5).then_inc(presets, 1)
            pool.wait_ge(presets, 9)
            for half in range(2):
                c, a = slice(64 * half, 64 * half + 64), AUG * half + HD
                nc.gpsimd.memset(vbd[c, :, :, :, a:a + 1], 1.0).then_inc(presets, 1)
                for b in range(2):
                    ins = nc.gpsimd.memset(qpad[c, b, :, :, a:a + 1], 1.0)
                ins.then_inc(presets, 1)

            def power(o, base, exponent):
                return nc.gpsimd.tensor_tensor(o, base, exponent[:, 0:o.shape[1]], ALU.pow)

            def unit_h(u):
                pool.wait_ge(C["gated"], u + 1)
                pool.wait_ge(C["u_in"], u + 1)
                nc.gpsimd.tensor_tensor(hh[:, u % NB, :], hh[:, u % NB, :], uu[:, u % NB, :], ALU.mult)\
                    .then_inc(C["h_ready"], 1)

            def rstd_one(n):
                t = tile[n]
                pool.wait_ge(S["var_ready"], n + 1)
                power(rstd[:, t:t + 1], powed[:, 0, t:t + 1], minus_half).then_inc(S["rstd_ready"], 1)

            def rms_power(n):
                i = nth(n, "A")
                pool.wait_ge(S["rms_ready"], i + 1)
                power(rms[:, i % 2, 1, :], rms[:, i % 2, 0, :], minus_half).then_inc(S["rms_in"], 1)

            def text_norms(_):
                pool.wait_ge(tsum_ready, 1)
                power(norms[:, :], text_sum[:, :], half_).then_inc(tnorm_ready, 1)

            def rstd_experts(q):
                tt = slice(2 * q, 2 * q + 2)
                pool.wait_ge(C["var_ready"], q + 1)
                power(rstd[:, tt], powed[:, 0, tt], minus_half).then_inc(C["rstd_ready"], 1)

            def powers_match(p):
                tt = slice(2 * p, 2 * p + 2)
                pool.wait_ge(G["var_ready"], p + 1)
                power(rstd[:, tt], powed[:, 0, tt], minus_half)
                power(xnorm[:, tt], powed[:, 1, tt], half_).then_inc(G["powers_ready"], 1)

            def rstd_last(p):
                tt = slice(2 * p, 2 * p + 2)
                pool.wait_ge(Z["var_ready"], p + 1)
                power(rstd[:, tt], powed[:, 0, tt], minus_half).then_inc(Z["rstd_ready"], 1)

            pieces = dict(h=unit_h, rstd=rstd_one, rms=rms_power, tnorm=text_norms, prstd=rstd_experts, gpow=powers_match,
                          zpow=rstd_last)
            for stage, i in order["pool"]:
                pieces[stage](i)

        @block.tensor
        def _(pe):
            mm, tr = nc.tensor.matmul, nc.tensor.transpose
            reader = {}

            def fill(bank, *readers):
                for r in reader.get(bank, ()):
                    pe.wait_ge(*r)
                reader[bank] = readers

            pe.wait_ge(dma_const, 16)
            pe.wait_ge(presets, PRESETS)
            pe.wait_ge(wabs_ready, 4)
            fill("Mp", (tern_ready, 2))
            mm(Mp[:, 0:4], ones[:, :], wabs[:, :], start=True, stop=True).then_inc(alpha_mm, 1)

            def gate_up(u):
                q, e, c = u // (E * FC), u // FC % E, u % FC
                if q == 0 and c == 0:
                    pe.wait_ge(dma_w[e], 48)
                if c == 0:
                    pe.wait_ge(C["xT_in"], q + 1)
                    pe.wait_ge(C["xwT_in"], u // FC + 1)
                fill(f"FU{u % 2}", (C["gated"], u + 1))
                mm(FU[:, u % 2, 0:256], w1s[:, e, c * P:c * P + P], xallT[:, q % 2, :, :].rearrange("p t n -> p (t n)"),
                   start=True, stop=True)
                mm(FU[:, u % 2, 256:512], w3s[:, e, c * P:c * P + P], xwT[:, (u // FC) % 2, :, :].rearrange("p t n -> p (t n)"),
                   start=True, stop=True).then_inc(C["gu_mm"], 1)

            def down(u):
                q, e, c = u // (E * FC), u // FC % E, u % FC
                if e == 0 and c == 0:
                    fill("AC", (C["oT_in"], q + 1))
                pe.wait_ge(C["h_ready"], u + 1)
                mm(AC[:, 0:256], w2s[:, e, c, :], hh[:, u % NB, :], start=(e == 0 and c == 0),
                   stop=(e == E - 1 and c == FC - 1)).then_inc(C["down_mm"], 1)

            def turn_x(n):
                fill("Mp", (S["xT_in"], n + 1))
                pe.wait_ge(S["xn_ready"], n + 1)
                if kind[n] == "A":
                    ins = tr(Mp[:, 0:64].bitcast(BF16), xint[:, n % 2, :], identb[:, :])
                else:
                    ins = tr(Mp[:, 0:P], xn[:, n % 2, :], ident)
                ins.then_inc(S["xT_mm"], 1)

            def project(n):
                L, b = kind[n], n % 2
                pe.wait_ge(S["xT_in"], n + 1)
                if L == "A":
                    if n == 0:
                        pe.wait_ge(tern_ready, 3)
                    fill("Mp", (S["qkv_in"], nth(n, "A") + 1))
                    mm(Mp[:, 0:192], xintT[:, b, :], tern[:, 0:192], start=True, stop=True).then_inc(S["proj_mm"], 1)
                    return
                fill("Mp", (S["added"], nth(n, "BD") + 1))
                pe.wait_ge(dma_param, 16)
                if L == "B":
                    pe.wait_ge(text_in, tile[n] // 2 + 1)
                    mm(Mp[:, 0:D], xnT[:, b, :], w_in["B"][:, 0:D], start=True, stop=True)
                    mm(Mp[:, D:384], textT[:, tile[n], :], w_in["B"][:, D:384], start=True, stop=True)\
                        .then_inc(S["proj_mm"], 1)
                else:
                    mm(Mp[:, 0:400], xnT[:, b, :], w_in["D"], start=True, stop=True).then_inc(S["proj_mm"], 1)

            def turn(n):
                L, b = kind[n], n % 2
                fill("Sp", (S["act_took"], n + 1), (S["dve_took"], n + 1))
                if L == "A":
                    pe.wait_ge(S["rotated"], nth(n, "A") + 1)
                else:
                    pe.wait_ge(S["padded"], nth(n, "BD") + 1)
                for r in range(NR):
                    tr(Sp[:, r * P:r * P + P], qpad[:, b, r, :, :].rearrange("p g c -> p (g c)"), ident)
                kp = kpad_m if L == "B" else kpad
                for r in range(1 if L == "A" else NR):
                    mm(Sp[:, 512 + 64 * r:576 + 64 * r], kp[:, b, r, :, :].rearrange("p g c -> p (g c)"), pairI,
                       start=True, stop=True)
                v, w = (vtok[:, b, :], 32) if L == "A" else (proj[:, b, 256:384], 128)
                for half in range(2):
                    ins = mm(Sp[:, 768 + w * half:768 + w * half + w], dup[:, half, :], v, start=True, stop=True)
                ins.then_inc(S["turn_mm"], 1)

            def scores(n):
                L, b = kind[n], n % 2
                fill("Sp", (S["shifted"], n + 1))
                if L == "A":
                    for gh in range(2):
                        mm(Sp[:, 512 * gh:512 * gh + 512], identb[:, :],
                           causal_b[:, :].unsqueeze(1).to_broadcast([P, 8, 64]), start=True, stop=False,
                           skip_group_check=True)
                for r in range(NR):
                    for gh in range(2):
                        c = slice(64 * gh, 64 * gh + 64)
                        at = 512 * gh + 128 * r
                        k = kbd[c, b, 0 if L == "A" else r, :, :].rearrange("p g c -> p (g c)")
                        ins = mm(Sp[:, at:at + 128], qT[c, b, r, :], k, start=L != "A", stop=True,
                                 skip_group_check=L == "A")
                ins.then_inc(S["scores_mm"], 1)

            def turn_probs(n, k):
                fill("Tp", (S["pT_in"], 2 * n + k + 1))
                if kind[n] == "D":
                    pe.wait_ge(S["shifted"], n + 1)
                else:
                    pe.wait_ge(S["probs_ready"], nth(n, "AB") + 1)
                flat = probs[:, n % 2, :, :].rearrange("p h k -> p (h k)")
                for j in range(4):
                    ins = tr(Tp[:, j * P:j * P + P], flat[:, (4 * k + j) * P:(4 * k + j) * P + P], ident)
                ins.then_inc(S["pT_mm"], 1)

            def values(n):
                L, b = kind[n], n % 2
                fill("Op", (S["y_ready"], n + 1))
                pe.wait_ge(S["dve_took"], n + 1)
                pe.wait_ge(S["pT_in"], 2 * n + 2)
                o = Op[:, 0:2 * OW].rearrange("p (a c) -> p a c", a=2)
                for j in range(8):
                    v = vbd[:, b, j // 4 if L == "A" else j, :, :]
                    ins = mm(o[:, :, 2 * AUG * j:2 * AUG * j + 2 * AUG], pT[:, b, j, :], v, start=True, stop=True)
                ins.then_inc(S["pv_mm"], 1)

            def turn_y(n):
                b = n % 2
                fill("Op", (S["yT_in"], n + 1))
                pe.wait_ge(S["y_ready"], n + 1)
                if kind[n] == "A":
                    ins = tr(Op[:, 0:64].bitcast(BF16), yint[:, b, :], identb[:, :])
                else:
                    ins = tr(Op[:, 0:P], y[:, b, :, :].rearrange("p h c -> p (h c)"), ident)
                ins.then_inc(S["yT_mm"], 1)

            def project_out(n):
                b = n % 2
                fill("Op", (S["x_updated"], n + 1))
                pe.wait_ge(S["yT_in"], n + 1)
                if kind[n] == "A":
                    ins = mm(Op[:, 0:D], yintT[:, b, :], tern[:, 192:320], start=True, stop=True)
                else:
                    ins = mm(Op[:, 0:D], yT[:, b, :], w_out[kind[n]], start=True, stop=True)
                ins.then_inc(S["out_mm"], 1)

            def turn_two(bank, name, src, signal, *readers):
                fill(name, *readers)
                for i in range(2):
                    ins = tr(bank[:, i * P:i * P + P], src[:, i, :], ident)
                ins.then_inc(signal, 1)

            def turn_text(i):
                pe.wait_ge(dma_text, 16)
                turn_two(Mp, "Mp", text[:, 2 * i:2 * i + 2, :], text_mm, (text_in, i + 1))

            def turn_tnorm(i):
                pe.wait_ge(tn_ready, i + 1)
                turn_two(Mp, "Mp", xz, tn_mm, (tn_in, i + 1))

            def turn_quarter(q):
                pe.wait_ge(C["xn_ready"], q + 1)
                turn_two(Tp, "Tp", xall[:, q % 2, :, :], C["xT_mm"], (C["xT_in"], q + 1))

            def logits(q):
                fill("Mp", (C["lg_in"], q + 1))
                pe.wait_ge(C["xT_in"], q + 1)
                for i in range(2):
                    ins = mm(Mp[:, E * i:E * i + E], xallT[:, q % 2, i, :], gate_w, start=True, stop=True)
                ins.then_inc(C["logits_mm"], 1)

            def turn_weighed(k):
                pe.wait_ge(C["xw_ready"], k + 1)
                turn_two(Tp, "Tp", xw[:, k % 2, :, :], C["xwT_mm"], (C["xwT_in"], k + 1))

            def turn_back(q):
                pe.wait_ge(C["oT_in"], q + 1)
                turn_two(Tp, "Tp", oT, C["back_mm"], (C["x_updated"], q + 1))

            def turn_match(p):
                pe.wait_ge(G["xn_ready"], p + 1)
                turn_two(Tp, "Tp", xz, G["xT_mm"], (G["xT_in"], p + 1))

            def similarity(p):
                fill("Mp", (G["pick_ready"], p + 1))
                pe.wait_ge(G["xT_in"], p + 1)
                pe.wait_ge(tn_in, NQ)
                for i in range(2):
                    for half in range(2):
                        c = slice(64 * half, 64 * half + 64)
                        ins = mm(Mp[c, 64 * i:64 * i + 64], xzT[:, i, c], tnormT[:, 2 * p + i, c], start=True, stop=True)
                ins.then_inc(G["sim_mm"], 1)

            def turn_pick(p):
                pe.wait_ge(G["pick_ready"], p + 1)
                turn_two(Tp, "Tp", pick, G["pickT_mm"], (G["pickT_in"], p + 1))

            def get_rows(p):
                fill("Op", (G["x_updated"], p + 1))
                pe.wait_ge(G["pickT_in"], p + 1)
                for i in range(2):
                    ins = mm(Op[:, P * i:P * i + P], pickT[:, i, :], text[:, 2 * p + i, :], start=True, stop=True)
                ins.then_inc(G["got_mm"], 1)

            def turn_last(p):
                pe.wait_ge(Z["xn_ready"], p + 1)
                turn_two(Tp, "Tp", xz, Z["xT_mm"], (Z["xT_in"], p + 1))

            def hidden(k):
                def piece(p):
                    bank, name = ((Tp, "Tp"), (Mp, "Mp"))[k]
                    fill(name, (Z["h_in"], 2 * p + k + 1))
                    pe.wait_ge(Z["xT_in"], p + 1)
                    for i in range(2):
                        c = 2 * k + i
                        ins = mm(bank[:, 256 * i:256 * i + 256], f_w1[:, c * P:c * P + P],
                                 xzT[:, :, :].rearrange("p t n -> p (t n)"), start=True, stop=True)
                    ins.then_inc(Z["h_mm"], 1)
                return piece

            def last_out(p):
                fill("Mp", (Z["fin"], p + 1))
                pe.wait_ge(Z["hq_ready"], 2 * p + 2)
                for i in range(2):
                    for c in range(FC):
                        ins = mm(Mp[:, P * i:P * i + P], hq[:, c, P * i:P * i + P], f_w2[:, c, :],
                                 start=(c == 0), stop=(c == FC - 1))
                ins.then_inc(Z["out_mm"], 1)

            pieces = dict(xT=turn_x, proj=project, turn=turn, scores=scores, tp0=lambda n: turn_probs(n, 0),
                          tp1=lambda n: turn_probs(n, 1), values=values, yT=turn_y, out=project_out,
                          text=turn_text, tnT=turn_tnorm, pT=turn_quarter, logits=logits, xwT=turn_weighed,
                          gu=gate_up, down=down, back=turn_back, gT=turn_match, sim=similarity, pickT=turn_pick,
                          got=get_rows, zT=turn_last, zh0=hidden(0), zh1=hidden(1), zout=last_out)
            for stage, i in order["tensor"]:
                pieces[stage](i)

        @block.scalar
        def _(act):
            act.dma_start(x[:, :, :], d["x"].rearrange("(t p) n -> p t n", p=P)).then_inc(dma_x, 16)
            act.dma_start(consts[:, :], d["consts"]).then_inc(dma_const, 16)

            def copy(o, i):
                return nc.scalar.activation(o, i, ACT.Copy)

            def copy_two(o, bank):
                return copy(o.rearrange("p t n -> p (t n)"), bank[:, 0:256])

            def unit_out(u):
                act.wait_ge(C["gu_mm"], u + 1)
                if u >= NB:
                    act.wait_ge(C["h_ready"], u - NB + 1)
                nc.scalar.activation(th[:, u % NB, :], FU[:, u % 2, 0:256], ACT.Tanh, scale=0.5)
                copy(uu[:, u % NB, :], FU[:, u % 2, 256:512]).then_inc(C["u_in"], 1)

            def x_turned(n):
                b = n % 2
                act.wait_ge(S["xT_mm"], n + 1)
                if n >= 2:
                    act.wait_ge(S["proj_mm"], n - 1)
                if kind[n] == "A":
                    copy(xintT[:, b, :], Mp[:, 0:64].bitcast(BF16)).then_inc(S["xT_in"], 1)
                else:
                    copy(xnT[:, b, :], Mp[:, 0:P]).then_inc(S["xT_in"], 1)

            def qkv_out(n):
                i = nth(n, "A")
                act.wait_ge(S["proj_mm"], n + 1)
                if i >= 2:
                    act.wait_ge(S["rotated"], i - 1)
                nc.scalar.activation(sq[:, i % 2, :, :].rearrange("p s c -> p (s c)"), Mp[:, 0:160], ACT.Square)
                copy(qkv[:, i % 2, :], Mp[:, 0:192]).then_inc(S["qkv_in"], 1)

            def pad(n):
                L, b, i = kind[n], n % 2, nth(n, "BD")
                act.wait_ge(S["added"], i + 1)
                if n >= 2:
                    act.wait_ge(S["turn_mm"], n - 1)
                kp = kpad_m if L == "B" else kpad
                for half in range(2):
                    c = slice(64 * half, 64 * half + 64)
                    o = slice(AUG * half, AUG * half + HD)
                    for dst, at in ((qpad, 0), (kp, D)):
                        ins = copy(dst[c, b, :, :, o].rearrange("p r g c -> p (r g) c"),
                                   proj[c, b, at:at + D].rearrange("p (s c) -> p s c", c=HD))
                    if L == "B":
                        t, a = tile[n], AUG * half + HD
                        act.wait_ge(mask_ready, 1)
                        ins = copy(kp[c, b, :, :, a:a + 1].rearrange("p r g c -> p (r g) c"),
                                   mask_neg[c, t:t + 1].unsqueeze(2).to_broadcast([64, H, 1]))
                ins.then_inc(S["padded"], 1)
                if L == "D":
                    j = nth(n, "D")
                    if j >= 2:
                        act.wait_ge(S["y_ready"], job("D", j - 2) + 1)
                    nc.scalar.activation(nexp[:, j % 2, :], proj[:, b, 384:400], ACT.Exp, scale=-1.0)\
                        .then_inc(S["n_in"], 1)

            def take(n):
                b = n % 2
                act.wait_ge(S["turn_mm"], n + 1)
                if n >= 2:
                    act.wait_ge(S["scores_mm"], n - 1)
                copy(qT[:, b, :, :].rearrange("p r n -> p (r n)"), Sp[:, 0:512]).then_inc(S["act_took"], 1)

            def exps(n):
                act.wait_ge(S["shifted"], n + 1)
                e = probs[:, n % 2, :, :].rearrange("p h k -> p (h k)")
                nc.scalar.activation(e, e, ACT.Exp, scale=SCALE).then_inc(S["probs_ready"], 1)

            def probs_turned(n, k):
                b = n % 2
                act.wait_ge(S["pT_mm"], 2 * n + k + 1)
                if n >= 2:
                    act.wait_ge(S["pv_mm"], n - 1)
                copy(pT[:, b, 4 * k:4 * k + 4, :].rearrange("p j n -> p (j n)"), Tp[:, :]).then_inc(S["pT_in"], 1)

            def y_turned(n):
                b = n % 2
                act.wait_ge(S["yT_mm"], n + 1)
                if n >= 2:
                    act.wait_ge(S["out_mm"], n - 1)
                if kind[n] == "A":
                    copy(yintT[:, b, :], Op[:, 0:64].bitcast(BF16)).then_inc(S["yT_in"], 1)
                else:
                    copy(yT[:, b, :], Op[:, 0:P]).then_inc(S["yT_in"], 1)

            def text_turned(i):
                act.wait_ge(text_mm, i + 1)
                copy_two(textT[:, 2 * i:2 * i + 2, :], Mp).then_inc(text_in, 1)

            def tnorm_turned(i):
                act.wait_ge(tn_mm, i + 1)
                copy_two(tnormT[:, 2 * i:2 * i + 2, :], Mp).then_inc(tn_in, 1)

            def quarter_turned(q):
                act.wait_ge(C["xT_mm"], q + 1)
                if q >= 2:
                    act.wait_ge(C["gu_mm"], E * FC * (q - 1))
                copy_two(xallT[:, q % 2, :, :], Tp).then_inc(C["xT_in"], 1)

            def route_exps(q):
                act.wait_ge(C["z_ready"], q + 1)
                for k in range(2):
                    ins = nc.scalar.activation(r8[5 + k][:, :, :], r8[5 + k][:, :, :], ACT.Exp)
                ins.then_inc(C["zexp_ready"], 1)

            def weighed_turned(k):
                act.wait_ge(C["xwT_mm"], k + 1)
                if k >= 2:
                    act.wait_ge(C["gu_mm"], FC * (k - 1))
                copy_two(xwT[:, k % 2, :, :], Tp).then_inc(C["xwT_in"], 1)

            def experts_out(q):
                act.wait_ge(C["down_mm"], E * FC * (q + 1))
                if q:
                    act.wait_ge(C["back_mm"], q)
                copy_two(oT[:, :, :], AC).then_inc(C["oT_in"], 1)

            def match_turned(p):
                act.wait_ge(G["xT_mm"], p + 1)
                if p:
                    act.wait_ge(Z["h_mm"], 2 * p)
                copy_two(xzT[:, :, :], Tp).then_inc(G["xT_in"], 1)

            def pick_turned(p):
                act.wait_ge(G["pickT_mm"], p + 1)
                if p:
                    act.wait_ge(G["got_mm"], p)
                copy_two(pickT[:, :, :], Tp).then_inc(G["pickT_in"], 1)

            def last_turned(p):
                act.wait_ge(Z["xT_mm"], p + 1)
                act.wait_ge(G["sim_mm"], p + 1)
                copy_two(xzT[:, :, :], Tp).then_inc(Z["xT_in"], 1)

            def hidden_out(k):
                def piece(p):
                    act.wait_ge(Z["h_mm"], 2 * p + k + 1)
                    act.wait_ge(Z["b1_ready"], 1)
                    if p:
                        act.wait_ge(Z["node_ready"], 2 * p + k - 1)
                    for i in range(2):
                        ins = nc.scalar.activation(ha[:, k, 256 * i:256 * i + 256], (Tp, Mp)[k][:, 256 * i:256 * i + 256],
                                                   ACT.Identity, bias=b1x[:, 2 * k + i:2 * k + i + 1], scale=FIX)
                    ins.then_inc(Z["h_in"], 1)
                return piece

            def gelus(p):
                for k in range(2):
                    act.wait_ge(Z["node_ready"], 2 * p + k + 1)
                    if p:
                        act.wait_ge(Z["hq_ready"], 2 * p)
                    nc.scalar.activation(g0[:, k, :], hn[:, k, :], ACT.Gelu, scale=0.25)
                    nc.scalar.activation(g1[:, k, :], hn[:, k, :], ACT.Gelu, bias=quarter[:, :], scale=0.25)\
                        .then_inc(Z["gelu_ready"], 1)

            pieces = dict(xTin=x_turned, qkvout=qkv_out, pad=pad, takeq=take, exps=exps,
                          tpin0=lambda n: probs_turned(n, 0), tpin1=lambda n: probs_turned(n, 1), yTin=y_turned,
                          textin=text_turned, tnin=tnorm_turned, pTin=quarter_turned, zexp=route_exps,
                          xwTin=weighed_turned, uo=unit_out, oT=experts_out, gTin=match_turned, pickin=pick_turned,
                          zTin=last_turned, ha0=hidden_out(0), ha1=hidden_out(1), gelu=gelus)
            for stage, i in order["scalar"]:
                pieces[stage](i)

        @block.vector
        def _(dve):
            v = nc.vector
            count = [0]

            def link(ins):
                count[0] += 1
                ins.then_inc(step, 1)
                dve.wait_ge(step, count[0])

            def moments(tiles):
                for t in tiles:
                    ins = v.bn_stats(stats[:, t, :], x[:, t, :])
                link(ins)
                for t in tiles:
                    ins = v.bn_aggr(mv[:, t, :], stats[:, t, :])
                link(ins)
                tt = slice(tiles[0], tiles[-1] + 1)
                return v.tensor_scalar(powed[:, 0, tt], mv[:, tt, 1], LN_EPS, None, ALU.add)

            def normalise(o, t):
                return v.tensor_scalar(o, x[:, t, :], mv[:, t, 0:1], rstd[:, t:t + 1], ALU.subtract, ALU.mult)

            def quantise(src, g, o):
                link(v.tensor_reduce(small[:, 0:1], src, X, ALU.max, apply_absolute_value=True))
                link(v.tensor_scalar(g, small[:, 0:1], 1e-8, 1.0 / 127.0, ALU.max, ALU.mult))
                link(v.reciprocal(small[:, 1:2], g))
                link(v.tensor_scalar(qt[:, :], src, small[:, 1:2], 127.0, ALU.mult, ALU.min))
                link(v.tensor_scalar(qt[:, :], qt[:, :], -128.0, MAGIC, ALU.max, ALU.add))
                return v.tensor_scalar(o, qt[:, :], MAGIC, None, ALU.subtract)

            dve.wait_ge(dma_param_a, 16)
            parts = ((0, 128), (128, 160), (160, 192))
            for i, (a, b) in enumerate(parts):
                v.tensor_reduce(wabs[:, i:i + 1], w_qkv[:, a:b], X, ALU.add, apply_absolute_value=True)\
                    .then_inc(wabs_ready, 1)
            v.tensor_reduce(wabs[:, 3:4], w_p, X, ALU.add, apply_absolute_value=True).then_inc(wabs_ready, 1)
            dve.wait_ge(dma_const, 16)
            v.tensor_copy(identb[:, :], ident).then_inc(tern_ready, 1)
            link(v.tensor_copy(causal_b[:, :], causal_add))
            link(v.tensor_tensor(cgain[:, :, :], rope_c, gain.unsqueeze(2).to_broadcast([P, 20, HD]), ALU.mult))
            link(v.tensor_tensor(sgain[:, :, :], rope_s, gain.unsqueeze(2).to_broadcast([P, 20, HD]), ALU.mult))
            dve.wait_ge(alpha_mm, 1)
            for i, n in enumerate((128, 32, 32, 128)):
                ins = v.tensor_scalar(alphas[:, i:i + 1], Mp[:, i:i + 1], 1.0 / (n * D), 1e-8, ALU.mult, ALU.max)
            ins.then_inc(tern_ready, 1)
            link(v.memset(alpha20[:, :], 1.0))
            link(v.tensor_scalar(alpha20[:, 0:16], alpha20[:, 0:16], alphas[:, 0:1], None, ALU.mult))
            link(v.tensor_scalar(alpha20[:, 16:20], alpha20[:, 16:20], alphas[:, 1:2], None, ALU.mult))
            link(v.reciprocal(inv_alphas[:, :], alphas[:, :]))
            for i, (a, b) in enumerate(parts + ((192, 320),)):
                src = w_qkv[:, a:b] if i < 3 else w_p
                ins = v.tensor_scalar(tq[:, a:b], src, inv_alphas[:, i:i + 1], 1.0, ALU.mult, ALU.min)
            link(ins)
            link(v.tensor_scalar(tq[:, :], tq[:, :], -1.0, MAGIC, ALU.max, ALU.add))
            v.tensor_scalar(tern[:, :], tq[:, :], MAGIC, None, ALU.subtract).then_inc(tern_ready, 1)
            dve.wait_ge(dma_x, 16)
            dve.wait_ge(presets, PRESETS)

            def job_stats(n):
                L, t = kind[n], tile[n]
                if L == "B":
                    dve.wait_ge(S["x_updated"], job("A", t) + 1)
                if L == "D":
                    dve.wait_ge(C["x_updated"], t // 2 + 1)
                moments([t]).then_inc(S["var_ready"], 1)

            def front(n):
                L, t, b = kind[n], tile[n], n % 2
                dve.wait_ge(S["rstd_ready"], n + 1)
                if n >= 2:
                    dve.wait_ge(S["xT_mm"], n - 1)
                if L == "A":
                    link(normalise(xn[:, b, :], t))
                    quantise(xn[:, b, :], gam[:, nth(n, "A") % 4, :], xint[:, b, :]).then_inc(S["xn_ready"], 1)
                else:
                    normalise(xn[:, b, :], t).then_inc(S["xn_ready"], 1)

            def rotate_a(n):
                i = nth(n, "A")
                b, g = i % 2, gam[:, i % 4, :]
                dve.wait_ge(S["qkv_in"], i + 1)
                if i:
                    dve.wait_ge(S["rms_ready"], i)
                if i >= 2:
                    dve.wait_ge(S["rotated"], i - 1)
                v.tensor_scalar(fac[:, b, :], alpha20[:, :], g, None, ALU.mult)
                link(v.tensor_reduce(rr[:, 0, :], sq[:, b, :, :], X, ALU.add))
                link(v.scalar_tensor_tensor(rr[:, 1, :], rr[:, 0, :], 1.0 / HD, fac[:, b, :], ALU.mult, ALU.mult))
                link(v.tensor_tensor(rr[:, 0, :], rr[:, 1, :], fac[:, b, :], ALU.mult))
                v.tensor_scalar(rms[:, b, 0, :], rr[:, 0, :], RMS_EPS, None, ALU.add).then_inc(S["rms_ready"], 1)

            def rotate_b(n):
                i = nth(n, "A")
                b, o_, g = i % 2, n % 2, gam[:, i % 4, :]
                dve.wait_ge(S["rms_in"], i + 1)
                if i:
                    dve.wait_ge(S["rotated"], i)
                v.tensor_tensor(gav[:, :], g, alphas[:, 2:3], ALU.mult)
                link(v.tensor_tensor(rk[:, :], rms[:, b, 1, :], fac[:, b, :], ALU.mult))
                qk = qkv[:, b, 0:160].rearrange("p (s c) -> p s c", c=HD)
                link(v.tensor_tensor(qn[:, :, :], qk, rk[:, :].unsqueeze(2).to_broadcast([P, 20, HD]), ALU.mult))
                if n >= 2:
                    dve.wait_ge(S["turn_mm"], n - 1)
                v.tensor_scalar(vtok[:, o_, :], qkv[:, b, 160:192], gav[:, :], None, ALU.mult)
                v.tensor_tensor(m1[:, :, :], qn[:, :, :], cgain[:, :, :], ALU.mult)
                swapped = qn[:, :, :].rearrange("p s (u c) -> p s u c", u=2)[:, :, ::-1, :]
                link(v.tensor_tensor(m2[:, :, :].rearrange("p s (u c) -> p s u c", u=2), swapped,
                                     sgain[:, :, :].rearrange("p s (u c) -> p s u c", u=2), ALU.mult))
                for half in range(2):
                    c = slice(64 * half, 64 * half + 64)
                    o = slice(AUG * half, AUG * half + HD)
                    v.tensor_tensor(qpad[c, o_, :, :, o], m1[c, 0:16, :].rearrange("p (r g) c -> p r g c", g=NG),
                                    m2[c, 0:16, :].rearrange("p (r g) c -> p r g c", g=NG), ALU.add)
                    ins = v.tensor_tensor(kpad[c, o_, 0, :, o], m1[c, 16:20, :], m2[c, 16:20, :], ALU.add)
                ins.then_inc(S["rotated"], 1)

            def add_bias(n):
                L, b = kind[n], n % 2
                w = 384 if L == "B" else 400
                dve.wait_ge(S["proj_mm"], n + 1)
                if n >= 2:
                    dve.wait_ge(S["turn_mm"], n - 1)
                    if kind[n - 2] == "D":
                        dve.wait_ge(S["n_in"], nth(n - 1, "D"))
                v.tensor_tensor(proj[:, b, 0:w], Mp[:, 0:w], b_in[L], ALU.add).then_inc(S["added"], 1)

            def take(n):
                L, b = kind[n], n % 2
                dve.wait_ge(S["turn_mm"], n + 1)
                if n >= 2:
                    dve.wait_ge(S["scores_mm"], n - 1)
                    dve.wait_ge(S["pv_mm"], n - 1)
                nr = 1 if L == "A" else NR
                k = Sp[:, 512:512 + 64 * nr].rearrange("p (r k) -> p r k", k=64).unsqueeze(2).to_broadcast([P, nr, 2, 64])
                v.tensor_tensor(kbd[:, b, 0:nr, :, :], k, gmask.unsqueeze(1).unsqueeze(3).to_broadcast([P, nr, 2, 64]), ALU.mult)
                j = 2 if L == "A" else 8
                vv = Sp[:, 768:768 + 32 * j].rearrange("p (a j w c) -> p a j w c", a=2, j=j, w=2)
                for w_ in range(2):
                    c = slice(64 * w_, 64 * w_ + 64)
                    ins = v.tensor_copy(vbd[c, b, 0:j, :, AUG * w_:AUG * w_ + HD].rearrange("p j a c -> p a j c"),
                                        vv[c, :, :, w_, :])
                ins.then_inc(S["dve_took"], 1)

            def shift(n):
                b = n % 2
                dve.wait_ge(S["scores_mm"], n + 1)
                if n >= 2:
                    dve.wait_ge(S["pT_mm"], 2 * (n - 1))
                sc = Sp[:, :].rearrange("p (h k) -> p h k", h=H)
                if kind[n] == "D":
                    v.tensor_tensor(probs[:, b, :, :], sc, causal01.unsqueeze(1).to_broadcast([P, H, 64]), ALU.mult)\
                        .then_inc(S["shifted"], 1)
                    return
                if n:
                    dve.wait_ge(S["shifted"], n)
                link(v.tensor_reduce(mx[:, :], sc, X, ALU.max))
                v.tensor_tensor(probs[:, b, :, :], sc, mx[:, :].unsqueeze(2).to_broadcast([P, H, 64]), ALU.subtract)\
                    .then_inc(S["shifted"], 1)

            def norm(n):
                L, b = kind[n], n % 2
                dve.wait_ge(S["pv_mm"], n + 1)
                if n >= 2:
                    dve.wait_ge(S["yT_mm"], n - 1)
                o = Op[:, 0:2 * OW].rearrange("p (a s c) -> p a s c", a=2, c=AUG)
                if L == "D":
                    j = nth(n, "D")
                    dve.wait_ge(S["n_in"], j + 1)
                else:
                    if n:
                        dve.wait_ge(S["y_ready"], n)
                    v.reciprocal(rden[0:64, :], o[0:64, 0, :, HD])
                    link(v.reciprocal(rden[64:128, :], o[64:128, 1, :, HD]))
                for half in range(2):
                    c = slice(64 * half, 64 * half + 64)
                    f = nexp[c, j % 2, :] if L == "D" else rden[c, :]
                    ins = v.tensor_tensor(y[c, b, :, :], o[c, half, :, 0:HD],
                                          f.unsqueeze(2).to_broadcast([64, H, HD]), ALU.mult)
                if L == "A":
                    link(ins)
                    ins = quantise(y[:, b, :, :].rearrange("p h c -> p (h c)"), ygam[:, b, :], yint[:, b, :])
                ins.then_inc(S["y_ready"], 1)

            def update(n):
                L, t, b = kind[n], tile[n], n % 2
                dve.wait_ge(S["out_mm"], n + 1)
                if L == "A":
                    link(v.tensor_tensor(small[:, 3:4], ygam[:, b, :], alphas[:, 3:4], ALU.mult))
                    v.scalar_tensor_tensor(x[:, t, :], Op[:, 0:D], small[:, 3:4], x[:, t, :], ALU.mult, ALU.add)\
                        .then_inc(S["x_updated"], 1)
                else:
                    dve.wait_ge(S["x_updated"], n)
                    link(v.tensor_tensor(out_b[:, :], Op[:, 0:D], b_out[L], ALU.add))
                    v.tensor_tensor(x[:, t, :], x[:, t, :], out_b[:, :], ALU.add).then_inc(S["x_updated"], 1)

            def two(t0):
                return x[:, t0:t0 + 2, :].rearrange("p t n -> p (t n)")

            it = iota8.unsqueeze(1).to_broadcast([P, 2, E])

            def over(a):
                return a[:, :].unsqueeze(2).to_broadcast([P, 2, E])

            def top(src, m, oh, tmp, i1):
                link(v.tensor_reduce(m[:, :], src[:, :, :], X, ALU.max))
                link(v.tensor_tensor(tmp[:, :, :], src[:, :, :], over(m), ALU.is_equal))
                link(v.scalar_tensor_tensor(tmp[:, :, :], tmp[:, :, :], -64.0, it, ALU.mult, ALU.add))
                link(v.tensor_reduce(i1[:, :], tmp[:, :, :], X, ALU.min))
                link(v.tensor_tensor(oh[:, :, :], tmp[:, :, :], over(i1), ALU.is_equal))

            def route_a(q):
                dve.wait_ge(C["lg_in"], q + 1)
                top(lg, r1[0], r8[0], r8[3], r1[2])
                link(v.scalar_tensor_tensor(r8[2][:, :, :], r8[0][:, :, :], -3.0e38, lg[:, :, :], ALU.mult, ALU.add))
                top(r8[2], r1[1], r8[1], r8[3], r1[2])
                for k, base in ((0, lg), (1, r8[2])):
                    thr, kept, z = r1[k], r8[3 + k], r8[5 + k]
                    link(v.scalar_tensor_tensor(kept[:, :, :], lg[:, :, :], -1.0, lg[:, :, :], ALU.mult, ALU.max))
                    link(v.tensor_tensor(kept[:, :, :], kept[:, :, :], over(thr), ALU.max))
                    link(v.tensor_scalar(kept[:, :, :], kept[:, :, :], 1e-30, None, ALU.max))
                    v.tensor_tensor(z[:, :, :], lg[:, :, :], over(thr), ALU.subtract)
                    link(v.reciprocal(kept[:, :, :], kept[:, :, :]))
                    link(v.tensor_tensor(kept[:, :, :], kept[:, :, :], z[:, :, :], ALU.mult))
                    v.tensor_scalar(kept[:, :, :], kept[:, :, :], -2.0 * JITTER, None, ALU.is_ge)
                    ins = v.tensor_tensor(z[:, :, :], base[:, :, :], over(thr), ALU.subtract)
                ins.then_inc(C["z_ready"], 1)

            def route_b(q):
                dve.wait_ge(C["zexp_ready"], q + 1)
                for k in range(2):
                    link(v.tensor_tensor(r8[5 + k][:, :, :], r8[5 + k][:, :, :], r8[3 + k][:, :, :], ALU.mult))
                    link(v.tensor_reduce(r1[3][:, :], r8[5 + k][:, :, :], X, ALU.add))
                    link(v.reciprocal(r1[4][:, :], r1[3][:, :]))
                    link(v.tensor_tensor(r8[k][:, :, :], r8[k][:, :, :], over(r1[4]), ALU.mult))
                link(v.tensor_tensor(wt[:, q % 2, :, :], r8[0][:, :, :], r8[1][:, :, :], ALU.add))

            def weigh(k):
                q, e = divmod(k, E)
                if k >= 2:
                    dve.wait_ge(C["xwT_mm"], k - 1)
                v.scalar_tensor_tensor(xw[:, k % 2, :, :], xall[:, q % 2, :, :], 0.5,
                                       wt[:, q % 2, :, e:e + 1].to_broadcast([P, 2, D]), ALU.mult, ALU.mult)\
                    .then_inc(C["xw_ready"], 1)

            def gate(u):
                dve.wait_ge(C["u_in"], u + 1)
                if u >= NB:
                    dve.wait_ge(C["down_mm"], u - NB + 1)
                v.scalar_tensor_tensor(hh[:, u % NB, :], th[:, u % NB, :], 1.0, FU[:, u % 2, 0:256], ALU.add, ALU.mult)\
                    .then_inc(C["gated"], 1)

            def best_row(p):
                dve.wait_ge(G["sim_mm"], p + 1)
                if p:
                    dve.wait_ge(G["pickT_mm"], p)
                sc = Mp[:, 0:128].rearrange("p (t k) -> p t k", t=2)
                link(v.tensor_reduce(best[0][:, :], sc, X, ALU.max))
                link(v.tensor_tensor(sim[:, :, :], sc, best[0][:, :].unsqueeze(2).to_broadcast([P, 2, 64]), ALU.is_equal))
                link(v.scalar_tensor_tensor(sim2[:, :, :], sim[:, :, :], -1024.0, iota64.unsqueeze(1).to_broadcast([P, 2, 64]),
                                            ALU.mult, ALU.add))
                link(v.tensor_reduce(best[1][:, :], sim2[:, :, :], X, ALU.min))
                for half in range(2):
                    c = slice(64 * half, 64 * half + 64)
                    ins = v.tensor_tensor(pick[c, :, c], sim2[c, :, :], best[1][c, :].unsqueeze(2).to_broadcast([64, 2, 64]),
                                          ALU.is_equal)
                ins.then_inc(G["pick_ready"], 1)

            def nodes(p, k):
                dve.wait_ge(Z["h_in"], 2 * p + k + 1)
                if p:
                    dve.wait_ge(Z["gelu_ready"], 2 * p - 1 + k)
                hi, n_ = hi_[:, k, :], hn[:, k, :]
                link(v.tensor_scalar(hi, ha[:, k, :], MAGIC, MAGIC, ALU.add, ALU.subtract))
                link(v.tensor_scalar(n_, hi, 1.0 / 64, -63.0 / 128, ALU.mult, ALU.add))
                v.tensor_scalar(n_, n_, MAGIC, MAGIC, ALU.add, ALU.subtract).then_inc(Z["node_ready"], 1)
                dve.wait_ge(Z["node_ready"], 2 * p + k + 1)
                link(v.scalar_tensor_tensor(hi, hi, 1.0 / 64, n_, ALU.mult, ALU.subtract))

            def blend(p, k):
                a, b = g0[:, k, :], g1[:, k, :]
                dve.wait_ge(Z["gelu_ready"], 2 * p + k + 1)
                if p:
                    dve.wait_ge(Z["out_mm"], p)
                link(v.tensor_tensor(b, b, a, ALU.subtract))
                link(v.tensor_tensor(b, b, hi_[:, k, :], ALU.mult))
                link(v.tensor_tensor(hd[:, :], b, a, ALU.add))
                link(v.tensor_scalar(hd[:, :], hd[:, :], FIX, MAGIC, ALU.mult, ALU.add))
                v.tensor_scalar(hq[:, 2 * k:2 * k + 2, :].rearrange("p c n -> p (c n)"), hd[:, :], MAGIC, 1.0 / FIX,
                                ALU.subtract, ALU.mult).then_inc(Z["hq_ready"], 1)

            def finish(p):
                dve.wait_ge(Z["out_mm"], p + 1)
                if p:
                    dve.wait_ge(Z["fin"], p)
                link(v.tensor_tensor(fo[:, :].rearrange("p (t n) -> p t n", t=2), Mp[:, 0:256].rearrange("p (t n) -> p t n", t=2),
                                     f_b2.unsqueeze(1).to_broadcast([P, 2, D]), ALU.add))
                link(v.tensor_scalar(fo[:, :], fo[:, :], FIX, MAGIC, ALU.mult, ALU.add))
                link(v.tensor_scalar(fo[:, :], fo[:, :], MAGIC, 1.0 / FIX, ALU.subtract, ALU.mult))
                v.tensor_tensor(two(2 * p), two(2 * p), fo[:, :], ALU.add).then_inc(Z["fin"], 1)

            def text_sums(_):
                dve.wait_ge(dma_text, 16)
                link(v.tensor_tensor(hq[:, :, :].rearrange("p c n -> p (c n)"), text[:, :, :].rearrange("p t n -> p (t n)"),
                                     text[:, :, :].rearrange("p t n -> p (t n)"), ALU.mult))
                v.tensor_reduce(text_sum[:, :], hq[:, :, :].rearrange("p c (a n) -> p (c a) n", n=D), X, ALU.add)\
                    .then_inc(tsum_ready, 1)

            def text_inverse(_):
                dve.wait_ge(tnorm_ready, 1)
                link(v.tensor_scalar(norms[:, :], norms[:, :], 1e-12, None, ALU.max))
                link(v.reciprocal(norms[:, :], norms[:, :]))

            def with_params(_):
                dve.wait_ge(dma_param, 16)
                v.tensor_scalar(b1x[:, :], f_b1, FIX, None, ALU.mult).then_inc(Z["b1_ready"], 1)
                v.tensor_scalar(mask_neg[:, :], mask, float(-1e9 / np.float64(SCALE)), None, ALU.mult).then_inc(mask_ready, 1)

            def text_normalised(i):
                if i:
                    dve.wait_ge(tn_mm, i)
                for j in range(2):
                    ins = v.tensor_scalar(xz[:, j, :], text[:, 2 * i + j, :], norms[:, 2 * i + j:2 * i + j + 1], None, ALU.mult)
                ins.then_inc(tn_ready, 1)

            def add_back(q):
                dve.wait_ge(C["back_mm"], q + 1)
                v.tensor_tensor(two(2 * q), two(2 * q), Tp[:, 0:256], ALU.add).then_inc(C["x_updated"], 1)

            def experts_stats(q):
                dve.wait_ge(S["x_updated"], job("B", 2 * q + 1) + 1)
                moments([2 * q, 2 * q + 1]).then_inc(C["var_ready"], 1)

            def experts_norm(q):
                dve.wait_ge(C["rstd_ready"], q + 1)
                if q >= 2:
                    dve.wait_ge(C["xT_mm"], q - 1)
                    dve.wait_ge(C["xw_ready"], E * (q - 1))
                for i in range(2):
                    ins = normalise(xall[:, q % 2, i, :], 2 * q + i)
                ins.then_inc(C["xn_ready"], 1)

            def logits_out(q):
                dve.wait_ge(C["logits_mm"], q + 1)
                v.tensor_copy(lg[:, :, :].rearrange("p t e -> p (t e)"), Mp[:, 0:2 * E]).then_inc(C["lg_in"], 1)

            def match_stats(p):
                dve.wait_ge(S["x_updated"], job("D", 2 * p + 1) + 1)
                link(moments([2 * p, 2 * p + 1]))
                v.tensor_scalar(powed[:, 1, 2 * p:2 * p + 2], mv[:, 2 * p:2 * p + 2, 1], float(D), None, ALU.mult)\
                    .then_inc(G["var_ready"], 1)

            def match_norm(p):
                tt = slice(2 * p, 2 * p + 2)
                dve.wait_ge(G["powers_ready"], p + 1)
                link(v.tensor_tensor(xnorm[:, tt], xnorm[:, tt], rstd[:, tt], ALU.mult))
                link(v.tensor_scalar(xnorm[:, tt], xnorm[:, tt], 1e-12, None, ALU.max))
                link(v.reciprocal(xnorm[:, tt], xnorm[:, tt]))
                link(v.tensor_tensor(rstd[:, tt], rstd[:, tt], xnorm[:, tt], ALU.mult))
                if p:
                    dve.wait_ge(Z["xT_mm"], p)
                else:
                    dve.wait_ge(tn_mm, NQ)
                for i in range(2):
                    ins = normalise(xz[:, i, :], 2 * p + i)
                ins.then_inc(G["xn_ready"], 1)

            def add_rows(p):
                dve.wait_ge(G["got_mm"], p + 1)
                v.tensor_tensor(two(2 * p), two(2 * p), Op[:, 0:256], ALU.add).then_inc(G["x_updated"], 1)
                dve.wait_ge(G["x_updated"], p + 1)
                moments([2 * p, 2 * p + 1]).then_inc(Z["var_ready"], 1)

            def last_norm(p):
                dve.wait_ge(Z["rstd_ready"], p + 1)
                dve.wait_ge(G["xT_mm"], p + 1)
                for i in range(2):
                    ins = normalise(xz[:, i, :], 2 * p + i)
                ins.then_inc(Z["xn_ready"], 1)

            pieces = dict(stats=job_stats, front=front, rotA=rotate_a, rotB=rotate_b, add=add_bias, take=take, shift=shift,
                          norm=norm, update=update, tsum=text_sums, tnorm2=text_inverse, params=with_params,
                          tn=text_normalised, pstats=experts_stats, pnorm=experts_norm, lgcopy=logits_out, routeA=route_a,
                          routeB=route_b, weigh=weigh, gate=gate, addback=add_back, gstats=match_stats, gnorm=match_norm,
                          best=best_row, gadd=add_rows, znorm=last_norm, nodes0=lambda p: nodes(p, 0),
                          nodes1=lambda p: nodes(p, 1), blend0=lambda p: blend(p, 0), blend1=lambda p: blend(p, 1),
                          finish=finish)
            for stage, i in order["vector"]:
                pieces[stage](i)


def layout(a):
    f = np.float32
    qk_order = np.array([4 * g + r for r in range(NR) for g in range(NG)])
    order = np.array([4 * (2 * gh + g) + r for gh in range(2) for r in range(NR) for g in range(2)])

    def heads(m, axis, order=order):
        shape = m.shape[:axis] + (H, HD) + m.shape[axis + 1:]
        return np.take(m.reshape(shape), order, axis).reshape(m.shape)

    def qk(m, axis):
        return heads(m, axis, qk_order)

    def wide(v, n=P):
        return np.broadcast_to(np.asarray(v, f).reshape(1, -1), (n, np.asarray(v).size))

    eye = np.eye(P, dtype=f)
    at = np.arange(P) % 64
    pair_i = (at[:, None] == np.arange(64)).astype(f)
    dup = np.stack([(np.arange(P)[:, None] == 64 * h + at[None, :]).astype(f) for h in range(2)], 1)
    gmask = (np.arange(P)[:, None] // 32 % 2 == np.arange(2)).astype(f)
    keep = np.arange(64)[None, :] <= at[:, None]
    inv = f(1.0) / np.power(f(10000.0), np.arange(0, HD, 2, dtype=f) / f(HD)).astype(f)
    ang = (at.astype(f)[:, None] * inv[None, :]).astype(f)
    c, s = np.cos(ang).astype(f), np.sin(ang).astype(f)
    rope_c = np.broadcast_to(np.concatenate([c, c], 1)[:, None], (P, 20, HD))
    rope_s = np.broadcast_to(np.concatenate([s, -s], 1)[:, None], (P, 20, HD))
    consts = [eye, pair_i, dup, gmask, keep.astype(f), np.where(keep, f(0), f(MASKED)), rope_c, rope_s,
              wide(np.arange(E)), wide(np.arange(64))]

    a = {n: np.asarray(v) for n, v in a.items()}
    w_qkv = np.concatenate([qk(a["L0_attn_Wq"].T, 1), a["L0_attn_Wk"].T, a["L0_attn_Wv"].T], 1)
    gain = np.concatenate([a["L0_attn_q_gain"][qk_order], np.ones(4, f)])
    params_a = [w_qkv, heads(a["L0_attn_Wp"].T, 0), wide(gain)]
    n = "L0_xattn_"
    params = [qk(a[n + "Wq"], 1), qk(a[n + "Wk"], 1), heads(a[n + "Wv"], 1), heads(a[n + "Wo"], 0)]
    params += [wide(qk(a[n + b][None], 1)) for b in ("bq", "bk")] + [wide(heads(a[n + "bv"][None], 1))] + [wide(a[n + "bo"])]
    wqk, bqk = a["L1_attn_Wqk_w"], a["L1_attn_Wqk_b"]
    params += [qk(wqk[:D].T, 1), qk(wqk[D:].T, 1), heads(a["L1_attn_Wv_w"].T, 1), a["L1_attn_Wn_w"][order].T,
               heads(a["L1_attn_Wo_w"].T, 0)]
    params += [wide(qk(b[None], 1)) for b in (bqk[:D], bqk[D:])] + [wide(heads(a["L1_attn_Wv_b"][None], 1))]
    params += [wide(a["L1_attn_Wn_b"][order]), wide(a["L1_attn_Wo_b"])]
    params += [a["mask_Bx1x1xS2_fk0"].reshape(NT, P).T, a["L0_ffn_gate_w"], a["L1_ffn_w1"],
               a["L1_ffn_b1"].reshape(FC, P).T, a["L1_ffn_w2"].reshape(FC, P, D).transpose(1, 0, 2), wide(a["L1_ffn_b2"])]

    def side_by_side(parts):
        return np.ascontiguousarray(np.concatenate([np.asarray(i).reshape(P, -1) for i in parts], 1).astype(f, copy=False))

    return {
        "consts": side_by_side(consts), "params_a": side_by_side(params_a), "params": side_by_side(params),
        "x": np.ascontiguousarray(a["x"]).reshape(NT * P, D), "ctx": np.ascontiguousarray(a["ctx_1024"]).reshape(NT * P, D),
        "w1": np.ascontiguousarray(a["L0_ffn_w1"]), "w2": np.ascontiguousarray(a["L0_ffn_w2"]),
        "w3": np.ascontiguousarray(a["L0_ffn_w3"]),
    }


def kernel(**inputs):
    from concourse import bacc
    from concourse.bass_utils import run_bass_kernel_spmd

    nc = bacc.Bacc("TRN2", target_bir_lowering=False, num_devices=1)
    arrays, d = {}, {}
    for name, a in layout(inputs).items():
        arrays[f"in_{name}"] = a
        d[name] = nc.dram_tensor(f"in_{name}", a.shape, mybir.dt.from_np(a.dtype), kind="ExternalInput").ap()
    out = nc.dram_tensor("out", (NT * P, D), F32, kind="ExternalOutput").ap()
    build(nc, d, out)
    r = run_bass_kernel_spmd(nc, [arrays], core_ids=[0])
    return np.asarray(r.results[0]["out"]).reshape(BATCH, SEQ, D)
```

```python
from contextlib import ExitStack

import numpy as np

import concourse.bass as bass
from concourse import mybir

F32 = mybir.dt.float32
BF16 = mybir.dt.bfloat16
ALU = mybir.AluOpType
ACT = mybir.ActivationFunctionType
X = mybir.AxisListType.X

P = 128
D = 128
BATCH, SEQ = 16, 64
NT = BATCH * SEQ // P
NQ = NT // 2
H, HD, NG, NR = 16, 8, 4, 4
E, F, FC = 8, 512, 4
SCALE = float(1.0 / np.sqrt(np.float32(HD)))
MASKED = -1.0e30
MAGIC = 1.5 * 2.0 ** 23
LN_EPS = 1e-5
RMS_EPS = float(np.finfo(np.float32).eps)
AUG = HD + 1
OW = H * AUG
FIX = 256.0
JITTER = 0.01
NB = 4

JOBS = [(j[0], int(j[1])) for j in (
    "A0 A1 A2 A3 B0 B1 A4 B2 A5 B3 B4 B5 A6 D0 A7 D1 B6 B7 D2 D3 D4 D5 D6 D7").split()]
URGENCY = {
    'add': 30, 'addback': 100, 'back': 10, 'bias': 100, 'finish': -10, 'gTin': 100,
    'gate': 30, 'gnorm': -30, 'gstats': -30, 'h': 100, 'ha0': -30, 'ha1': -10,
    'logits': 10, 'nodes1': -10, 'norm': -30, 'pT': 100, 'pTin': -30, 'pad': -30,
    'params': -10, 'pickT': -10, 'pnorm': 10, 'proj': -10, 'prstd': -100, 'qkvout': -10,
    'rotA': 100, 'rotB': -30, 'routeA': 10, 'routeB': -10, 'rstd': -100, 'shift': -10,
    'sim': -30, 'stats': -30, 'take': -100, 'tn': 10, 'tnT': -30, 'tnin': -10,
    'tnorm': -10, 'tnorm2': -10, 'tp0': -10, 'tpin1': -100, 'turn': -100, 'values': -30,
    'weigh': 10, 'xT': 30, 'xTin': 10, 'xwT': -10, 'yTin': -100, 'zT': 30,
    'zexp': -30, 'zh0': -30, 'znorm': 30}
AHEAD = 3
LATENCY = 0.17
WARM = 0.22


def stages():
    st = {}

    def add(name, i, engine, cost, after, bank=None, emptied_by=()):
        st[name, i] = (engine, cost, [a for a in after if a and a[1] >= 0], bank, emptied_by)

    where = {j: n for n, j in enumerate(JOBS)}
    a_jobs = [n for n, (L, _) in enumerate(JOBS) if L == "A"]
    for n, (L, t) in enumerate(JOBS):
        def before(name):
            return name, n - 2
        A, masked = L == "A", L != "D"
        x_from = {"A": None, "B": ("update", where["A", t]), "D": ("addback", t // 2)}[L]
        if n >= AHEAD:
            add("stats", n, "vector", 0.6, [x_from])
        add("rstd", n, "pool", 0.5, [("stats", n)])
        add("front", n, "vector", 1.75 if A else 0.3, [("rstd", n), before("xT")])
        add("xT", n, "tensor", 0.1, [("front", n), before("proj")], "Mp", [("xTin", n)])
        add("xTin", n, "scalar", 0.2, [("xT", n), before("proj")])
        add("proj", n, "tensor", 0.1 if A else 0.7, [("xTin", n), L == "B" and ("textin", t // 2)], "Mp",
            [("qkvout" if A else "add", n)])
        if A:
            add("qkvout", n, "scalar", 0.4, [("proj", n), n >= 2 and ("rotB", a_jobs[max(a_jobs.index(n) - 2, 0)])])
            if a_jobs.index(n) < 2:
                add("qkvout", n, "scalar", 0.4, [("proj", n)])
            add("rotA", n, "vector", 1.1, [("qkvout", n)])
            add("rms", n, "pool", 3.6, [("rotA", n)])
            add("rotB", n, "vector", 2.4, [("rms", n), before("turn")])
        else:
            add("add", n, "vector", 0.5, [("proj", n), before("turn"), n >= 2 and JOBS[n - 2][0] != "A" and before("pad")])
            add("bias", n, "pool", 0.4, [("front", n), ("params", 0)])
            add("pad", n, "scalar", 1.0, [("add", n), before("turn"), ("params", 0),
                                          L == "D" and t >= 4 and ("norm", where["D", t - 4])])
        add("turn", n, "tensor", 0.9 if A else 1.9, [("rotB" if A else "pad", n), before("scores")], "Sp", [("take", n)])
        add("take", n, "scalar", 0.9 if A else 1.6, [("turn", n), before("scores"), before("values")])
        add("scores", n, "tensor", 2.1 if A else 1.8, [("take", n)], "Sp", [("shift", n)])
        add("shift", n, "vector", 2.4 if masked else 1.1, [("scores", n), masked and before("exps"), before("tp1"), before("values")])
        if masked:
            add("exps", n, "scalar", 0.9, [("shift", n)])
            add("tp0", n, "tensor", 0.4, [("exps", n)], "Tp", [("tpin0", n)])
            add("tp1", n, "tensor", 0.4, [("tp0", n)], "Tp", [("tpin1", n)])
            add("tpin0", n, "scalar", 0.5, [("tp0", n), before("values")])
            add("tpin1", n, "scalar", 0.5, [("tp1", n), ("tpin0", n)])
        add("values", n, "tensor", 1.7, [("tpin1" if masked else "shift", n), ("take", n), before("yT")], "Op", [("norm", n)])
        add("norm", n, "vector", {"A": 2.45, "B": 0.9, "D": 0.5}[L], [("values", n), before("yT")])
        add("yT", n, "tensor", 0.1, [("norm", n), before("out")], "Op", [("yTin", n)])
        add("yTin", n, "scalar", 0.2, [("yT", n), before("out")])
        add("out", n, "tensor", 0.2, [("yTin", n)], "Op", [("update", n)])
        add("update", n, "vector", 0.4, [("out", n), ("bias", n)])
    add("params", 0, "vector", 0.3, [("front", where["A", 1])])
    add("tnorm", 0, "pool", 1.6, [("tsum", 0)])
    add("tnorm2", 0, "vector", 0.6, [("tnorm", 0)])
    for i in range(NQ):
        add("text", i, "tensor", 0.2, [], "Mp", [("textin", i)])
        add("textin", i, "scalar", 0.3, [("text", i)])
        add("tn", i, "vector", 0.4, [("tnorm2", 0), ("tnT", i - 1)])
        add("tnT", i, "tensor", 0.2, [("tn", i)], "Mp", [("tnin", i)])
        add("tnin", i, "scalar", 0.3, [("tnT", i)])
    for q in range(NQ):
        reused = ("weigh", E * (q - 1) - 1)
        add("pstats", q, "vector", 0.9, [("update", where["B", 2 * q + i]) for i in range(2)])
        add("prstd", q, "pool", 0.6, [("pstats", q)])
        add("pnorm", q, "vector", 0.5, [("prstd", q), reused, ("pT", q - 2)])
        add("pT", q, "tensor", 0.2, [("pnorm", q)], "Tp", [("pTin", q)])
        add("pTin", q, "scalar", 0.3, [("pT", q), q >= 2 and ("gu", E * FC * (q - 1) - 1)])
        add("logits", q, "tensor", 0.1, [("pTin", q)], "Mp", [("lgcopy", q)])
        add("lgcopy", q, "vector", 0.1, [("logits", q), ("routeB", q - 1)])
        add("routeA", q, "vector", 4.0, [("lgcopy", q)])
        add("zexp", q, "scalar", 0.2, [("routeA", q)])
        add("routeB", q, "vector", 1.2, [("zexp", q), reused])
        add("oT", q, "scalar", 0.3, [("down", E * FC * (q + 1) - 1), ("back", q - 1)])
        add("back", q, "tensor", 0.2, [("oT", q)], "Tp", [("addback", q)])
        add("addback", q, "vector", 0.3, [("back", q)])
    for k in range(NQ * E):
        add("weigh", k, "pool", 0.7, [("routeB", k // E), ("xwT", k - 2)])
        add("xwT", k, "tensor", 0.2, [("weigh", k)], "Tp", [("xwTin", k)])
        add("xwTin", k, "scalar", 0.3, [("xwT", k), k >= 2 and ("gu", FC * (k - 1) - 1)])
    for u in range(NQ * E * FC):
        q = u // (E * FC)
        add("gu", u, "tensor", 0.87, [("xwTin", u // FC), ("pTin", q)], f"FU{u % 2}", [("gate", u)])
        add("uo", u, "scalar", 0.53, [("gu", u), ("h", u - NB)])
        add("gate", u, "vector", 0.34, [("uo", u), ("down", u - NB)])
        add("h", u, "pool", 0.7, [("gate", u)])
        add("down", u, "tensor", 0.44, [("h", u), u % (E * FC) == 0 and ("oT", q - 1)])
    for p in range(NQ):
        add("gstats", p, "vector", 1.0, [("update", where["D", 2 * p + i]) for i in range(2)])
        add("gpow", p, "pool", 1.2, [("gstats", p)])
        add("gnorm", p, "vector", 1.3, [("gpow", p), ("zT", p - 1), ("tnT", NQ - 1)])
        add("gT", p, "tensor", 0.2, [("gnorm", p), ("zh1", p - 1)], "Tp", [("gTin", p)])
        add("gTin", p, "scalar", 0.3, [("gT", p), ("zh1", p - 1)])
        add("sim", p, "tensor", 0.4, [("gTin", p), ("tnin", NQ - 1)], "Mp", [("best", p)])
        add("best", p, "vector", 1.3, [("sim", p), ("pickT", p - 1)])
        add("pickT", p, "tensor", 0.2, [("best", p)], "Tp", [("pickin", p)])
        add("pickin", p, "scalar", 0.3, [("pickT", p), ("got", p - 1)])
        add("got", p, "tensor", 0.4, [("pickin", p)], "Op", [("gadd", p)])
        add("gadd", p, "vector", 1.3, [("got", p)])
        add("zpow", p, "pool", 0.6, [("gadd", p)])
        add("znorm", p, "vector", 0.5, [("zpow", p), ("gT", p)])
        add("zT", p, "tensor", 0.2, [("znorm", p)], "Tp", [("zTin", p)])
        add("zTin", p, "scalar", 0.3, [("zT", p), ("sim", p)])
        for k in range(2):
            add(f"zh{k}", p, "tensor", 0.9, [("zTin", p), k == 1 and ("zh0", p)], ("Tp", "Mp")[k], [(f"ha{k}", p)])
            add(f"ha{k}", p, "scalar", 0.5, [(f"zh{k}", p), (f"nodes{k}", p - 1), k == 1 and ("ha0", p)])
            add(f"nodes{k}", p, "vector", 2.0, [(f"ha{k}", p), (f"blend{k}", p - 1), k == 1 and ("nodes0", p)])
            add(f"blend{k}", p, "vector", (1.1, 3.1)[k], [(("mix", "gelu")[k], p), ("zout", p - 1)])
        add("mix", p, "pool", 4.2, [("gelu", p)])
        add("gelu", p, "scalar", 4.6, [("nodes0", p), ("nodes1", p), ("blend1", p - 1), ("blend0", p - 1)])
        add("zout", p, "tensor", 1.7, [("blend0", p), ("blend1", p)], "Mp", [("finish", p)])
        add("finish", p, "vector", 1.4, [("zout", p)])
    last = {}
    for n in range(1, len(JOBS)):
        if ("tp0", n) in st:
            done = max((m for m in range(n) if ("tp1", m) in st), default=-1)
            st["tp0", n][2].append(("tp1", done))
            st["tpin0", n][2].append(("tpin1", done))
    for name, i in sorted(st):
        if name in last:
            st[name, i][2].append((name, last[name]))
        last[name] = i
    for s in st:
        st[s][2][:] = [a for a in st[s][2] if a in st]
    return st


def plan():
    st = stages()
    followers, path = {}, {}
    for s, (_, _, after, _, _) in st.items():
        for a in after:
            followers.setdefault(a, []).append(s)
    missing = {s: len(followers.get(s, ())) for s in st}
    stack = [s for s in st if not missing[s]]
    while stack:
        s = stack.pop()
        path[s] = st[s][1] + LATENCY + max((path[f] for f in followers.get(s, ())), default=0.0)
        for a in st[s][2]:
            missing[a] -= 1
            if not missing[a]:
                stack.append(a)
    urgency = {s: path[s] + URGENCY.get(s[0], 0) for s in st}
    engines = ("vector", "scalar", "tensor", "pool")
    order = {e: [] for e in engines}
    ready = {e: [] for e in engines}
    missing = {s: len(st[s][2]) for s in st}
    for s in st:
        if not missing[s]:
            ready[st[s][0]].append(s)
    free_at = {"vector": 12.0, "scalar": 6.0, "tensor": 13.0, "pool": 9.0}
    full, empties, units = {}, {}, [0]
    for s, (_, _, _, bank, emptied_by) in st.items():
        for r in emptied_by:
            empties.setdefault(r, []).append(s)

    def ready_soon():
        return any(s[0] != "keep_warm" for e in engines for s in ready[e]) or any(ev[2] for ev in events)

    events = [(t, 1, ()) for t in free_at.values()]
    while events:
        now = min(e[0] for e in events)
        for event in sorted(e for e in events if e[0] == now):
            events.remove(event)
            s = event[2]
            if not s:
                continue
            for filler in empties.get(s, ()):
                full[st[filler][3]] -= 1
            for f in followers.get(s, ()):
                missing[f] -= 1
                if not missing[f]:
                    ready[st[f][0]].append(f)
        for e in engines:
            can = [s for s in ready[e] if not full.get(st[s][3])] if free_at[e] <= now else []
            if e == "tensor" and not can and free_at[e] <= now and ready_soon() and not 0 < units[0] < NQ * E * FC:
                order[e].append(("keep_warm", 0))
                free_at[e] = now + WARM
                events.append((free_at[e], 1, ()))
            if can:
                s = max(can, key=lambda c: (urgency[c], c))
                ready[e].remove(s)
                order[e].append(s)
                if st[s][3]:
                    full[st[s][3]] = len(st[s][4])
                units[0] += s[0] == "gu"
                free_at[e] = now + st[s][1]
                events += [(free_at[e], 1, ()), (free_at[e] + LATENCY, 0, s)]
    assert sum(s in st for o in order.values() for s in o) == len(st)
    return order


def build(nc, d, out):
    ctx = ExitStack()
    with ctx:
        def sb(name, shape, dt=F32):
            return ctx.enter_context(nc.sbuf_tensor(name, shape, dt))

        def sem(name):
            return ctx.enter_context(nc.semaphore(name))

        def carve(tensor):
            at = [0]

            def take(*shape):
                n = int(np.prod(shape))
                ap = tensor[:, at[0]:at[0] + n]
                at[0] += n
                return ap.rearrange("p (a b) -> p a b", b=shape[1]) if len(shape) == 2 else ap
            return take

        x = sb("x", [P, NT, D])
        text = sb("text", [P, NT, D])
        textT = sb("textT", [P, NT, P])
        tnormT = sb("tnormT", [P, NT, P])
        consts = sb("consts", [P, d["consts"].shape[1]])
        const = carve(consts)
        ident, pairI, dup = const(P), const(64), const(2, P)
        gmask, causalT, causal_add = const(2), const(P), const(64)
        rope_c, rope_s = const(20, HD), const(20, HD)
        iota8, iota64 = const(E), const(64)
        params_a = sb("params_a", [P, d["params_a"].shape[1]])
        param = carve(params_a)
        w_qkv, w_p, gain = param(192), param(D), param(20)
        params = sb("params", [P, d["params"].shape[1]])
        param = carve(params)
        w_in, w_out, b_in, b_out = {}, {}, {}, {}
        for L, n in (("B", 384), ("D", 400)):
            w_in[L], w_out[L], b_in[L], b_out[L] = param(n), param(D), param(n), param(D)
        mask = param(NT)
        gate_w = param(E)
        f_w1, f_b1, f_w2, f_b2 = param(F), param(FC), param(FC, D), param(D)

        w1s, w3s = sb("w1s", [P, E, F]), sb("w3s", [P, E, F])
        w2s = sb("w2s", [P, E, FC, D])

        identb = sb("identb", [P, P], BF16)
        causal_b = sb("causal_b", [P, 64], BF16)
        ones = sb("ones", [P, P])
        tern = sb("tern", [P, 320], BF16)
        tq = sb("tq", [P, 320])
        wabs = sb("wabs", [P, 4])
        alphas = sb("alphas", [P, 4])
        inv_alphas = sb("inv_alphas", [P, 4])
        alpha20 = sb("alpha20", [P, 20])
        cgain, sgain = sb("cgain", [P, 20, HD]), sb("sgain", [P, 20, HD])
        mask_neg = sb("mask_neg", [P, NT])

        stats = sb("stats", [P, NT, 6])
        mv = sb("mv", [P, NT, 2])
        powed = sb("powed", [P, 2, NT])
        rstd = sb("rstd", [P, NT])
        norms, xnorm = sb("norms", [P, NT]), sb("xnorm", [P, NT])
        text_sum = sb("text_sum", [P, NT])
        minus_half, half_ = sb("minus_half", [P, 20]), sb("half", [P, 20])
        small = sb("small", [P, 4])
        xn = sb("xn", [P, 2, D])
        xint = sb("xint", [P, 2, D])
        gam = sb("gam", [P, 4, 1])
        xnT = sb("xnT", [P, 2, P])
        xintT = sb("xintT", [P, 2, P], BF16)
        qkv = sb("qkv", [P, 2, 192])
        proj = sb("proj", [P, 2, 400])
        sq = sb("sq", [P, 2, 20, HD])
        rr, rk = sb("rr", [P, 2, 20]), sb("rk", [P, 20])
        rms = sb("rms", [P, 2, 2, 20])
        fac = sb("fac", [P, 2, 20])
        qn, m1, m2 = (sb(n, [P, 20, HD]) for n in ("qn", "m1", "m2"))
        gav = sb("gav", [P, 1])
        qpad = sb("qpad", [P, 2, NR, NG, 32])
        kpad = sb("kpad", [P, 2, NR, NG, 32])
        kpad_m = sb("kpad_m", [P, 2, NR, NG, 32])
        vtok = sb("vtok", [P, 2, NG * HD])
        qT = sb("qT", [P, 2, NR, P])
        kbd = sb("kbd", [P, 2, NR, 2, 64])
        vbd = sb("vbd", [P, 2, 8, 2, 2 * AUG])
        probs = sb("probs", [P, 2, H, 64])
        mx = sb("mx", [P, H])
        pT = sb("pT", [P, 2, 8, P])
        rden = sb("rden", [P, H])
        nexp = sb("nexp", [P, 4, H])
        y = sb("y", [P, 2, H, HD])
        yint = sb("yint", [P, 2, D])
        ygam = sb("ygam", [P, 2, 1])
        yT = sb("yT", [P, 2, P])
        yintT = sb("yintT", [P, 2, P], BF16)
        qt = sb("qt", [P, D])

        xall = sb("xall", [P, 2, 2, D])
        xallT = sb("xallT", [P, 2, 2, P])
        xw = sb("xw", [P, 2, 2, D])
        xwT = sb("xwT", [P, 2, 2, P])
        th = sb("th", [P, NB, 256])
        hh = sb("hh", [P, NB, 256])
        uu = sb("uu", [P, NB, 256])
        oT = sb("oT", [P, 2, P])
        base, hot, kept, zz = (sb(n, [P, 2, 2, E]) for n in ("base", "hot", "kept", "zz"))
        thr, zsum = sb("thr", [P, 2, 2]), sb("zsum", [P, 2, 2])
        first, tied, absl = sb("first", [P, 2]), sb("tied", [P, 2, E]), sb("absl", [P, 2, E])
        wt = sb("wt", [P, 2, 2, E])

        xz = sb("xz", [P, 2, D])
        xzT = sb("xzT", [P, 2, P])
        sim, sim2 = sb("sim", [P, 2, 64]), sb("sim2", [P, 2, 64])
        best = [sb(f"best{i}", [P, 2]) for i in range(2)]
        pick = sb("pick", [P, 2, P])
        pickT = sb("pickT", [P, 2, P])
        ha, hi_, hn, g0, g1 = (sb(n, [P, 2, 512]) for n in ("ha", "hi", "hn", "g0", "g1"))
        hd, fo = sb("hd", [P, 2, 512]), sb("fo", [P, 2 * D])
        hq = sb("hq", [P, FC, 256])
        b1x = sb("b1x", [P, FC])
        quarter = sb("quarter", [P, 1])

        Sp = ctx.enter_context(nc.psum_tensor("Sp", [P, 1024], F32))
        FU = ctx.enter_context(nc.psum_tensor("FU", [P, 2, 512], F32))
        Tp = ctx.enter_context(nc.psum_tensor("Tp", [P, 512], F32))
        Op = ctx.enter_context(nc.psum_tensor("Op", [P, 512], F32))
        Mp = ctx.enter_context(nc.psum_tensor("Mp", [P, 512], F32))
        AC = ctx.enter_context(nc.psum_tensor("AC", [P, 512], F32))

        dma_x, dma_text, dma_const, dma_param_a, dma_param = (sem(n) for n in (
            "x_loaded", "text_loaded", "consts_loaded", "params_a_loaded", "params_loaded"))
        dma_w = [sem(f"expert{e}_loaded") for e in range(E)]
        stored = sem("stored")
        presets, step, pool_step = sem("presets_done"), sem("dve_step"), sem("pool_step")
        wabs_ready, alpha_mm, tern_ready = sem("wabs_ready"), sem("alpha_mm"), sem("tern_ready")
        tsum_ready, tnorm_ready, tn_ready = sem("tsum_ready"), sem("tnorm_ready"), sem("tn_ready")
        mask_ready = sem("mask_ready")
        text_mm, text_in, tn_mm, tn_in = sem("text_mm"), sem("text_in"), sem("tn_mm"), sem("tn_in")
        S = {n: sem("S_" + n) for n in (
            "var_ready rstd_ready xn_ready xT_mm xT_in proj_mm turn_mm act_took scores_mm shifted "
            "pT_mm pT_in pv_mm y_ready yT_mm yT_in out_mm x_updated "
            "biased qkv_in rms_ready rms_in rotated added padded probs_ready n_in").split()}
        C = {n: sem("C_" + n) for n in "var_ready rstd_ready xn_ready xT_mm xT_in logits_mm z_ready zexp_ready wt_ready xw_ready xwT_mm xwT_in "
             "lg_in gu_mm u_in gated h_ready down_mm oT_in back_mm x_updated".split()}
        G = {n: sem("G_" + n) for n in "var_ready powers_ready xn_ready xT_mm xT_in sim_mm pick_ready pickT_mm pickT_in got_mm x_updated".split()}
        Z = {n: sem("Z_" + n) for n in "b1_ready var_ready rstd_ready xn_ready xT_mm xT_in h_mm h_in node_ready f_ready gelu_ready mixed hq_ready out_mm fin".split()}

        kind = [L for L, _ in JOBS]
        tile = [t for _, t in JOBS]
        order = plan()

        def nth(n, kinds):
            return sum(k in kinds for k in kind[:n])

        def job(L, t):
            return JOBS.index((L, t))

        block = ctx.enter_context(nc.Block())

        @block.sync
        def _(sp):
            sp.dma_start(params_a[:, :], d["params_a"]).then_inc(dma_param_a, 16)
            sp.dma_start(text[:, :, :], d["ctx"].rearrange("(t p) n -> p t n", p=P)).then_inc(dma_text, 16)
            sp.dma_start(params[:, :], d["params"]).then_inc(dma_param, 16)
            for e in range(E):
                sp.dma_start(w1s[:, e, :], d["w1"][e]).then_inc(dma_w[e], 16)
                sp.dma_start(w3s[:, e, :], d["w3"][e]).then_inc(dma_w[e], 16)
                sp.dma_start(w2s[:, e, :, :], d["w2"][e].rearrange("(c p) n -> p c n", p=P)).then_inc(dma_w[e], 16)
            for p in range(NQ):
                sp.wait_ge(Z["fin"], p + 1)
                sp.dma_start(out.rearrange("(t p) n -> p t n", p=P)[:, 2 * p:2 * p + 2, :],
                             x[:, 2 * p:2 * p + 2, :]).then_inc(stored, 16)
            sp.wait_ge(stored, 16 * NQ)

        PRESETS = 13

        @block.gpsimd
        def _(pool):
            for m in (qpad, kpad, kpad_m, vbd, pick):
                nc.gpsimd.memset(m[:], 0.0).then_inc(presets, 1)
            nc.gpsimd.memset(ones[:], 1.0).then_inc(presets, 1)
            nc.gpsimd.memset(quarter[:], 0.25).then_inc(presets, 1)
            nc.gpsimd.memset(minus_half[:], -0.5).then_inc(presets, 1)
            nc.gpsimd.memset(half_[:], 0.5).then_inc(presets, 1)
            pool.wait_ge(presets, 9)
            for half in range(2):
                c, a = slice(64 * half, 64 * half + 64), AUG * half + HD
                nc.gpsimd.memset(vbd[c, :, :, :, a:a + 1], 1.0).then_inc(presets, 1)
                for b in range(2):
                    ins = nc.gpsimd.memset(qpad[c, b, :, :, a:a + 1], 1.0)
                ins.then_inc(presets, 1)

            pool.wait_ge(presets, PRESETS)

            def power(o, base, exponent):
                return nc.gpsimd.tensor_tensor(o, base, exponent[:, 0:o.shape[1]], ALU.pow)

            def unit_h(u):
                pool.wait_ge(C["gated"], u + 1)
                pool.wait_ge(C["u_in"], u + 1)
                nc.gpsimd.tensor_tensor(hh[:, u % NB, :], hh[:, u % NB, :], uu[:, u % NB, :], ALU.mult)\
                    .then_inc(C["h_ready"], 1)

            def rstd_one(n):
                t = tile[n]
                pool.wait_ge(S["var_ready"], n + 1)
                power(rstd[:, t:t + 1], powed[:, 0, t:t + 1], minus_half).then_inc(S["rstd_ready"], 1)

            def add_out_bias(n):
                t = tile[n]
                pool.wait_ge(dma_param, 16)
                pool.wait_ge(S["xn_ready"], n + 1)
                nc.gpsimd.tensor_tensor(x[:, t, :], x[:, t, :], b_out[kind[n]], ALU.add).then_inc(S["biased"], 1)

            def weigh(k):
                q, e = divmod(k, E)
                pool.wait_ge(C["wt_ready"], q + 1)
                if k >= 2:
                    pool.wait_ge(C["xwT_mm"], k - 1)
                nc.gpsimd.tensor_tensor(xw[:, k % 2, :, :], xall[:, q % 2, :, :],
                                        wt[:, q % 2, :, e:e + 1].to_broadcast([P, 2, D]), ALU.mult).then_inc(C["xw_ready"], 1)

            def mix(p):
                a, b = g0[:, 0, :], g1[:, 0, :]
                pool.wait_ge(Z["gelu_ready"], 2 * p + 1)
                pool.wait_ge(Z["f_ready"], 2 * p + 1)
                nc.gpsimd.tensor_tensor(b, b, a, ALU.subtract).then_inc(pool_step, 1)
                pool.wait_ge(pool_step, 2 * p + 1)
                nc.gpsimd.tensor_tensor(b, b, hi_[:, 0, :], ALU.mult).then_inc(pool_step, 1)
                pool.wait_ge(pool_step, 2 * p + 2)
                nc.gpsimd.tensor_tensor(b, b, a, ALU.add).then_inc(Z["mixed"], 1)

            def rms_power(n):
                i = nth(n, "A")
                pool.wait_ge(S["rms_ready"], i + 1)
                power(rms[:, i % 2, 1, :], rms[:, i % 2, 0, :], minus_half).then_inc(S["rms_in"], 1)

            def text_norms(_):
                pool.wait_ge(tsum_ready, 1)
                power(norms[:, :], text_sum[:, :], half_).then_inc(tnorm_ready, 1)

            def rstd_experts(q):
                tt = slice(2 * q, 2 * q + 2)
                pool.wait_ge(C["var_ready"], q + 1)
                power(rstd[:, tt], powed[:, 0, tt], minus_half).then_inc(C["rstd_ready"], 1)

            def powers_match(p):
                tt = slice(2 * p, 2 * p + 2)
                pool.wait_ge(G["var_ready"], p + 1)
                power(rstd[:, tt], powed[:, 0, tt], minus_half)
                power(xnorm[:, tt], powed[:, 1, tt], half_).then_inc(G["powers_ready"], 1)

            def rstd_last(p):
                tt = slice(2 * p, 2 * p + 2)
                pool.wait_ge(Z["var_ready"], p + 1)
                power(rstd[:, tt], powed[:, 0, tt], minus_half).then_inc(Z["rstd_ready"], 1)

            pieces = dict(h=unit_h, bias=add_out_bias, weigh=weigh, mix=mix, rstd=rstd_one, rms=rms_power, tnorm=text_norms, prstd=rstd_experts, gpow=powers_match,
                          zpow=rstd_last)
            for stage, i in order["pool"]:
                pieces[stage](i)

        @block.tensor
        def _(pe):
            mm, tr = nc.tensor.matmul, nc.tensor.transpose
            reader = {}

            def fill(bank, *readers):
                for r in reader.get(bank, ()):
                    pe.wait_ge(*r)
                reader[bank] = readers

            pe.wait_ge(dma_const, 16)
            pe.wait_ge(presets, PRESETS)
            pe.wait_ge(wabs_ready, 4)
            fill("Mp", (tern_ready, 2))
            mm(Mp[:, 0:4], ones[:, :], wabs[:, :], start=True, stop=True).then_inc(alpha_mm, 1)

            pe.wait_ge(tern_ready, 2)

            def gate_up(u):
                q, e, c = u // (E * FC), u // FC % E, u % FC
                if q == 0 and c == 0:
                    pe.wait_ge(dma_w[e], 48)
                if c == 0:
                    pe.wait_ge(C["xT_in"], q + 1)
                    pe.wait_ge(C["xwT_in"], u // FC + 1)
                fill(f"FU{u % 2}", (C["gated"], u + 1))
                mm(FU[:, u % 2, 0:256], w1s[:, e, c * P:c * P + P], xallT[:, q % 2, :, :].rearrange("p t n -> p (t n)"),
                   start=True, stop=True)
                mm(FU[:, u % 2, 256:512], w3s[:, e, c * P:c * P + P], xwT[:, (u // FC) % 2, :, :].rearrange("p t n -> p (t n)"),
                   start=True, stop=True).then_inc(C["gu_mm"], 1)

            def down(u):
                q, e, c = u // (E * FC), u // FC % E, u % FC
                if e == 0 and c == 0:
                    fill("AC", (C["oT_in"], q + 1))
                pe.wait_ge(C["h_ready"], u + 1)
                mm(AC[:, 0:256], w2s[:, e, c, :], hh[:, u % NB, :], start=(e == 0 and c == 0),
                   stop=(e == E - 1 and c == FC - 1)).then_inc(C["down_mm"], 1)

            def turn_x(n):
                fill("Mp", (S["xT_in"], n + 1))
                pe.wait_ge(S["xn_ready"], n + 1)
                if kind[n] == "A":
                    ins = tr(Mp[:, 0:P], xint[:, n % 2, :], ident)
                else:
                    ins = tr(Mp[:, 0:P], xn[:, n % 2, :], ident)
                ins.then_inc(S["xT_mm"], 1)

            def project(n):
                L, b = kind[n], n % 2
                pe.wait_ge(S["xT_in"], n + 1)
                if L == "A":
                    if n == 0:
                        pe.wait_ge(tern_ready, 3)
                    fill("Mp", (S["qkv_in"], nth(n, "A") + 1))
                    mm(Mp[:, 0:192], xintT[:, b, :], tern[:, 0:192], start=True, stop=True).then_inc(S["proj_mm"], 1)
                    return
                fill("Mp", (S["added"], nth(n, "BD") + 1))
                pe.wait_ge(dma_param, 16)
                if L == "B":
                    pe.wait_ge(text_in, tile[n] // 2 + 1)
                    mm(Mp[:, 0:D], xnT[:, b, :], w_in["B"][:, 0:D], start=True, stop=True)
                    mm(Mp[:, D:384], textT[:, tile[n], :], w_in["B"][:, D:384], start=True, stop=True)\
                        .then_inc(S["proj_mm"], 1)
                else:
                    mm(Mp[:, 0:400], xnT[:, b, :], w_in["D"], start=True, stop=True).then_inc(S["proj_mm"], 1)

            def turn(n):
                L, b = kind[n], n % 2
                fill("Sp", (S["act_took"], n + 1))
                if L == "A":
                    pe.wait_ge(S["rotated"], nth(n, "A") + 1)
                else:
                    pe.wait_ge(S["padded"], nth(n, "BD") + 1)
                for r in range(NR):
                    tr(Sp[:, r * P:r * P + P], qpad[:, b, r, :, :].rearrange("p g c -> p (g c)"), ident)
                kp = kpad_m if L == "B" else kpad
                for r in range(1 if L == "A" else NR):
                    mm(Sp[:, 512 + 64 * r:576 + 64 * r], kp[:, b, r, :, :].rearrange("p g c -> p (g c)"), pairI,
                       start=True, stop=True)
                v, w = (vtok[:, b, :], 32) if L == "A" else (proj[:, b, 256:384], 128)
                for half in range(2):
                    ins = mm(Sp[:, 768 + w * half:768 + w * half + w], dup[:, half, :], v, start=True, stop=True)
                ins.then_inc(S["turn_mm"], 1)

            def scores(n):
                L, b = kind[n], n % 2
                fill("Sp", (S["shifted"], n + 1))
                if L == "A":
                    for gh in range(2):
                        mm(Sp[:, 512 * gh:512 * gh + 512], identb[:, :],
                           causal_b[:, :].unsqueeze(1).to_broadcast([P, 8, 64]), start=True, stop=False,
                           skip_group_check=True)
                for r in range(NR):
                    for gh in range(2):
                        c = slice(64 * gh, 64 * gh + 64)
                        at = 512 * gh + 128 * r
                        k = kbd[c, b, 0 if L == "A" else r, :, :].rearrange("p g c -> p (g c)")
                        if L == "D":
                            ins = mm(Sp[:, at:at + 128], k, qT[c, b, r, :], start=True, stop=True)
                        else:
                            ins = mm(Sp[:, at:at + 128], qT[c, b, r, :], k, start=L != "A", stop=True,
                                     skip_group_check=L == "A")
                ins.then_inc(S["scores_mm"], 1)

            def turn_probs(n, k):
                i = nth(n, "AB")
                fill("Tp", (S["pT_in"], 2 * i + k + 1))
                pe.wait_ge(S["probs_ready"], i + 1)
                flat = probs[:, i % 2, :, :].rearrange("p h k -> p (h k)")
                for j in range(4):
                    ins = tr(Tp[:, j * P:j * P + P], flat[:, (4 * k + j) * P:(4 * k + j) * P + P], ident)
                ins.then_inc(S["pT_mm"], 1)

            def values(n):
                L, b = kind[n], n % 2
                fill("Op", (S["y_ready"], n + 1))
                if L == "D":
                    pe.wait_ge(S["shifted"], n + 1)
                else:
                    pe.wait_ge(S["pT_in"], 2 * nth(n, "AB") + 2)
                pe.wait_ge(S["act_took"], n + 1)
                o = Op[:, 0:2 * OW].rearrange("p (a c) -> p a c", a=2)
                for j in range(8):
                    v = vbd[:, b, j // 4 if L == "A" else j, :, :]
                    ins = mm(o[:, :, 2 * AUG * j:2 * AUG * j + 2 * AUG], pT[:, b, j, :], v, start=True, stop=True)
                ins.then_inc(S["pv_mm"], 1)

            def turn_y(n):
                b = n % 2
                fill("Op", (S["yT_in"], n + 1))
                pe.wait_ge(S["y_ready"], n + 1)
                if kind[n] == "A":
                    ins = tr(Op[:, 0:P], yint[:, b, :], ident)
                else:
                    ins = tr(Op[:, 0:P], y[:, b, :, :].rearrange("p h c -> p (h c)"), ident)
                ins.then_inc(S["yT_mm"], 1)

            def project_out(n):
                b = n % 2
                fill("Op", (S["x_updated"], n + 1))
                pe.wait_ge(S["yT_in"], n + 1)
                if kind[n] == "A":
                    ins = mm(Op[:, 0:D], yintT[:, b, :], tern[:, 192:320], start=True, stop=True)
                else:
                    ins = mm(Op[:, 0:D], yT[:, b, :], w_out[kind[n]], start=True, stop=True)
                ins.then_inc(S["out_mm"], 1)

            def turn_two(bank, name, src, signal, *readers):
                fill(name, *readers)
                for i in range(2):
                    ins = tr(bank[:, i * P:i * P + P], src[:, i, :], ident)
                ins.then_inc(signal, 1)

            def turn_text(i):
                pe.wait_ge(dma_text, 16)
                turn_two(Mp, "Mp", text[:, 2 * i:2 * i + 2, :], text_mm, (text_in, i + 1))

            def turn_tnorm(i):
                pe.wait_ge(tn_ready, i + 1)
                turn_two(Mp, "Mp", xz, tn_mm, (tn_in, i + 1))

            def turn_quarter(q):
                pe.wait_ge(C["xn_ready"], q + 1)
                turn_two(Tp, "Tp", xall[:, q % 2, :, :], C["xT_mm"], (C["xT_in"], q + 1))

            def logits(q):
                fill("Mp", (C["lg_in"], q + 1))
                pe.wait_ge(C["xT_in"], q + 1)
                for i in range(2):
                    ins = mm(Mp[:, E * i:E * i + E], xallT[:, q % 2, i, :], gate_w, start=True, stop=True)
                ins.then_inc(C["logits_mm"], 1)

            def turn_weighed(k):
                pe.wait_ge(C["xw_ready"], k + 1)
                turn_two(Tp, "Tp", xw[:, k % 2, :, :], C["xwT_mm"], (C["xwT_in"], k + 1))

            def turn_back(q):
                pe.wait_ge(C["oT_in"], q + 1)
                turn_two(Tp, "Tp", oT, C["back_mm"], (C["x_updated"], q + 1))

            def turn_match(p):
                pe.wait_ge(G["xn_ready"], p + 1)
                turn_two(Tp, "Tp", xz, G["xT_mm"], (G["xT_in"], p + 1))

            def similarity(p):
                fill("Mp", (G["pick_ready"], p + 1))
                pe.wait_ge(G["xT_in"], p + 1)
                pe.wait_ge(tn_in, NQ)
                for i in range(2):
                    for half in range(2):
                        c = slice(64 * half, 64 * half + 64)
                        ins = mm(Mp[c, 64 * i:64 * i + 64], xzT[:, i, c], tnormT[:, 2 * p + i, c], start=True, stop=True)
                ins.then_inc(G["sim_mm"], 1)

            def turn_pick(p):
                pe.wait_ge(G["pick_ready"], p + 1)
                turn_two(Tp, "Tp", pick, G["pickT_mm"], (G["pickT_in"], p + 1))

            def get_rows(p):
                fill("Op", (G["x_updated"], p + 1))
                pe.wait_ge(G["pickT_in"], p + 1)
                for i in range(2):
                    ins = mm(Op[:, P * i:P * i + P], pickT[:, i, :], text[:, 2 * p + i, :], start=True, stop=True)
                ins.then_inc(G["got_mm"], 1)

            def turn_last(p):
                pe.wait_ge(Z["xn_ready"], p + 1)
                turn_two(Tp, "Tp", xz, Z["xT_mm"], (Z["xT_in"], p + 1))

            def hidden(k):
                def piece(p):
                    bank, name = ((Tp, "Tp"), (Mp, "Mp"))[k]
                    fill(name, (Z["h_in"], 2 * p + k + 1))
                    pe.wait_ge(Z["xT_in"], p + 1)
                    for i in range(2):
                        c = 2 * k + i
                        ins = mm(bank[:, 256 * i:256 * i + 256], f_w1[:, c * P:c * P + P],
                                 xzT[:, :, :].rearrange("p t n -> p (t n)"), start=True, stop=True)
                    ins.then_inc(Z["h_mm"], 1)
                return piece

            def last_out(p):
                fill("Mp", (Z["fin"], p + 1))
                pe.wait_ge(Z["hq_ready"], 2 * p + 2)
                for i in range(2):
                    for c in range(FC):
                        ins = mm(Mp[:, P * i:P * i + P], hq[:, c, P * i:P * i + P], f_w2[:, c, :],
                                 start=(c == 0), stop=(c == FC - 1))
                ins.then_inc(Z["out_mm"], 1)

            def keep_warm(_):
                fill("FU0")
                mm(FU[:, 0, :], identb[:, :], causal_b[:, :].unsqueeze(1).to_broadcast([P, 8, 64]), start=True, stop=True)

            pieces = dict(keep_warm=keep_warm, xT=turn_x, proj=project, turn=turn, scores=scores, tp0=lambda n: turn_probs(n, 0),
                          tp1=lambda n: turn_probs(n, 1), values=values, yT=turn_y, out=project_out,
                          text=turn_text, tnT=turn_tnorm, pT=turn_quarter, logits=logits, xwT=turn_weighed,
                          gu=gate_up, down=down, back=turn_back, gT=turn_match, sim=similarity, pickT=turn_pick,
                          got=get_rows, zT=turn_last, zh0=hidden(0), zh1=hidden(1), zout=last_out)
            for stage, i in order["tensor"]:
                pieces[stage](i)

        @block.scalar
        def _(act):
            act.dma_start(x[:, :, :], d["x"].rearrange("(t p) n -> p t n", p=P)).then_inc(dma_x, 16)
            act.dma_start(consts[:, :], d["consts"]).then_inc(dma_const, 16)

            def copy(o, i):
                return nc.scalar.activation(o, i, ACT.Copy)

            def copy_two(o, bank):
                return copy(o.rearrange("p t n -> p (t n)"), bank[:, 0:256])

            def unit_out(u):
                act.wait_ge(C["gu_mm"], u + 1)
                if u >= NB:
                    act.wait_ge(C["h_ready"], u - NB + 1)
                nc.scalar.activation(th[:, u % NB, :], FU[:, u % 2, 0:256], ACT.Tanh, scale=0.5)
                copy(uu[:, u % NB, :], FU[:, u % 2, 256:512]).then_inc(C["u_in"], 1)

            def x_turned(n):
                b = n % 2
                act.wait_ge(S["xT_mm"], n + 1)
                if n >= 2:
                    act.wait_ge(S["proj_mm"], n - 1)
                if kind[n] == "A":
                    nc.scalar.activation(xintT[:, b, :], Mp[:, 0:P], ACT.Copy, bias=-MAGIC).then_inc(S["xT_in"], 1)
                else:
                    copy(xnT[:, b, :], Mp[:, 0:P]).then_inc(S["xT_in"], 1)

            def qkv_out(n):
                i = nth(n, "A")
                act.wait_ge(S["proj_mm"], n + 1)
                if i >= 2:
                    act.wait_ge(S["rotated"], i - 1)
                nc.scalar.activation(sq[:, i % 2, :, :].rearrange("p s c -> p (s c)"), Mp[:, 0:160], ACT.Square)
                copy(qkv[:, i % 2, :], Mp[:, 0:192]).then_inc(S["qkv_in"], 1)

            def pad(n):
                L, b, i = kind[n], n % 2, nth(n, "BD")
                act.wait_ge(S["added"], i + 1)
                if n >= 2:
                    act.wait_ge(S["turn_mm"], n - 1)
                kp = kpad_m if L == "B" else kpad
                for half in range(2):
                    c = slice(64 * half, 64 * half + 64)
                    o = slice(AUG * half, AUG * half + HD)
                    for dst, at in ((qpad, 0), (kp, D)):
                        ins = copy(dst[c, b, :, :, o].rearrange("p r g c -> p (r g) c"),
                                   proj[c, b, at:at + D].rearrange("p (s c) -> p s c", c=HD))
                    if L == "B":
                        t, a = tile[n], AUG * half + HD
                        act.wait_ge(mask_ready, 1)
                        ins = copy(kp[c, b, :, :, a:a + 1].rearrange("p r g c -> p (r g) c"),
                                   mask_neg[c, t:t + 1].unsqueeze(2).to_broadcast([64, H, 1]))
                ins.then_inc(S["padded"], 1)
                if L == "D":
                    j = nth(n, "D")
                    if j >= 4:
                        act.wait_ge(S["y_ready"], job("D", j - 4) + 1)
                    nc.scalar.activation(nexp[:, j % 4, :], proj[:, b, 384:400], ACT.Exp, scale=-1.0)\
                        .then_inc(S["n_in"], 1)

            def take(n):
                L, b = kind[n], n % 2
                act.wait_ge(S["turn_mm"], n + 1)
                if n >= 2:
                    act.wait_ge(S["scores_mm"], n - 1)
                    act.wait_ge(S["pv_mm"], n - 1)
                copy(qT[:, b, :, :].rearrange("p r n -> p (r n)"), Sp[:, 0:512])
                nr, j = (1, 2) if L == "A" else (NR, 8)
                for g in range(2):
                    nc.scalar.activation(kbd[:, b, 0:nr, g, :], Sp[:, 512:512 + 64 * nr].rearrange("p (r k) -> p r k", k=64),
                                         ACT.Copy, scale=gmask[:, g:g + 1])
                vv = Sp[:, 768:768 + 32 * j].rearrange("p (a j w c) -> p a j w c", a=2, j=j, w=2)
                for w_ in range(2):
                    c = slice(64 * w_, 64 * w_ + 64)
                    ins = copy(vbd[c, b, 0:j, :, AUG * w_:AUG * w_ + HD].rearrange("p j a c -> p a j c"), vv[c, :, :, w_, :])
                ins.then_inc(S["act_took"], 1)

            def exps(n):
                i = nth(n, "AB")
                act.wait_ge(S["shifted"], n + 1)
                e = probs[:, i % 2, :, :].rearrange("p h k -> p (h k)")
                nc.scalar.activation(e, e, ACT.Exp, scale=SCALE).then_inc(S["probs_ready"], 1)

            def probs_turned(n, k):
                b = n % 2
                act.wait_ge(S["pT_mm"], 2 * nth(n, "AB") + k + 1)
                if n >= 2:
                    act.wait_ge(S["pv_mm"], n - 1)
                copy(pT[:, b, 4 * k:4 * k + 4, :].rearrange("p j n -> p (j n)"), Tp[:, :]).then_inc(S["pT_in"], 1)

            def y_turned(n):
                b = n % 2
                act.wait_ge(S["yT_mm"], n + 1)
                if n >= 2:
                    act.wait_ge(S["out_mm"], n - 1)
                if kind[n] == "A":
                    nc.scalar.activation(yintT[:, b, :], Op[:, 0:P], ACT.Copy, bias=-MAGIC).then_inc(S["yT_in"], 1)
                else:
                    copy(yT[:, b, :], Op[:, 0:P]).then_inc(S["yT_in"], 1)

            def text_turned(i):
                act.wait_ge(text_mm, i + 1)
                copy_two(textT[:, 2 * i:2 * i + 2, :], Mp).then_inc(text_in, 1)

            def tnorm_turned(i):
                act.wait_ge(tn_mm, i + 1)
                copy_two(tnormT[:, 2 * i:2 * i + 2, :], Mp).then_inc(tn_in, 1)

            def quarter_turned(q):
                act.wait_ge(C["xT_mm"], q + 1)
                if q >= 2:
                    act.wait_ge(C["gu_mm"], E * FC * (q - 1))
                copy_two(xallT[:, q % 2, :, :], Tp).then_inc(C["xT_in"], 1)

            def route_exps(q):
                act.wait_ge(C["z_ready"], q + 1)
                flat = zz[:, :, :, :].rearrange("p k t e -> p (k t e)")
                nc.scalar.activation(flat, flat, ACT.Exp).then_inc(C["zexp_ready"], 1)

            def weighed_turned(k):
                act.wait_ge(C["xwT_mm"], k + 1)
                if k >= 2:
                    act.wait_ge(C["gu_mm"], FC * (k - 1))
                copy_two(xwT[:, k % 2, :, :], Tp).then_inc(C["xwT_in"], 1)

            def experts_out(q):
                act.wait_ge(C["down_mm"], E * FC * (q + 1))
                if q:
                    act.wait_ge(C["back_mm"], q)
                copy_two(oT[:, :, :], AC).then_inc(C["oT_in"], 1)

            def match_turned(p):
                act.wait_ge(G["xT_mm"], p + 1)
                if p:
                    act.wait_ge(Z["h_mm"], 2 * p)
                copy_two(xzT[:, :, :], Tp).then_inc(G["xT_in"], 1)

            def pick_turned(p):
                act.wait_ge(G["pickT_mm"], p + 1)
                if p:
                    act.wait_ge(G["got_mm"], p)
                copy_two(pickT[:, :, :], Tp).then_inc(G["pickT_in"], 1)

            def last_turned(p):
                act.wait_ge(Z["xT_mm"], p + 1)
                act.wait_ge(G["sim_mm"], p + 1)
                copy_two(xzT[:, :, :], Tp).then_inc(Z["xT_in"], 1)

            def hidden_out(k):
                def piece(p):
                    act.wait_ge(Z["h_mm"], 2 * p + k + 1)
                    act.wait_ge(Z["b1_ready"], 1)
                    if p:
                        act.wait_ge(Z["node_ready"], 2 * p + k - 1)
                    for i in range(2):
                        ins = nc.scalar.activation(ha[:, k, 256 * i:256 * i + 256], (Tp, Mp)[k][:, 256 * i:256 * i + 256],
                                                   ACT.Identity, bias=b1x[:, 2 * k + i:2 * k + i + 1], scale=FIX)
                    ins.then_inc(Z["h_in"], 1)
                return piece

            def gelus(p):
                for k in range(2):
                    act.wait_ge(Z["node_ready"], 2 * p + k + 1)
                    if p:
                        act.wait_ge(Z["hq_ready"], 2 * p)
                    nc.scalar.activation(g0[:, k, :], hn[:, k, :], ACT.Gelu, scale=0.25)
                    nc.scalar.activation(g1[:, k, :], hn[:, k, :], ACT.Gelu, bias=quarter[:, :], scale=0.25)\
                        .then_inc(Z["gelu_ready"], 1)

            pieces = dict(xTin=x_turned, qkvout=qkv_out, pad=pad, take=take, exps=exps,
                          tpin0=lambda n: probs_turned(n, 0), tpin1=lambda n: probs_turned(n, 1), yTin=y_turned,
                          textin=text_turned, tnin=tnorm_turned, pTin=quarter_turned, zexp=route_exps,
                          xwTin=weighed_turned, uo=unit_out, oT=experts_out, gTin=match_turned, pickin=pick_turned,
                          zTin=last_turned, ha0=hidden_out(0), ha1=hidden_out(1), gelu=gelus)
            for stage, i in order["scalar"]:
                pieces[stage](i)

        @block.vector
        def _(dve):
            v = nc.vector
            count = [0]

            def link(ins):
                count[0] += 1
                ins.then_inc(step, 1)
                dve.wait_ge(step, count[0])

            def moments(tiles):
                for t in tiles:
                    ins = v.bn_stats(stats[:, t, :], x[:, t, :])
                link(ins)
                for t in tiles:
                    ins = v.bn_aggr(mv[:, t, :], stats[:, t, :])
                link(ins)
                tt = slice(tiles[0], tiles[-1] + 1)
                return v.tensor_scalar(powed[:, 0, tt], mv[:, tt, 1], LN_EPS, None, ALU.add)

            def normalise(o, t):
                return v.tensor_scalar(o, x[:, t, :], mv[:, t, 0:1], rstd[:, t:t + 1], ALU.subtract, ALU.mult)

            def quantise(src, g, o):
                link(v.tensor_reduce(small[:, 0:1], src, X, ALU.max, apply_absolute_value=True))
                link(v.tensor_scalar(g, small[:, 0:1], 1e-8, 1.0 / 127.0, ALU.max, ALU.mult))
                link(v.reciprocal(small[:, 1:2], g))
                link(v.tensor_scalar(qt[:, :], src, small[:, 1:2], 127.0, ALU.mult, ALU.min))
                return v.tensor_scalar(o, qt[:, :], -128.0, MAGIC, ALU.max, ALU.add)

            dve.wait_ge(dma_param_a, 16)
            parts = ((0, 128), (128, 160), (160, 192))
            for i, (a, b) in enumerate(parts):
                v.tensor_reduce(wabs[:, i:i + 1], w_qkv[:, a:b], X, ALU.add, apply_absolute_value=True)\
                    .then_inc(wabs_ready, 1)
            v.tensor_reduce(wabs[:, 3:4], w_p, X, ALU.add, apply_absolute_value=True).then_inc(wabs_ready, 1)
            def job_stats(n):
                L, t = kind[n], tile[n]
                if L == "B":
                    dve.wait_ge(S["x_updated"], job("A", t) + 1)
                if L == "D":
                    dve.wait_ge(C["x_updated"], t // 2 + 1)
                moments([t]).then_inc(S["var_ready"], 1)

            dve.wait_ge(dma_x, 16)
            for n in range(AHEAD):
                job_stats(n)
            dve.wait_ge(dma_text, 16)
            link(v.tensor_tensor(hq[:, :, :].rearrange("p c n -> p (c n)"), text[:, :, :].rearrange("p t n -> p (t n)"),
                                 text[:, :, :].rearrange("p t n -> p (t n)"), ALU.mult))
            v.tensor_reduce(text_sum[:, :], hq[:, :, :].rearrange("p c (a n) -> p (c a) n", n=D), X, ALU.add)\
                .then_inc(tsum_ready, 1)

            dve.wait_ge(dma_const, 16)
            v.tensor_copy(identb[:, :], ident).then_inc(tern_ready, 1)
            link(v.tensor_copy(causal_b[:, :], causal_add))
            link(v.tensor_tensor(cgain[:, :, :], rope_c, gain.unsqueeze(2).to_broadcast([P, 20, HD]), ALU.mult))
            link(v.tensor_tensor(sgain[:, :, :], rope_s, gain.unsqueeze(2).to_broadcast([P, 20, HD]), ALU.mult))
            dve.wait_ge(alpha_mm, 1)
            for i, n in enumerate((128, 32, 32, 128)):
                ins = v.tensor_scalar(alphas[:, i:i + 1], Mp[:, i:i + 1], 1.0 / (n * D), 1e-8, ALU.mult, ALU.max)
            ins.then_inc(tern_ready, 1)
            link(v.memset(alpha20[:, :], 1.0))
            link(v.tensor_scalar(alpha20[:, 0:16], alpha20[:, 0:16], alphas[:, 0:1], None, ALU.mult))
            link(v.tensor_scalar(alpha20[:, 16:20], alpha20[:, 16:20], alphas[:, 1:2], None, ALU.mult))
            link(v.reciprocal(inv_alphas[:, :], alphas[:, :]))
            for i, (a, b) in enumerate(parts + ((192, 320),)):
                src = w_qkv[:, a:b] if i < 3 else w_p
                ins = v.tensor_scalar(tq[:, a:b], src, inv_alphas[:, i:i + 1], 1.0, ALU.mult, ALU.min)
            link(ins)
            link(v.tensor_scalar(tq[:, :], tq[:, :], -1.0, MAGIC, ALU.max, ALU.add))
            v.tensor_scalar(tern[:, :], tq[:, :], MAGIC, None, ALU.subtract).then_inc(tern_ready, 1)
            dve.wait_ge(presets, PRESETS)

            def front(n):
                L, t, b = kind[n], tile[n], n % 2
                dve.wait_ge(S["rstd_ready"], n + 1)
                if n >= 2:
                    dve.wait_ge(S["xT_mm"], n - 1)
                if L == "A":
                    link(normalise(xn[:, b, :], t))
                    quantise(xn[:, b, :], gam[:, nth(n, "A") % 4, :], xint[:, b, :]).then_inc(S["xn_ready"], 1)
                else:
                    normalise(xn[:, b, :], t).then_inc(S["xn_ready"], 1)

            def rotate_a(n):
                i = nth(n, "A")
                b, g = i % 2, gam[:, i % 4, :]
                dve.wait_ge(S["qkv_in"], i + 1)
                if i:
                    dve.wait_ge(S["rms_ready"], i)
                if i >= 2:
                    dve.wait_ge(S["rotated"], i - 1)
                v.tensor_scalar(fac[:, b, :], alpha20[:, :], g, None, ALU.mult)
                link(v.tensor_reduce(rr[:, 0, :], sq[:, b, :, :], X, ALU.add))
                link(v.scalar_tensor_tensor(rr[:, 1, :], rr[:, 0, :], 1.0 / HD, fac[:, b, :], ALU.mult, ALU.mult))
                link(v.tensor_tensor(rr[:, 0, :], rr[:, 1, :], fac[:, b, :], ALU.mult))
                v.tensor_scalar(rms[:, b, 0, :], rr[:, 0, :], RMS_EPS, None, ALU.add).then_inc(S["rms_ready"], 1)

            def rotate_b(n):
                i = nth(n, "A")
                b, o_, g = i % 2, n % 2, gam[:, i % 4, :]
                dve.wait_ge(S["rms_in"], i + 1)
                if i:
                    dve.wait_ge(S["rotated"], i)
                v.tensor_tensor(gav[:, :], g, alphas[:, 2:3], ALU.mult)
                link(v.tensor_tensor(rk[:, :], rms[:, b, 1, :], fac[:, b, :], ALU.mult))
                qk = qkv[:, b, 0:160].rearrange("p (s c) -> p s c", c=HD)
                link(v.tensor_tensor(qn[:, :, :], qk, rk[:, :].unsqueeze(2).to_broadcast([P, 20, HD]), ALU.mult))
                if n >= 2:
                    dve.wait_ge(S["turn_mm"], n - 1)
                v.tensor_scalar(vtok[:, o_, :], qkv[:, b, 160:192], gav[:, :], None, ALU.mult)
                v.tensor_tensor(m1[:, :, :], qn[:, :, :], cgain[:, :, :], ALU.mult)
                swapped = qn[:, :, :].rearrange("p s (u c) -> p s u c", u=2)[:, :, ::-1, :]
                link(v.tensor_tensor(m2[:, :, :].rearrange("p s (u c) -> p s u c", u=2), swapped,
                                     sgain[:, :, :].rearrange("p s (u c) -> p s u c", u=2), ALU.mult))
                for half in range(2):
                    c = slice(64 * half, 64 * half + 64)
                    o = slice(AUG * half, AUG * half + HD)
                    v.tensor_tensor(qpad[c, o_, :, :, o], m1[c, 0:16, :].rearrange("p (r g) c -> p r g c", g=NG),
                                    m2[c, 0:16, :].rearrange("p (r g) c -> p r g c", g=NG), ALU.add)
                    ins = v.tensor_tensor(kpad[c, o_, 0, :, o], m1[c, 16:20, :], m2[c, 16:20, :], ALU.add)
                ins.then_inc(S["rotated"], 1)

            def add_bias(n):
                L, b = kind[n], n % 2
                w = 384 if L == "B" else 400
                dve.wait_ge(S["proj_mm"], n + 1)
                if n >= 2:
                    dve.wait_ge(S["turn_mm"], n - 1)
                    if kind[n - 2] == "D":
                        dve.wait_ge(S["n_in"], nth(n - 1, "D"))
                v.tensor_tensor(proj[:, b, 0:w], Mp[:, 0:w], b_in[L], ALU.add).then_inc(S["added"], 1)

            def shift(n):
                dve.wait_ge(S["scores_mm"], n + 1)
                if kind[n] == "D":
                    dve.wait_ge(S["pv_mm"], n - 1)
                    v.tensor_tensor(pT[:, n % 2, :, :], Sp[:, :].rearrange("p (j n) -> p j n", j=8),
                                    causalT.unsqueeze(1).to_broadcast([P, 8, P]), ALU.mult).then_inc(S["shifted"], 1)
                    return
                i = nth(n, "AB")
                if i >= 2:
                    dve.wait_ge(S["pT_mm"], 2 * (i - 1))
                if n:
                    dve.wait_ge(S["shifted"], n)
                sc = Sp[:, :].rearrange("p (h k) -> p h k", h=H)
                link(v.tensor_reduce(mx[:, :], sc, X, ALU.max))
                v.tensor_tensor(probs[:, i % 2, :, :], sc, mx[:, :].unsqueeze(2).to_broadcast([P, H, 64]), ALU.subtract)\
                    .then_inc(S["shifted"], 1)

            def norm(n):
                L, b = kind[n], n % 2
                dve.wait_ge(S["pv_mm"], n + 1)
                if n >= 2:
                    dve.wait_ge(S["yT_mm"], n - 1)
                o = Op[:, 0:2 * OW].rearrange("p (a s c) -> p a s c", a=2, c=AUG)
                if L == "D":
                    j = nth(n, "D")
                    dve.wait_ge(S["n_in"], j + 1)
                else:
                    if n:
                        dve.wait_ge(S["y_ready"], n)
                    v.reciprocal(rden[0:64, :], o[0:64, 0, :, HD])
                    link(v.reciprocal(rden[64:128, :], o[64:128, 1, :, HD]))
                for half in range(2):
                    c = slice(64 * half, 64 * half + 64)
                    f = nexp[c, j % 4, :] if L == "D" else rden[c, :]
                    ins = v.tensor_tensor(y[c, b, :, :], o[c, half, :, 0:HD],
                                          f.unsqueeze(2).to_broadcast([64, H, HD]), ALU.mult)
                if L == "A":
                    link(ins)
                    ins = quantise(y[:, b, :, :].rearrange("p h c -> p (h c)"), ygam[:, b, :], yint[:, b, :])
                ins.then_inc(S["y_ready"], 1)

            def update(n):
                L, t, b = kind[n], tile[n], n % 2
                dve.wait_ge(S["out_mm"], n + 1)
                if L == "A":
                    link(v.tensor_tensor(small[:, 3:4], ygam[:, b, :], alphas[:, 3:4], ALU.mult))
                    v.scalar_tensor_tensor(x[:, t, :], Op[:, 0:D], small[:, 3:4], x[:, t, :], ALU.mult, ALU.add)\
                        .then_inc(S["x_updated"], 1)
                else:
                    dve.wait_ge(S["biased"], nth(n, "BD") + 1)
                    v.tensor_tensor(x[:, t, :], x[:, t, :], Op[:, 0:D], ALU.add).then_inc(S["x_updated"], 1)

            def two(t0):
                return x[:, t0:t0 + 2, :].rearrange("p t n -> p (t n)")

            it = iota8.unsqueeze(1).to_broadcast([P, 2, E])

            def both(a):
                return a.unsqueeze(1).to_broadcast([P, 2, 2, E])

            def top(k):
                link(v.tensor_reduce(thr[:, k, :], base[:, k, :, :], X, ALU.max))
                link(v.tensor_tensor(tied[:, :, :], base[:, k, :, :], thr[:, k, :].unsqueeze(2).to_broadcast([P, 2, E]),
                                     ALU.is_equal))
                link(v.scalar_tensor_tensor(tied[:, :, :], tied[:, :, :], -64.0, it, ALU.mult, ALU.add))
                link(v.tensor_reduce(first[:, :], tied[:, :, :], X, ALU.min))
                link(v.tensor_tensor(hot[:, k, :, :], tied[:, :, :], first[:, :].unsqueeze(2).to_broadcast([P, 2, E]),
                                     ALU.is_equal))

            def route_a(q):
                dve.wait_ge(C["lg_in"], q + 1)
                lg = base[:, 0, :, :]
                v.scalar_tensor_tensor(absl[:, :, :], lg, -1.0, lg, ALU.mult, ALU.max)
                top(0)
                link(v.scalar_tensor_tensor(base[:, 1, :, :], hot[:, 0, :, :], -3.0e38, lg, ALU.mult, ALU.add))
                top(1)
                threshold = thr[:, :, :].unsqueeze(3).to_broadcast([P, 2, 2, E])
                v.tensor_tensor(zz[:, :, :, :], both(lg), threshold, ALU.subtract)
                link(v.tensor_tensor(kept[:, :, :, :], both(absl[:, :, :]), threshold, ALU.max))
                link(v.tensor_scalar(kept[:, :, :, :], kept[:, :, :, :], 1e-30, None, ALU.max))
                link(v.reciprocal(kept[:, :, :, :], kept[:, :, :, :]))
                link(v.tensor_tensor(kept[:, :, :, :], kept[:, :, :, :], zz[:, :, :, :], ALU.mult))
                link(v.tensor_scalar(kept[:, :, :, :], kept[:, :, :, :], -2.0 * JITTER, None, ALU.is_ge))
                v.tensor_tensor(zz[:, :, :, :], base[:, :, :, :], threshold, ALU.subtract).then_inc(C["z_ready"], 1)

            def route_b(q):
                dve.wait_ge(C["zexp_ready"], q + 1)
                if q >= 2:
                    dve.wait_ge(C["xw_ready"], E * (q - 1))
                link(v.tensor_tensor(zz[:, :, :, :], zz[:, :, :, :], kept[:, :, :, :], ALU.mult))
                link(v.tensor_reduce(zsum[:, :, :], zz[:, :, :, :], X, ALU.add))
                link(v.reciprocal(zsum[:, :, :], zsum[:, :, :]))
                link(v.scalar_tensor_tensor(hot[:, :, :, :], hot[:, :, :, :], 0.5,
                                            zsum[:, :, :].unsqueeze(3).to_broadcast([P, 2, 2, E]), ALU.mult, ALU.mult))
                v.tensor_tensor(wt[:, q % 2, :, :], hot[:, 0, :, :], hot[:, 1, :, :], ALU.add).then_inc(C["wt_ready"], 1)

            def gate(u):
                dve.wait_ge(C["u_in"], u + 1)
                if u >= NB:
                    dve.wait_ge(C["down_mm"], u - NB + 1)
                v.scalar_tensor_tensor(hh[:, u % NB, :], th[:, u % NB, :], 1.0, FU[:, u % 2, 0:256], ALU.add, ALU.mult)\
                    .then_inc(C["gated"], 1)

            def best_row(p):
                dve.wait_ge(G["sim_mm"], p + 1)
                if p:
                    dve.wait_ge(G["pickT_mm"], p)
                sc = Mp[:, 0:128].rearrange("p (t k) -> p t k", t=2)
                link(v.tensor_reduce(best[0][:, :], sc, X, ALU.max))
                link(v.tensor_tensor(sim[:, :, :], sc, best[0][:, :].unsqueeze(2).to_broadcast([P, 2, 64]), ALU.is_equal))
                link(v.scalar_tensor_tensor(sim2[:, :, :], sim[:, :, :], -1024.0, iota64.unsqueeze(1).to_broadcast([P, 2, 64]),
                                            ALU.mult, ALU.add))
                link(v.tensor_reduce(best[1][:, :], sim2[:, :, :], X, ALU.min))
                for half in range(2):
                    c = slice(64 * half, 64 * half + 64)
                    ins = v.tensor_tensor(pick[c, :, c], sim2[c, :, :], best[1][c, :].unsqueeze(2).to_broadcast([64, 2, 64]),
                                          ALU.is_equal)
                ins.then_inc(G["pick_ready"], 1)

            def nodes(p, k):
                dve.wait_ge(Z["h_in"], 2 * p + k + 1)
                if p:
                    dve.wait_ge(Z["gelu_ready"], 2 * p - 1 + k)
                hi, n_ = hi_[:, k, :], hn[:, k, :]
                link(v.tensor_scalar(hi, ha[:, k, :], MAGIC, MAGIC, ALU.add, ALU.subtract))
                link(v.tensor_scalar(n_, hi, 1.0 / 64, -63.0 / 128, ALU.mult, ALU.add))
                v.tensor_scalar(n_, n_, MAGIC, MAGIC, ALU.add, ALU.subtract).then_inc(Z["node_ready"], 1)
                dve.wait_ge(Z["node_ready"], 2 * p + k + 1)
                v.scalar_tensor_tensor(hi, hi, 1.0 / 64, n_, ALU.mult, ALU.subtract).then_inc(Z["f_ready"], 1)

            def blend(p, k):
                a, b, h = g0[:, k, :], g1[:, k, :], hd[:, k, :]
                if p:
                    dve.wait_ge(Z["out_mm"], p)
                    dve.wait_ge(Z["hq_ready"], 2 * p)
                if k == 0:
                    dve.wait_ge(Z["mixed"], p + 1)
                else:
                    dve.wait_ge(Z["gelu_ready"], 2 * p + k + 1)
                    dve.wait_ge(Z["f_ready"], 2 * p + k + 1)
                    link(v.tensor_tensor(b, b, a, ALU.subtract))
                    link(v.tensor_tensor(b, b, hi_[:, k, :], ALU.mult))
                    link(v.tensor_tensor(b, b, a, ALU.add))
                link(v.tensor_scalar(h, b, FIX, MAGIC, ALU.mult, ALU.add))
                v.tensor_scalar(hq[:, 2 * k:2 * k + 2, :].rearrange("p c n -> p (c n)"), h, MAGIC, 1.0 / FIX,
                                ALU.subtract, ALU.mult).then_inc(Z["hq_ready"], 1)

            def finish(p):
                dve.wait_ge(Z["out_mm"], p + 1)
                if p:
                    dve.wait_ge(Z["fin"], p)
                link(v.tensor_tensor(fo[:, :].rearrange("p (t n) -> p t n", t=2), Mp[:, 0:256].rearrange("p (t n) -> p t n", t=2),
                                     f_b2.unsqueeze(1).to_broadcast([P, 2, D]), ALU.add))
                link(v.tensor_scalar(fo[:, :], fo[:, :], FIX, MAGIC, ALU.mult, ALU.add))
                link(v.tensor_scalar(fo[:, :], fo[:, :], MAGIC, 1.0 / FIX, ALU.subtract, ALU.mult))
                v.tensor_tensor(two(2 * p), two(2 * p), fo[:, :], ALU.add).then_inc(Z["fin"], 1)

            def text_inverse(_):
                dve.wait_ge(tnorm_ready, 1)
                link(v.tensor_scalar(norms[:, :], norms[:, :], 1e-12, None, ALU.max))
                link(v.reciprocal(norms[:, :], norms[:, :]))

            def with_params(_):
                dve.wait_ge(dma_param, 16)
                v.tensor_scalar(b1x[:, :], f_b1, FIX, None, ALU.mult).then_inc(Z["b1_ready"], 1)
                v.tensor_scalar(mask_neg[:, :], mask, float(-1e9 / np.float64(SCALE)), None, ALU.mult).then_inc(mask_ready, 1)

            def text_normalised(i):
                if i:
                    dve.wait_ge(tn_mm, i)
                for j in range(2):
                    ins = v.tensor_scalar(xz[:, j, :], text[:, 2 * i + j, :], norms[:, 2 * i + j:2 * i + j + 1], None, ALU.mult)
                ins.then_inc(tn_ready, 1)

            def add_back(q):
                dve.wait_ge(C["back_mm"], q + 1)
                v.tensor_tensor(two(2 * q), two(2 * q), Tp[:, 0:256], ALU.add).then_inc(C["x_updated"], 1)

            def experts_stats(q):
                dve.wait_ge(S["x_updated"], job("B", 2 * q + 1) + 1)
                moments([2 * q, 2 * q + 1]).then_inc(C["var_ready"], 1)

            def experts_norm(q):
                dve.wait_ge(C["rstd_ready"], q + 1)
                if q >= 2:
                    dve.wait_ge(C["xT_mm"], q - 1)
                    dve.wait_ge(C["xw_ready"], E * (q - 1))
                for i in range(2):
                    ins = normalise(xall[:, q % 2, i, :], 2 * q + i)
                ins.then_inc(C["xn_ready"], 1)

            def logits_out(q):
                dve.wait_ge(C["logits_mm"], q + 1)
                v.tensor_copy(base[:, 0, :, :].rearrange("p t e -> p (t e)"), Mp[:, 0:2 * E]).then_inc(C["lg_in"], 1)

            def match_stats(p):
                dve.wait_ge(S["x_updated"], job("D", 2 * p + 1) + 1)
                link(moments([2 * p, 2 * p + 1]))
                v.tensor_scalar(powed[:, 1, 2 * p:2 * p + 2], mv[:, 2 * p:2 * p + 2, 1], float(D), None, ALU.mult)\
                    .then_inc(G["var_ready"], 1)

            def match_norm(p):
                tt = slice(2 * p, 2 * p + 2)
                dve.wait_ge(G["powers_ready"], p + 1)
                link(v.tensor_tensor(xnorm[:, tt], xnorm[:, tt], rstd[:, tt], ALU.mult))
                link(v.tensor_scalar(xnorm[:, tt], xnorm[:, tt], 1e-12, None, ALU.max))
                link(v.reciprocal(xnorm[:, tt], xnorm[:, tt]))
                link(v.tensor_tensor(rstd[:, tt], rstd[:, tt], xnorm[:, tt], ALU.mult))
                if p:
                    dve.wait_ge(Z["xT_mm"], p)
                else:
                    dve.wait_ge(tn_mm, NQ)
                for i in range(2):
                    ins = normalise(xz[:, i, :], 2 * p + i)
                ins.then_inc(G["xn_ready"], 1)

            def add_rows(p):
                dve.wait_ge(G["got_mm"], p + 1)
                v.tensor_tensor(two(2 * p), two(2 * p), Op[:, 0:256], ALU.add).then_inc(G["x_updated"], 1)
                dve.wait_ge(G["x_updated"], p + 1)
                moments([2 * p, 2 * p + 1]).then_inc(Z["var_ready"], 1)

            def last_norm(p):
                dve.wait_ge(Z["rstd_ready"], p + 1)
                dve.wait_ge(G["xT_mm"], p + 1)
                for i in range(2):
                    ins = normalise(xz[:, i, :], 2 * p + i)
                ins.then_inc(Z["xn_ready"], 1)

            pieces = dict(stats=job_stats, front=front, rotA=rotate_a, rotB=rotate_b, add=add_bias, shift=shift,
                          norm=norm, update=update, tnorm2=text_inverse, params=with_params,
                          tn=text_normalised, pstats=experts_stats, pnorm=experts_norm, lgcopy=logits_out, routeA=route_a,
                          routeB=route_b, gate=gate, addback=add_back, gstats=match_stats, gnorm=match_norm,
                          best=best_row, gadd=add_rows, znorm=last_norm, nodes0=lambda p: nodes(p, 0),
                          nodes1=lambda p: nodes(p, 1), blend0=lambda p: blend(p, 0), blend1=lambda p: blend(p, 1),
                          finish=finish)
            for stage, i in order["vector"]:
                pieces[stage](i)


def layout(a):
    f = np.float32
    qk_order = np.array([4 * g + r for r in range(NR) for g in range(NG)])
    order = np.array([4 * (2 * gh + g) + r for gh in range(2) for r in range(NR) for g in range(2)])

    def heads(m, axis, order=order):
        shape = m.shape[:axis] + (H, HD) + m.shape[axis + 1:]
        return np.take(m.reshape(shape), order, axis).reshape(m.shape)

    def qk(m, axis):
        return heads(m, axis, qk_order)

    def wide(v, n=P):
        return np.broadcast_to(np.asarray(v, f).reshape(1, -1), (n, np.asarray(v).size))

    eye = np.eye(P, dtype=f)
    at = np.arange(P) % 64
    pair_i = (at[:, None] == np.arange(64)).astype(f)
    dup = np.stack([(np.arange(P)[:, None] == 64 * h + at[None, :]).astype(f) for h in range(2)], 1)
    gmask = (np.arange(P)[:, None] // 32 % 2 == np.arange(2)).astype(f)
    keep = np.arange(64)[None, :] <= at[:, None]
    keepT = ((np.arange(P) % 64)[:, None] <= at[None, :]).astype(f)
    inv = f(1.0) / np.power(f(10000.0), np.arange(0, HD, 2, dtype=f) / f(HD)).astype(f)
    ang = (at.astype(f)[:, None] * inv[None, :]).astype(f)
    c, s = np.cos(ang).astype(f), np.sin(ang).astype(f)
    rope_c = np.broadcast_to(np.concatenate([c, c], 1)[:, None], (P, 20, HD))
    rope_s = np.broadcast_to(np.concatenate([s, -s], 1)[:, None], (P, 20, HD))
    consts = [eye, pair_i, dup, gmask, keepT, np.where(keep, f(0), f(MASKED)), rope_c, rope_s,
              wide(np.arange(E)), wide(np.arange(64))]

    a = {n: np.asarray(v) for n, v in a.items()}
    w_qkv = np.concatenate([qk(a["L0_attn_Wq"].T, 1), a["L0_attn_Wk"].T, a["L0_attn_Wv"].T], 1)
    gain = np.concatenate([a["L0_attn_q_gain"][qk_order], np.ones(4, f)])
    params_a = [w_qkv, heads(a["L0_attn_Wp"].T, 0), wide(gain)]
    n = "L0_xattn_"
    params = [qk(a[n + "Wq"], 1), qk(a[n + "Wk"], 1), heads(a[n + "Wv"], 1), heads(a[n + "Wo"], 0)]
    params += [wide(qk(a[n + b][None], 1)) for b in ("bq", "bk")] + [wide(heads(a[n + "bv"][None], 1))] + [wide(a[n + "bo"])]
    wqk, bqk = a["L1_attn_Wqk_w"], a["L1_attn_Wqk_b"]
    params += [qk(wqk[:D].T, 1), qk(wqk[D:].T, 1), heads(a["L1_attn_Wv_w"].T, 1), a["L1_attn_Wn_w"][order].T,
               heads(a["L1_attn_Wo_w"].T, 0)]
    params += [wide(qk(b[None], 1)) for b in (bqk[:D], bqk[D:])] + [wide(heads(a["L1_attn_Wv_b"][None], 1))]
    params += [wide(a["L1_attn_Wn_b"][order]), wide(a["L1_attn_Wo_b"])]
    params += [a["mask_Bx1x1xS2_fk0"].reshape(NT, P).T, a["L0_ffn_gate_w"], a["L1_ffn_w1"],
               a["L1_ffn_b1"].reshape(FC, P).T, a["L1_ffn_w2"].reshape(FC, P, D).transpose(1, 0, 2), wide(a["L1_ffn_b2"])]

    def side_by_side(parts):
        return np.ascontiguousarray(np.concatenate([np.asarray(i).reshape(P, -1) for i in parts], 1).astype(f, copy=False))

    return {
        "consts": side_by_side(consts), "params_a": side_by_side(params_a), "params": side_by_side(params),
        "x": np.ascontiguousarray(a["x"]).reshape(NT * P, D), "ctx": np.ascontiguousarray(a["ctx_1024"]).reshape(NT * P, D),
        "w1": np.ascontiguousarray(a["L0_ffn_w1"]), "w2": np.ascontiguousarray(a["L0_ffn_w2"]),
        "w3": np.ascontiguousarray(a["L0_ffn_w3"]),
    }


def kernel(**inputs):
    from concourse import bacc
    from concourse.bass_utils import run_bass_kernel_spmd

    nc = bacc.Bacc("TRN2", target_bir_lowering=False, num_devices=1)
    arrays, d = {}, {}
    for name, a in layout(inputs).items():
        arrays[f"in_{name}"] = a
        d[name] = nc.dram_tensor(f"in_{name}", a.shape, mybir.dt.from_np(a.dtype), kind="ExternalInput").ap()
    out = nc.dram_tensor("out", (NT * P, D), F32, kind="ExternalOutput").ap()
    build(nc, d, out)
    r = run_bass_kernel_spmd(nc, [arrays], core_ids=[0])
    return np.asarray(r.results[0]["out"]).reshape(BATCH, SEQ, D)
```
